# Optimizing a Trainium2 kernel written in Bass

```python
import numpy as np
import jax
import jax.numpy as jnp

def _softmax(x, axis=-1):
    return jax.nn.softmax(x, axis=axis)

def _gelu(x):
    return jax.nn.gelu(x, approximate=True)

def _silu(x):
    return jax.nn.silu(x)

def _sigmoid(x):
    return jax.nn.sigmoid(x)

def _layernorm(x, axis=-1, eps=1e-05):
    m = jnp.mean(x, axis=axis, keepdims=True)
    v = jnp.var(x, axis=axis, keepdims=True)
    return (x - m) / jnp.sqrt(v + eps)

def _scatter_add(tgt, idx, src, axis=0):
    return tgt.at[idx].add(src)

def _segment_sum(src, seg, n):
    return jax.ops.segment_sum(src, seg, n)
kernel_name = 'mk_perceiver_d2_seqx_r2_f3252c'

def setup_inputs(seed: int=0):
    np.random.seed(seed)
    _w = jnp.asarray

    def _rec_inputs():
        import jax
        import jax.numpy as jnp
        _rk = jax.random.key(seed)
        x = -0.0003929 + 0.9999 * jax.random.normal(jax.random.fold_in(_rk, 1), (8, 64, 512), jnp.float32)
        _lenS = 64 - jax.random.randint(jax.random.fold_in(_rk, 7), (8,), 0, max(1, 64 // 4) + 1, jnp.int32)
        _lenS2 = 1601 - jax.random.randint(jax.random.fold_in(_rk, 8), (8,), 0, max(1, 1601 // 4) + 1, jnp.int32)
        _ctx_1024P = jax.random.normal(jax.random.fold_in(_rk, 11), (8, 16, 512), jnp.float32)
        _ctx_1024c = jax.random.dirichlet(jax.random.fold_in(_rk, 511), 0.3 * jnp.ones((16,), jnp.float32), (8, 1601))
        _ctx_1024t = jnp.einsum('bsk,bkd->bsd', _ctx_1024c, _ctx_1024P)
        _ctx_1024t = _ctx_1024t * jax.lax.rsqrt(jnp.mean(jnp.square(_ctx_1024t)) + 1e-12) * 0.953939
        ctx_1024 = 4.13588e-05 + 0.999923 * (_ctx_1024t + 0.3 * jax.random.normal(jax.random.fold_in(_rk, 611), (8, 1601, 512), jnp.float32))
        fside_BxSxS2_0 = jax.random.uniform(jax.random.fold_in(_rk, 12), (8, 64, 1601), jnp.float32, 0.0, 1)
        _validS = jnp.arange(64)[None, :] < _lenS[:, None]
        _validS2 = jnp.arange(1601)[None, :] < _lenS2[:, None]
        _causal = jnp.tril(jnp.ones((64, 64), dtype=bool))
        mask_BxSxS2_ik1 = jnp.where(jnp.broadcast_to(_validS2[:, None, :], (8, 64, 1601)), 1, 0).astype(jnp.int32)
        return (x, ctx_1024, fside_BxSxS2_0, mask_BxSxS2_ik1)
    x, ctx_1024, fside_BxSxS2_0, mask_BxSxS2_ik1 = _rec_inputs()

    def _L0_xattn_setup():
        import jax, jax.numpy as jnp
        import numpy as np
        key = jax.random.key(seed)
        k1, k2 = jax.random.split(key)
        B, L, V, D = (8, 1024, 512, 512)
        hidden_states = jax.random.normal(k1, (B, L, D), dtype=jnp.float32)
        visual_hidden_state = jax.random.normal(k2, (B, V, D), dtype=jnp.float32)
        return {'hidden_states': hidden_states, 'visual_hidden_state': visual_hidden_state}
    _L0_xattn_all = _L0_xattn_setup()
    _L0_xattn_in = {k: v for k, v in _L0_xattn_all.items() if k in ()}
    del _L0_xattn_all

    def _L0_attn_setup():
        import jax, jax.numpy as jnp
        import numpy as np
        EMBED = 512
        HEADS = 16
        HEAD_DIM = EMBED // HEADS
        key = jax.random.key(seed)
        k1, k2, k3, k4, k5 = jax.random.split(key, 5)
        s = 1.0 / np.sqrt(EMBED)
        return {'x': jax.random.normal(k1, (4, 1024, EMBED), dtype=jnp.float32), 'Wqkv': jax.random.uniform(k2, (EMBED, 3 * EMBED), jnp.float32, -s, s), 'bqkv': jax.random.uniform(k3, (3 * EMBED,), jnp.float32, -s, s), 'Wo': jax.random.uniform(k4, (EMBED, EMBED), jnp.float32, -s, s), 'bo': jax.random.uniform(k5, (EMBED,), jnp.float32, -s, s)}
    _L0_attn_all = _L0_attn_setup()
    _L0_attn_in = {k: v for k, v in _L0_attn_all.items() if k in ('Wqkv', 'bqkv', 'Wo', 'bo')}
    del _L0_attn_all

    def _L0_ffn_setup():
        import jax, jax.numpy as jnp
        import numpy as np
        from jax import lax
        D_MODEL = 512
        INTER = 512
        N_EXPERTS = 8
        TOP_K = 2
        ROUTE_SCALE = 1.0
        B, S = (2, 2048)
        key = jax.random.key(seed)
        ks = jax.random.split(key, 16)
        sc_d = 1.0 / np.sqrt(D_MODEL)
        sc_f = 1.0 / np.sqrt(INTER)
        inp = {'x': jax.random.normal(ks[0], (B, S, D_MODEL), dtype=jnp.float32), 'gate_w': jax.random.normal(ks[1], (N_EXPERTS, D_MODEL), dtype=jnp.float32) * sc_d, 'w1': jax.random.normal(ks[2], (N_EXPERTS, D_MODEL, INTER), dtype=jnp.float32) * sc_d, 'b1': jnp.zeros((N_EXPERTS, INTER), dtype=jnp.float32), 'w2': jax.random.normal(ks[3], (N_EXPERTS, INTER, D_MODEL), dtype=jnp.float32) * sc_f, 'b2': jnp.zeros((N_EXPERTS, D_MODEL), dtype=jnp.float32), 'w3': jax.random.normal(ks[4], (N_EXPERTS, D_MODEL, INTER), dtype=jnp.float32) * sc_d, 'b3': jnp.zeros((N_EXPERTS, INTER), dtype=jnp.float32), 'sw1': jax.random.normal(ks[5], (D_MODEL, INTER), dtype=jnp.float32) * sc_d, 'sb1': jnp.zeros((INTER,), dtype=jnp.float32), 'sw2': jax.random.normal(ks[6], (INTER, D_MODEL), dtype=jnp.float32) * sc_f, 'sb2': jnp.zeros((D_MODEL,), dtype=jnp.float32), 'sw3': jax.random.normal(ks[7], (D_MODEL, INTER), dtype=jnp.float32) * sc_d, 'sb3': jnp.zeros((INTER,), dtype=jnp.float32)}
        return inp
    _L0_ffn_all = _L0_ffn_setup()
    _L0_ffn_in = {k: v for k, v in _L0_ffn_all.items() if k in ('gate_w', 'w1', 'b1', 'w2', 'b2', 'w3', 'b3', 'sw1', 'sb1', 'sw2', 'sb2', 'sw3', 'sb3')}
    del _L0_ffn_all

    def _L1_xattn_setup():
        import jax, jax.numpy as jnp
        import numpy as np
        NUM_HEADS = 16
        HIDDEN = 512
        B, S = (2, 1024)

        def _split_heads(x, H):
            b, s, d = x.shape
            return x.reshape(b, s, H, d // H).transpose(0, 2, 1, 3)
        key = jax.random.key(seed)
        ks = jax.random.split(key, 14)
        D = HIDDEN
        scale = 1.0 / np.sqrt(D)
        inp = {'query': jax.random.normal(ks[0], (B, S, D), jnp.float32), 'key_in': jax.random.normal(ks[1], (B, S, D), jnp.float32), 'value': jax.random.normal(ks[2], (B, S, D), jnp.float32), 'group_prob': jax.random.uniform(ks[3], (B, S, S), jnp.float32), 'mask': jax.random.randint(ks[4], (B, S, S), 0, 2, jnp.int32), 'wq_k': jax.random.normal(ks[5], (D, D), jnp.float32) * scale, 'wq_b': jnp.zeros((D,), jnp.float32), 'wk_k': jax.random.normal(ks[6], (D, D), jnp.float32) * scale, 'wk_b': jnp.zeros((D,), jnp.float32), 'wv_k': jax.random.normal(ks[7], (D, D), jnp.float32) * scale, 'wv_b': jnp.zeros((D,), jnp.float32), 'wo_k': jax.random.normal(ks[8], (D, D), jnp.float32) * scale, 'wo_b': jnp.zeros((D,), jnp.float32)}
        return inp
    _L1_xattn_all = _L1_xattn_setup()
    _L1_xattn_in = {k: v for k, v in _L1_xattn_all.items() if k in ('wq_k', 'wq_b', 'wk_k', 'wk_b', 'wv_k', 'wv_b', 'wo_k', 'wo_b')}
    del _L1_xattn_all

    def _L1_attn_setup():
        import jax, jax.numpy as jnp
        import numpy as np
        N_INPUT = 512
        N_HEAD = 16
        ATT_DIM = N_INPUT // N_HEAD * N_HEAD
        V_DIM = N_INPUT // 2 * N_HEAD
        COMB_DIM = 2 * ATT_DIM + V_DIM
        SCALE = (N_INPUT // N_HEAD) ** 0.5
        key = jax.random.key(seed)
        k1, k2, k3 = jax.random.split(key, 3)
        B, T = (8, 512)
        representations = jax.random.normal(k1, (B, T, N_INPUT), dtype=jnp.float32)
        Wc = jax.random.normal(k2, (COMB_DIM, N_INPUT), dtype=jnp.float32) * (0.1 * np.sqrt(2.0 / (COMB_DIM + N_INPUT)))
        bc = jnp.zeros((COMB_DIM,), dtype=jnp.float32)
        Wo = jax.random.normal(k3, (N_INPUT, V_DIM), dtype=jnp.float32) * (0.1 * np.sqrt(2.0 / (N_INPUT + V_DIM)))
        bo = jnp.zeros((N_INPUT,), dtype=jnp.float32)
        return {'representations': representations, 'Wc': Wc, 'bc': bc, 'Wo': Wo, 'bo': bo}
    _L1_attn_all = _L1_attn_setup()
    _L1_attn_in = {k: v for k, v in _L1_attn_all.items() if k in ('Wc', 'bc', 'Wo', 'bo')}
    del _L1_attn_all

    def _L1_ffn_setup():
        import jax, jax.numpy as jnp
        import numpy as np
        GROUP = 16
        EPS = 1e-05

        def _dequant(q, scale):
            w = q.astype(jnp.float32) / 7.5 - 1.0
            return w * jnp.repeat(scale, GROUP, axis=1)

        def _qlora_linear(x, q, scale, bias, la, lb):
            w = _dequant(q, scale)
            base = jnp.einsum('btd,od->bto', x, w) + bias
            lora = jnp.einsum('btr,or->bto', jnp.einsum('btd,rd->btr', x, la), lb)
            return base + lora

        def _layernorm(x, g, b):
            mu = jnp.mean(x, axis=-1, keepdims=True)
            var = jnp.mean(jnp.square(x - mu), axis=-1, keepdims=True)
            return (x - mu) * jax.lax.rsqrt(var + EPS) * g + b
        key = jax.random.key(seed)
        ks = jax.random.split(key, 6)
        D, R, B, T = (512, 32, 8, 2048)
        x = jax.random.normal(ks[0], (B, T, D), dtype=jnp.float32)
        qweights = jax.random.randint(ks[1], (6, D, D), 0, 16, dtype=jnp.int32)
        scales = jax.random.uniform(ks[2], (6, D, D // GROUP), dtype=jnp.float32)
        biases = jax.random.normal(ks[3], (6, D), dtype=jnp.float32) * 0.02
        lora_a = jax.random.normal(ks[4], (6, R, D), dtype=jnp.float32) * 0.02
        lora_b = jax.random.normal(ks[5], (6, D, R), dtype=jnp.float32) * 0.02
        ln_gamma = jnp.ones((3, D), dtype=jnp.float32)
        ln_beta = jnp.zeros((3, D), dtype=jnp.float32)
        return {'x': x, 'qweights': qweights, 'scales': scales, 'biases': biases, 'lora_a': lora_a, 'lora_b': lora_b, 'ln_gamma': ln_gamma, 'ln_beta': ln_beta}
    _L1_ffn_all = _L1_ffn_setup()
    _L1_ffn_in = {k: v for k, v in _L1_ffn_all.items() if k in ('qweights', 'scales', 'biases', 'lora_a', 'lora_b', 'ln_gamma', 'ln_beta')}
    del _L1_ffn_all
    return {'x': x, 'ctx_1024': ctx_1024, 'fside_BxSxS2_0': fside_BxSxS2_0, 'mask_BxSxS2_ik1': mask_BxSxS2_ik1, 'L0_attn_Wqkv': _L0_attn_in['Wqkv'], 'L0_attn_bqkv': _L0_attn_in['bqkv'], 'L0_attn_Wo': _L0_attn_in['Wo'], 'L0_attn_bo': _L0_attn_in['bo'], 'L0_ffn_gate_w': _L0_ffn_in['gate_w'], 'L0_ffn_w1': _L0_ffn_in['w1'], 'L0_ffn_b1': _L0_ffn_in['b1'], 'L0_ffn_w2': _L0_ffn_in['w2'], 'L0_ffn_b2': _L0_ffn_in['b2'], 'L0_ffn_w3': _L0_ffn_in['w3'], 'L0_ffn_b3': _L0_ffn_in['b3'], 'L0_ffn_sw1': _L0_ffn_in['sw1'], 'L0_ffn_sb1': _L0_ffn_in['sb1'], 'L0_ffn_sw2': _L0_ffn_in['sw2'], 'L0_ffn_sb2': _L0_ffn_in['sb2'], 'L0_ffn_sw3': _L0_ffn_in['sw3'], 'L0_ffn_sb3': _L0_ffn_in['sb3'], 'L1_xattn_wq_k': _L1_xattn_in['wq_k'], 'L1_xattn_wq_b': _L1_xattn_in['wq_b'], 'L1_xattn_wk_k': _L1_xattn_in['wk_k'], 'L1_xattn_wk_b': _L1_xattn_in['wk_b'], 'L1_xattn_wv_k': _L1_xattn_in['wv_k'], 'L1_xattn_wv_b': _L1_xattn_in['wv_b'], 'L1_xattn_wo_k': _L1_xattn_in['wo_k'], 'L1_xattn_wo_b': _L1_xattn_in['wo_b'], 'L1_attn_Wc': _L1_attn_in['Wc'], 'L1_attn_bc': _L1_attn_in['bc'], 'L1_attn_Wo': _L1_attn_in['Wo'], 'L1_attn_bo': _L1_attn_in['bo'], 'L1_ffn_qweights': _L1_ffn_in['qweights'], 'L1_ffn_scales': _L1_ffn_in['scales'], 'L1_ffn_biases': _L1_ffn_in['biases'], 'L1_ffn_lora_a': _L1_ffn_in['lora_a'], 'L1_ffn_lora_b': _L1_ffn_in['lora_b'], 'L1_ffn_ln_gamma': _L1_ffn_in['ln_gamma'], 'L1_ffn_ln_beta': _L1_ffn_in['ln_beta']}

def reference(x, ctx_1024, fside_BxSxS2_0, mask_BxSxS2_ik1, L0_attn_Wqkv, L0_attn_bqkv, L0_attn_Wo, L0_attn_bo, L0_ffn_gate_w, L0_ffn_w1, L0_ffn_b1, L0_ffn_w2, L0_ffn_b2, L0_ffn_w3, L0_ffn_b3, L0_ffn_sw1, L0_ffn_sb1, L0_ffn_sw2, L0_ffn_sb2, L0_ffn_sw3, L0_ffn_sb3, L1_xattn_wq_k, L1_xattn_wq_b, L1_xattn_wk_k, L1_xattn_wk_b, L1_xattn_wv_k, L1_xattn_wv_b, L1_xattn_wo_k, L1_xattn_wo_b, L1_attn_Wc, L1_attn_bc, L1_attn_Wo, L1_attn_bo, L1_ffn_qweights, L1_ffn_scales, L1_ffn_biases, L1_ffn_lora_a, L1_ffn_lora_b, L1_ffn_ln_gamma, L1_ffn_ln_beta):
    import jax
    import jax.numpy as jnp

    def _L0_xattn_ref(hidden_states, visual_hidden_state):
        import jax, jax.numpy as jnp
        import numpy as np
        scores = jnp.einsum('bld,bvd->blv', hidden_states, visual_hidden_state)
        probs = jax.nn.softmax(scores, axis=-1)
        return jnp.einsum('blv,bvd->bld', probs, visual_hidden_state)

    def _L0_attn_ref(x, Wqkv, bqkv, Wo, bo):
        import jax, jax.numpy as jnp
        import numpy as np
        EMBED = 512
        HEADS = 16
        HEAD_DIM = EMBED // HEADS
        B, S, E = x.shape
        qkv = x @ Wqkv + bqkv
        qkv = qkv.reshape(B, S, 3, HEADS, HEAD_DIM)
        qkv = jnp.transpose(qkv, (2, 0, 3, 1, 4))
        q, k, v = (qkv[0], qkv[1], qkv[2])
        scale = 1.0 / np.sqrt(HEAD_DIM).astype(np.float32)
        scores = jnp.einsum('bhqd,bhkd->bhqk', q, k) * scale
        attn = jax.nn.softmax(scores, axis=-1)
        out = jnp.einsum('bhqk,bhkd->bhqd', attn, v)
        out = jnp.transpose(out, (0, 2, 1, 3)).reshape(B, S, E)
        return out @ Wo + bo

    def _L0_ffn_ref(x, gate_w, w1, b1, w2, b2, w3, b3, sw1, sb1, sw2, sb2, sw3, sb3):
        import jax, jax.numpy as jnp
        import numpy as np
        from jax import lax
        D_MODEL = 512
        INTER = 512
        N_EXPERTS = 8
        TOP_K = 2
        ROUTE_SCALE = 1.0
        B, S = (2, 2048)
        Bx, Sx, D = x.shape
        xt = x.reshape(-1, D)
        scores = jax.nn.softmax((xt @ gate_w.T).astype(jnp.float32), axis=-1)
        top_vals, top_idx = lax.top_k(scores, TOP_K)
        weights = (top_vals * ROUTE_SCALE).astype(x.dtype)
        combine = jnp.sum(jax.nn.one_hot(top_idx, N_EXPERTS, dtype=x.dtype) * weights[..., None], axis=1)

        def body(acc, p):
            W1, B1, W2, B2, W3, B3, c = p
            h = jax.nn.silu(xt @ W1 + B1) * (xt @ W3 + B3)
            return (acc + c[:, None] * (h @ W2 + B2), None)
        y, _ = lax.scan(body, jnp.zeros_like(xt), (w1, b1, w2, b2, w3, b3, combine.T))
        z = jax.nn.silu(xt @ sw1 + sb1) * (xt @ sw3 + sb3) @ sw2 + sb2
        return (y + z).reshape(Bx, Sx, D)

    def _L1_xattn_ref(query, key_in, value, group_prob, mask, wq_k, wq_b, wk_k, wk_b, wv_k, wv_b, wo_k, wo_b):
        import jax, jax.numpy as jnp
        import numpy as np
        NUM_HEADS = 16
        HIDDEN = 512
        B, S = (2, 1024)

        def _split_heads(x, H):
            b, s, d = x.shape
            return x.reshape(b, s, H, d // H).transpose(0, 2, 1, 3)
        H = NUM_HEADS
        dh = query.shape[-1] // H
        q = _split_heads(query @ wq_k + wq_b, H)
        k = _split_heads(key_in @ wk_k + wk_b, H)
        v = _split_heads(value @ wv_k + wv_b, H)
        logits = jnp.einsum('bhqd,bhkd->bhqk', q, k) / jnp.sqrt(jnp.asarray(dh, q.dtype))
        neg = (1.0 - mask.astype(q.dtype)) * -1000000000.0
        logits = logits + neg[:, None, :, :]
        attn = jax.nn.softmax(logits, axis=-1)
        attn = attn * group_prob[:, None, :, :]
        out = jnp.einsum('bhqk,bhkd->bhqd', attn, v)
        out = out.transpose(0, 2, 1, 3).reshape(query.shape[0], -1, H * dh)
        return out @ wo_k + wo_b

    def _L1_attn_ref(representations, Wc, bc, Wo, bo):
        import jax, jax.numpy as jnp
        import numpy as np
        N_INPUT = 512
        N_HEAD = 16
        ATT_DIM = N_INPUT // N_HEAD * N_HEAD
        V_DIM = N_INPUT // 2 * N_HEAD
        COMB_DIM = 2 * ATT_DIM + V_DIM
        SCALE = (N_INPUT // N_HEAD) ** 0.5
        B, T, D = representations.shape
        H = N_HEAD
        dh = ATT_DIM // H
        dv = V_DIM // H
        cp = jax.nn.leaky_relu(jnp.einsum('btd,cd->btc', representations, Wc) + bc)
        q = cp[..., :ATT_DIM].reshape(B, T, H, dh)
        k = cp[..., ATT_DIM:2 * ATT_DIM].reshape(B, T, H, dh)
        v = cp[..., 2 * ATT_DIM:].reshape(B, T, H, dv)
        scores = jnp.einsum('bqhd,bkhd->bhqk', q, k) / SCALE
        attn = jax.nn.softmax(scores, axis=-1)
        out = jnp.einsum('bhqk,bkhd->bqhd', attn, v).reshape(B, T, V_DIM)
        proj = jax.nn.leaky_relu(jnp.einsum('btv,dv->btd', out, Wo) + bo)
        return representations + proj

    def _L1_ffn_ref(x, qweights, scales, biases, lora_a, lora_b, ln_gamma, ln_beta):
        import jax, jax.numpy as jnp
        import numpy as np
        GROUP = 16
        EPS = 1e-05

        def _dequant(q, scale):
            w = q.astype(jnp.float32) / 7.5 - 1.0
            return w * jnp.repeat(scale, GROUP, axis=1)

        def _qlora_linear(x, q, scale, bias, la, lb):
            w = _dequant(q, scale)
            base = jnp.einsum('btd,od->bto', x, w) + bias
            lora = jnp.einsum('btr,or->bto', jnp.einsum('btd,rd->btr', x, la), lb)
            return base + lora

        def _layernorm(x, g, b):
            mu = jnp.mean(x, axis=-1, keepdims=True)
            var = jnp.mean(jnp.square(x - mu), axis=-1, keepdims=True)
            return (x - mu) * jax.lax.rsqrt(var + EPS) * g + b
        h = x
        for blk in range(3):
            i0, i1 = (2 * blk, 2 * blk + 1)
            y = _qlora_linear(h, qweights[i0], scales[i0], biases[i0], lora_a[i0], lora_b[i0])
            y = _layernorm(y, ln_gamma[blk], ln_beta[blk])
            y = jax.nn.gelu(y, approximate=False)
            y = _qlora_linear(y, qweights[i1], scales[i1], biases[i1], lora_a[i1], lora_b[i1])
            h = y + h
        return h
    x = x + _L0_xattn_ref(_layernorm(x, axis=-1), ctx_1024)
    x = x + _L0_attn_ref(_layernorm(x, axis=-1), L0_attn_Wqkv, L0_attn_bqkv, L0_attn_Wo, L0_attn_bo)
    x = x + _L0_ffn_ref(_layernorm(x, axis=-1), L0_ffn_gate_w, L0_ffn_w1, L0_ffn_b1, L0_ffn_w2, L0_ffn_b2, L0_ffn_w3, L0_ffn_b3, L0_ffn_sw1, L0_ffn_sb1, L0_ffn_sw2, L0_ffn_sb2, L0_ffn_sw3, L0_ffn_sb3)
    x = x + _L1_xattn_ref(_layernorm(x, axis=-1), ctx_1024, ctx_1024, fside_BxSxS2_0, mask_BxSxS2_ik1, L1_xattn_wq_k, L1_xattn_wq_b, L1_xattn_wk_k, L1_xattn_wk_b, L1_xattn_wv_k, L1_xattn_wv_b, L1_xattn_wo_k, L1_xattn_wo_b)
    x = x + _L1_attn_ref(_layernorm(x, axis=-1), L1_attn_Wc, L1_attn_bc, L1_attn_Wo, L1_attn_bo)
    x = x + _L1_ffn_ref(_layernorm(x, axis=-1), L1_ffn_qweights, L1_ffn_scales, L1_ffn_biases, L1_ffn_lora_a, L1_ffn_lora_b, L1_ffn_ln_gamma, L1_ffn_ln_beta)
    return x

_drawn_inputs = setup_inputs


def setup_inputs(seed=0):
    import zlib

    import numpy as np

    out = dict(_drawn_inputs(seed))
    spreads = {'L0_ffn_b1': (0.0, 0.501),
     'L0_ffn_b2': (0.0, 0.306),
     'L0_ffn_b3': (0.0, 0.514),
     'L0_ffn_sb1': (0.0, 0.325),
     'L0_ffn_sb2': (0.0, 0.1),
     'L0_ffn_sb3': (0.0, 0.342),
     'L1_xattn_wq_b': (0.0, 0.8),
     'L1_xattn_wk_b': (0.0, 2.0),
     'L1_xattn_wv_b': (0.0, 0.308),
     'L1_xattn_wo_b': (0.0, 0.1),
     'L1_attn_bc': (0.0, 0.8),
     'L1_attn_bo': (0.0, 0.383),
     'L1_ffn_ln_gamma': (1.0, 0.2),
     'L1_ffn_ln_beta': (0.0, 0.1)}
    factors = {'fside_BxSxS2_0': 7.027,
     'L0_attn_bqkv': 5.156,
     'L0_attn_bo': 2.8,
     'L1_attn_Wc': 8.0,
     'L1_attn_Wo': 8.0,
     'L1_ffn_biases': 8.0,
     'L1_ffn_lora_a': 4.89,
     'L1_ffn_lora_b': 4.855}
    for name, (base, spread) in spreads.items():
        noise = np.random.default_rng([zlib.crc32(name.encode()), seed]).standard_normal(out[name].shape)
        drawn = base * np.exp(spread * noise) if base else spread * noise
        out[name] = jnp.asarray(drawn.astype(out[name].dtype))
    for name, factor in factors.items():
        out[name] = (out[name] * factor).astype(out[name].dtype)
    return out
```

```python
from contextlib import ExitStack
from math import sqrt

import concourse.bass as bass
from concourse import mybir

F32 = mybir.dt.float32
F32R = mybir.dt.float32r
I32 = mybir.dt.int32
ALU = mybir.AluOpType
ACT = mybir.ActivationFunctionType
AX_X = mybir.AxisListType.X

P = 128
B, S, D = 8, 64, 512
TOK = B * S
NT = TOK // P
KT = D // P
S2 = 1601
S2P = S2 + 1
CH0 = [0, 402, 802, 1202]
CHW = [402, 400, 400, 400]
CHV = [402, 400, 400, 399]
NJ = 13
JR = [P] * 12 + [S2 - 12 * P]
JG = [(0, 4), (4, 8), (8, 12), (12, 13)]
H = 16
HG = 4
NG = H // HG
DH = D // H
NE = 9
EPS = 1e-5
LOW = -3.0e38


def as_f32(ap):
    return ap.bitcast(F32)


def three(hi_a, lo_a, hi_b, lo_b):
    return ((hi_a, hi_b), (hi_a, lo_b), (lo_a, hi_b))


class Memory:

    def __init__(self, nc, ctx, stage):
        self.nc, self.ctx, self.stage = nc, ctx, stage
        self.used = []
        ctx.callback(self.clear)

    def sb(self, name, shape, dt=F32):
        return self.ctx.enter_context(self.nc.sbuf_tensor(f"{self.stage}_{name}", shape, dt))

    def pb(self, name, shape, dt=F32):
        return self.ctx.enter_context(self.nc.psum_tensor(f"{self.stage}_{name}", shape, dt))

    def sem(self, name):
        self.used.append(self.nc.alloc_semaphore(f"{self.stage}_{name}"))
        return self.used[-1]

    def clear(self):
        if self.used:
            self.nc.clear_and_free_semaphores(self.used)
            self.nc.all_engine_barrier()

    def sems(self, name, n):
        return [self.sem(f"{name}{i}") for i in range(n)]


def layernorm(nc, stage, x, xn, xT_hi, xT_lo, ident):
    with ExitStack() as ctx:
        m = Memory(nc, ctx, stage)
        stats = m.sb("stats", [P, NT, 6])
        mv = m.sb("mv", [P, NT, 2])
        var = m.sb("var", [P, NT])
        std = m.sb("std", [P, NT])
        rstd = m.sb("rstd", [P, NT])
        turned = m.pb("turned", [P, KT, TOK])
        stats_ready, mv_ready, var_ready = m.sem("stats_ready"), m.sem("mv_ready"), m.sem("var_ready")
        std_ready, rstd_ready, xn_ready = m.sem("std_ready"), m.sem("rstd_ready"), m.sem("xn_ready")
        turned_ready, hi_ready, lo_ready = m.sem("turned_ready"), m.sem("hi_ready"), m.sem("lo_ready")
        block = ctx.enter_context(nc.Block())

        @block.vector
        def _(dve):
            for t in range(NT):
                dve.bn_stats(stats[:, t, :], x[:, t, :]).then_inc(stats_ready, 1)
            for t in range(NT):
                dve.wait_ge(stats_ready, t + 1)
                dve.bn_aggr(mv[:, t, :], stats[:, t, :]).then_inc(mv_ready, 1)
            dve.wait_ge(mv_ready, NT)
            dve.tensor_scalar(var[:, :], mv[:, :, 1], EPS, None, ALU.add).then_inc(var_ready, 1)
            dve.wait_ge(std_ready, 1)
            dve.reciprocal(rstd[:, :], std[:, :]).then_inc(rstd_ready, 1)
            dve.wait_ge(rstd_ready, 1)
            for t in range(NT):
                dve.tensor_scalar(xn[:, t, :], x[:, t, :], mv[:, t, 0:1], rstd[:, t:t + 1],
                                  ALU.subtract, ALU.mult).then_inc(xn_ready, 1)
            for k in range(KT):
                dve.wait_ge(hi_ready, k + 1)
                dve.tensor_tensor(xT_lo[:, k, :], turned[:, k, :], as_f32(xT_hi[:, k, :]),
                                  ALU.subtract).then_inc(lo_ready, 1)

        @block.scalar
        def _(act):
            act.wait_ge(var_ready, 1)
            act.activation(std[:, :], var[:, :], ACT.Sqrt).then_inc(std_ready, 1)
            for k in range(KT):
                act.wait_ge(turned_ready, k + 1)
                act.activation(xT_hi[:, k, :], turned[:, k, :], ACT.Copy).then_inc(hi_ready, 1)

        @block.tensor
        def _(pe):
            for t in range(NT):
                pe.wait_ge(xn_ready, t + 1)
                for k in range(KT):
                    turn = pe.transpose(turned[:, k, t * P:(t + 1) * P], xn[:, t, k * P:(k + 1) * P], ident[:, :])
                    if t == NT - 1:
                        turn.then_inc(turned_ready, 1)


def context_attention(nc, stage, x, xT_hi, xT_lo, ident, ctxT, ctxN):
    with ExitStack() as ctx:
        m = Memory(nc, ctx, stage)
        raw_T = m.sb("raw_T", [P, KT, S2P])
        T_hi, T_lo = m.sb("T_hi", [P, KT, S2P], F32R), m.sb("T_lo", [P, KT, S2P], F32R)
        raw_N = m.sb("raw_N", [P, NJ, D])
        N_hi, N_lo = m.sb("N_hi", [P, NJ, D], F32R), m.sb("N_lo", [P, NJ, D], F32R)
        xs = m.sb("xs", [P, KT, 2 * S], F32R)
        below = m.sb("below", [S, S2P])
        sc = m.sb("sc", [S, S2P])
        pT = m.sb("pT", [P, NJ, 2 * S], F32R)
        cmax = m.sb("cmax", [S, 4])
        rmax = m.sb("rmax", [S, 1])
        nmax = m.sb("nmax", [S, 1])
        rsum = m.sb("rsum", [S, 1])
        rinv = m.sb("rinv", [S, 1])
        o_below = below[:, 0:D]
        o_sum = below[:, D:2 * D]
        o_norm = m.sb("o_norm", [P, D])
        ps_s = m.pb("ps_s", [P, 4, 512])
        ps_t = m.pb("ps_t", [P, 16, S])
        ps_o = m.pb("ps_o", [P, D])

        T_loaded, T_hi_ready, T_lo_ready, T_used = (m.sems(n, KT) for n in ("T_loaded", "T_hi_ready", "T_lo_ready", "T_used"))
        N_loaded, N_hi_ready, N_lo_ready, N_used = (m.sems(n, len(JG)) for n in ("N_loaded", "N_hi_ready", "N_lo_ready", "N_used"))
        xs_ready, below_ready, sum_ready, rmax_ready, nmax_ready = (m.sem(n) for n in ("xs_ready", "below_ready", "sum_ready", "rmax_ready", "nmax_ready"))
        exp_ready, rinv_ready, pT_turned, pT_hi_ready, pT_ready = (m.sem(n) for n in ("exp_ready", "rinv_ready", "pT_turned", "pT_hi_ready", "pT_ready"))
        waited = m.sems("waited", 2)
        o_below_ready, o_sum_ready, o_norm_ready, x_ready = (m.sem(n) for n in ("o_below_ready", "o_sum_ready", "o_norm_ready", "x_ready"))
        block = ctx.enter_context(nc.Block())

        @block.sync
        def _(sp):
            with sp.Fori(0, B) as b:
                for k in range(KT):
                    sp.wait_ge(T_lo_ready[k], b)
                    sp.dma_start(raw_T[:, k, :], ctxT[b, :, k, :]).then_inc(T_loaded[k], 16)
                for g, (j0, j1) in enumerate(JG):
                    sp.wait_ge(N_lo_ready[g], b)
                    if g < 3:
                        rows = ctxN[b, j0 * P:j1 * P, :].rearrange("(j p) d -> p j d", p=P)
                        sp.dma_start(raw_N[:, j0:j1, :], rows).then_inc(N_loaded[g], 16)
                    else:
                        sp.dma_start(raw_N[0:JR[-1], j0, :], ctxN[b, j0 * P:S2, :]).then_inc(N_loaded[g], 16)

        @block.scalar
        def _(act):
            def split_T(b):
                for k in range(KT):
                    act.wait_ge(T_loaded[k], 16 * (b + 1))
                    act.wait_ge(T_used[k], b)
                    act.activation(T_hi[:, k, :], raw_T[:, k, :], ACT.Copy).then_inc(T_hi_ready[k], 1)

            def split_N(b):
                for g, (j0, j1) in enumerate(JG):
                    r = JR[j0]
                    act.wait_ge(N_loaded[g], 16 * (b + 1))
                    act.wait_ge(N_used[g], b)
                    act.activation(N_hi[0:r, j0:j1, :], raw_N[0:r, j0:j1, :], ACT.Copy).then_inc(N_hi_ready[g], 1)

            def copy_below(b):
                act.wait_ge(T_used[KT - 1], b + 1)
                act.wait_ge(x_ready, b)
                for c in range(4):
                    act.activation(below[:, CH0[c]:CH0[c] + CHW[c]], ps_s[S:2 * S, c, 0:CHW[c]],
                                   ACT.Copy).then_inc(below_ready, 1)

            def exps(b):
                act.wait_ge(nmax_ready, b + 1)
                act.activation(sc[:, 0:S2], sc[:, 0:S2], ACT.Exp, bias=nmax[:, :],
                               accum_out=rsum[:, :]).then_inc(exp_ready, 1)

            def turned_high(b):
                act.wait_ge(pT_turned, b + 1)
                act.wait_ge(N_used[len(JG) - 1], b)
                for j0, j1, r in ((0, 8, P), (8, 12, P), (12, 13, JR[-1])):
                    act.activation(pT[0:r, j0:j1, 0:S], ps_t[0:r, j0:j1, :], ACT.Copy).then_inc(pT_hi_ready, 1)

            def out_below(b):
                act.wait_ge(N_used[len(JG) - 1], b + 1)
                act.activation(o_below, ps_o[S:2 * S, :], ACT.Copy).then_inc(o_below_ready, 1)

            with act.Fori(0, NT) as t:
                split_T(2 * t)
                copy_below(2 * t)
                split_N(2 * t)
                split_T(2 * t + 1)
                exps(2 * t)
                turned_high(2 * t)
                out_below(2 * t)
                copy_below(2 * t + 1)
                split_N(2 * t + 1)
                exps(2 * t + 1)
                turned_high(2 * t + 1)
                out_below(2 * t + 1)

        @block.gpsimd
        def _(pool):
            with pool.Fori(0, B) as b:
                for g, (j0, j1) in enumerate(JG):
                    r = JR[j0]
                    pool.wait_ge(N_hi_ready[g], b + 1)
                    pool.tensor_tensor(N_lo[0:r, j0:j1, :], raw_N[0:r, j0:j1, :], as_f32(N_hi[0:r, j0:j1, :]),
                                       ALU.subtract).then_inc(N_lo_ready[g], 1)

        @block.vector
        def _(dve):
            def stage_x(b):
                dve.wait_ge(T_used[KT - 1], b)
                dve.tensor_copy(xs[:, :, 0:S], as_f32(xT_hi[:, :, bass.ts(b, S)])).then_inc(xs_ready, 1)
                dve.tensor_copy(xs[:, :, S:2 * S], as_f32(xT_lo[:, :, bass.ts(b, S)])).then_inc(xs_ready, 1)

            def split_T(b):
                for k in range(KT):
                    dve.wait_ge(T_hi_ready[k], b + 1)
                    dve.tensor_tensor(T_lo[:, k, :], raw_T[:, k, :], as_f32(T_hi[:, k, :]),
                                      ALU.subtract).then_inc(T_lo_ready[k], 1)

            def scores_max(b):
                dve.wait_ge(pT_turned, b)
                for c in range(4):
                    dve.wait_ge(below_ready, 4 * b + c + 1)
                    dve.sem_inc(waited[0], 1)
                    w = CHV[c]
                    dve.tensor_tensor_reduce(sc[:, CH0[c]:CH0[c] + w], ps_s[0:S, c, 0:w],
                                             below[:, CH0[c]:CH0[c] + w], 1.0, LOW, ALU.add, ALU.max,
                                             cmax[:, c:c + 1]).then_inc(sum_ready, 1)
                dve.wait_ge(sum_ready, 4 * b + 4)
                dve.tensor_reduce(rmax[:, :], cmax[:, :], AX_X, ALU.max).then_inc(rmax_ready, 1)
                dve.wait_ge(rmax_ready, b + 1)
                dve.tensor_scalar(nmax[:, :], rmax[:, :], -1.0, None, ALU.mult).then_inc(nmax_ready, 1)

            def turned_low(b):
                for i, (j0, j1, r) in enumerate(((0, 8, P), (8, 12, P), (12, 13, JR[-1]))):
                    dve.wait_ge(pT_hi_ready, 3 * b + (1 if i == 0 else 3))
                    dve.tensor_tensor(pT[0:r, j0:j1, S:2 * S], ps_t[0:r, j0:j1, :], as_f32(pT[0:r, j0:j1, 0:S]),
                                      ALU.subtract).then_inc(pT_ready, 1)

            def add_out(b, t, half):
                q = slice(S * half, S * half + S)
                dve.wait_ge(exp_ready, b + 1)
                dve.reciprocal(rinv[:, :], rsum[:, :]).then_inc(rinv_ready, 1)
                dve.wait_ge(o_below_ready, b + 1)
                dve.tensor_tensor(o_sum, ps_o[0:S, :], o_below, ALU.add).then_inc(o_sum_ready, 1)
                dve.wait_ge(rinv_ready, b + 1)
                dve.wait_ge(o_sum_ready, b + 1)
                dve.tensor_scalar(o_norm[q, :], o_sum, rinv[:, 0:1], None, ALU.mult).then_inc(o_norm_ready, 1)
                dve.wait_ge(o_norm_ready, b + 1)
                dve.tensor_tensor(x[q, t, :], x[q, t, :], o_norm[q, :], ALU.add).then_inc(x_ready, 1)

            with dve.Fori(0, NT) as t:
                stage_x(2 * t)
                split_T(2 * t)
                scores_max(2 * t)
                stage_x(2 * t + 1)
                split_T(2 * t + 1)
                turned_low(2 * t)
                add_out(2 * t, t, 0)
                scores_max(2 * t + 1)
                turned_low(2 * t + 1)
                add_out(2 * t + 1, t, 1)

        @block.tensor
        def _(pe):
            def scores(b):
                pe.wait_ge(xs_ready, 2 * b + 2)
                pe.wait_ge(sum_ready, 4 * b)
                for k in range(KT):
                    pe.wait_ge(T_lo_ready[k], b + 1)
                    for c in range(4):
                        cols = slice(CH0[c], CH0[c] + CHW[c])
                        pairs = [(2 * S, T_hi), (S, T_lo)] if k < KT - 1 else [(S, T_lo), (2 * S, T_hi)]
                        for n, (rows, half) in enumerate(pairs):
                            mm = pe.matmul(ps_s[0:rows, c, 0:CHW[c]], xs[:, k, 0:rows], half[:, k, cols],
                                           start=(k == 0 and n == 0), stop=(k == KT - 1 and n == 1))
                    mm.then_inc(T_used[k], 1)

            def turn(b):
                pe.wait_ge(pT_ready, 3 * b)
                pe.wait_ge(exp_ready, b + 1)
                pe.sem_inc(waited[1], 1)
                for j in range(NJ):
                    last = pe.transpose(ps_t[0:JR[j], j, :], sc[:, j * P:j * P + JR[j]], ident[0:S, 0:S])
                last.then_inc(pT_turned, 1)

            def values(b):
                pe.wait_ge(pT_ready, 3 * b + 3)
                pe.wait_ge(o_sum_ready, b)
                for g, (j0, j1) in enumerate(JG):
                    pe.wait_ge(N_lo_ready[g], b + 1)
                    for j in range(j0, j1):
                        r = JR[j]
                        pairs = [(2 * S, N_hi), (S, N_lo)] if j < NJ - 1 else [(S, N_lo), (2 * S, N_hi)]
                        for n, (rows, half) in enumerate(pairs):
                            mm = pe.matmul(ps_o[0:rows, :], pT[0:r, j, 0:rows], half[0:r, j, :],
                                           start=(j == 0 and n == 0), stop=(j == NJ - 1 and n == 1))
                    mm.then_inc(N_used[g], 1)

            with pe.Fori(0, NT) as t:
                scores(2 * t)
                turn(2 * t)
                scores(2 * t + 1)
                values(2 * t)
                turn(2 * t + 1)
                values(2 * t + 1)


def head_attention(nc, stage, x, xn, xT_hi, xT_lo, ident, wqk, wv, wo, bqk, bv, bo, dv, rectified):
    parts = max(1, HG * dv // 512)
    vc = HG * dv // parts
    hp = HG // parts
    ko = vc // P
    kc = max(1, dv // P)
    proj = 2 + 2 * NT * parts
    scale = 1.0 / sqrt(DH)
    with ExitStack() as ctx:
        m = Memory(nc, ctx, stage)
        raw_qk = m.sb("raw_qk", [P, KT, 2 * P])
        raw_v = m.sb("raw_v", [P, KT, vc])
        raw_o = m.sb("raw_o", [P, ko, D])
        qk_hi, qk_lo = m.sb("qk_hi", [P, KT, 2 * P], F32R), m.sb("qk_lo", [P, KT, 2 * P], F32R)
        wv_hi, wv_lo = m.sb("wv_hi", [P, KT, vc], F32R), m.sb("wv_lo", [P, KT, vc], F32R)
        wo_hi, wo_lo = m.sb("wo_hi", [P, ko, D], F32R), m.sb("wo_lo", [P, ko, D], F32R)
        bqk_sb = m.sb("bqk_sb", [P, NG, 2])
        bv_sb = m.sb("bv_sb", [P, parts, vc])
        qk = m.sb("qk", [P, 2, TOK])
        v_sum = m.sb("v_sum", [P, 2, vc])
        v_hi, v_lo = m.sb("v_hi", [P, NT, vc], F32R), m.sb("v_lo", [P, NT, vc], F32R)
        smax, rsum, rinv = m.sb("smax", [P, HG, NT]), m.sb("rsum", [P, HG, NT]), m.sb("rinv", [P, HG, NT])
        sc = m.sb("sc", [P, HG, NT, S])
        probs = m.sb("probs", [P, HG, NT, P])
        pT_hi, pT_lo = m.sb("pT_hi", [P, 2, TOK], F32R), m.sb("pT_lo", [P, 2, TOK], F32R)
        o_hi, o_lo = m.sb("o_hi", [P, ko, TOK], F32R), m.sb("o_lo", [P, ko, TOK], F32R)
        y = m.sb("y", [P, NT, D])
        ps_p = m.pb("ps_p", [P, 2, 512])
        ps_s = m.pb("ps_s", [P, HG, 512])
        ps_o = m.pb("ps_o", [P, 2, 512])

        start_loaded, qk_loaded, v_loaded, o_loaded, bv_loaded = (m.sem(n) for n in ("start_loaded", "qk_loaded", "v_loaded", "o_loaded", "bv_loaded"))
        wqk_hi_ready, wqk_ready, wv_hi_ready, wv_ready, wo_hi_ready, wo_ready = (m.sem(n) for n in (
            "wqk_hi_ready", "wqk_ready", "wv_hi_ready", "wv_ready", "wo_hi_ready", "wo_ready"))
        proj_done = m.sem("proj_done")
        proj_free = m.sems("proj_free", 2)
        qk_sum_ready, qk_ready, scores_done, smax_ready, sub_ready = (m.sem(n) for n in ("qk_sum_ready", "qk_ready", "scores_done", "smax_ready", "sub_ready"))
        exp_ready, rsum_ready, rinv_ready, zero_ready, probs_ready = (m.sem(n) for n in ("exp_ready", "rsum_ready", "rinv_ready", "zero_ready", "probs_ready"))
        turned, pT_hi_ready, pT_ready = (m.sem(n) for n in ("turned", "pT_hi_ready", "pT_ready"))
        v_sum_ready, v_hi_ready, v_ready = (m.sem(n) for n in ("v_sum_ready", "v_hi_ready", "v_ready"))
        o_done, o_hi_ready, o_ready, x_ready = (m.sem(n) for n in ("o_done", "o_hi_ready", "o_ready", "x_ready"))
        block = ctx.enter_context(nc.Block())

        def v_use(part, t):
            return 2 + part * 2 * NT + t if part == 0 else 2 + NT + (part - 1) * 2 * NT + t

        def y_use(part, t):
            return 2 + 2 * NT + part * 2 * NT + t if part < parts - 1 else 2 + (2 * parts - 1) * NT + t

        n_o = ko if dv >= P else HG

        def freed(g, u):
            return g * (proj // 2) + u // 2 + 1

        def wait_v_sum(eng, g, part, t):
            u = v_use(part, t)
            if rectified:
                eng.wait_ge(v_sum_ready, (g * parts + part) * NT + t + 1)
            else:
                eng.wait_ge(proj_free[u % 2], freed(g, u))

        def outputs_of(g, h):
            return g * parts * n_o + h * kc

        @block.sync
        def _(sp):
            sp.dma_start(bqk_sb[:, :, :], bqk).then_inc(start_loaded, 16)
            for t in range(NT):
                sp.dma_start(y[:, t, :], bo.to_broadcast([P, D])).then_inc(start_loaded, 16)
            with sp.Fori(0, NG) as g:
                sp.wait_ge(wqk_ready, g)
                sp.dma_start(raw_qk[:, :, :], wqk[g]).then_inc(qk_loaded, 16)
                sp.wait_ge(v_ready, g * parts * NT)
                sp.dma_start(bv_sb[:, :, :].rearrange("p a c -> p (a c)"),
                             bv[g].to_broadcast([P, HG * dv])).then_inc(bv_loaded, 16)
                for part in range(parts):
                    sp.wait_ge(wv_ready, g * parts + part)
                    sp.dma_start(raw_v[:, :, :], wv[g, part]).then_inc(v_loaded, 16)
                    sp.wait_ge(wo_ready, g * parts + part)
                    sp.dma_start(raw_o[:, :, :], wo[g, part]).then_inc(o_loaded, 16)

        @block.scalar
        def _(act):
            def split_qk(g):
                act.wait_ge(qk_loaded, 16 * (g + 1))
                act.wait_ge(proj_done, g * proj)
                act.activation(qk_hi[:, :, :], raw_qk[:, :, :], ACT.Copy).then_inc(wqk_hi_ready, 1)

            def split_v(g, part):
                act.wait_ge(v_loaded, 16 * (g * parts + part + 1))
                act.wait_ge(proj_done, g * proj + (v_use(part - 1, NT - 1) + 1 if part else 0))
                act.activation(wv_hi[:, :, :], raw_v[:, :, :], ACT.Copy).then_inc(wv_hi_ready, 1)

            def split_o(g, part):
                act.wait_ge(o_loaded, 16 * (g * parts + part + 1))
                act.wait_ge(proj_done, g * proj + (y_use(part - 1, NT - 1) + 1 if part else 0))
                act.activation(wo_hi[:, :, :], raw_o[:, :, :], ACT.Copy).then_inc(wo_hi_ready, 1)

            def values_high(g, part, t):
                wait_v_sum(act, g, part, t)
                act.wait_ge(o_done, outputs_of(g, part * hp))
                act.activation(v_hi[:, t, :], v_sum[:, t % 2, :], ACT.Copy).then_inc(v_hi_ready, 1)

            def turned_high(g, h):
                act.wait_ge(turned, g * HG + h + 1)
                act.wait_ge(o_done, outputs_of(g, max(0, h - 1)))
                act.activation(pT_hi[:, h % 2, :], ps_s[:, h, :], ACT.Copy).then_inc(pT_hi_ready, 1)

            def outputs_high(g, part):
                act.wait_ge(proj_done, g * proj + (y_use(part - 1, NT - 1) + 1 if part else 0))
                for i in range(n_o):
                    n = part * n_o + i
                    act.wait_ge(o_done, g * parts * n_o + n + 1)
                    if dv >= P:
                        act.activation(o_hi[:, i, :], ps_o[:, n % 2, :], ACT.Copy).then_inc(o_hi_ready, 1)
                    else:
                        rows = slice(dv * i, dv * i + dv)
                        act.activation(o_hi[rows, 0, :], ps_o[rows, n % 2, :], ACT.Copy).then_inc(o_hi_ready, 1)

            with act.Fori(0, NG) as g:
                split_qk(g)
                split_v(g, 0)
                split_o(g, 0)
                act.wait_ge(sub_ready, HG * (g + 1))
                act.activation(sc[:, :, :, :], sc[:, :, :, :], ACT.Exp, scale=scale).then_inc(exp_ready, 1)
                for part in range(parts):
                    for t in range(NT):
                        values_high(g, part, t)
                    if part:
                        split_o(g, part)
                    for h in range(part * hp, (part + 1) * hp):
                        turned_high(g, h)
                    if part < parts - 1:
                        outputs_high(g, part)
                        split_v(g, part + 1)
                outputs_high(g, parts - 1)

        @block.gpsimd
        def _(pool):
            pool.memset(probs[:, :, :, :], 0.0).then_inc(zero_ready, 1)

            def split_o(g, part):
                pool.wait_ge(wo_hi_ready, g * parts + part + 1)
                pool.tensor_tensor(wo_lo[:, :, :], raw_o[:, :, :], as_f32(wo_hi[:, :, :]), ALU.subtract).then_inc(wo_ready, 1)

            with pool.Fori(0, NG) as g:
                pool.wait_ge(wqk_hi_ready, g + 1)
                pool.tensor_tensor(qk_lo[:, :, :], raw_qk[:, :, :], as_f32(qk_hi[:, :, :]), ALU.subtract).then_inc(wqk_ready, 1)
                for part in range(parts):
                    pool.wait_ge(wv_hi_ready, g * parts + part + 1)
                    pool.tensor_tensor(wv_lo[:, :, :], raw_v[:, :, :], as_f32(wv_hi[:, :, :]), ALU.subtract).then_inc(wv_ready, 1)
                    if part == 0:
                        split_o(g, 0)
                    for t in range(NT):
                        n = (g * parts + part) * NT + t
                        pool.wait_ge(v_hi_ready, n + 1)
                        pool.tensor_tensor(v_lo[:, t, :], v_sum[:, t % 2, :], as_f32(v_hi[:, t, :]), ALU.subtract).then_inc(v_ready, 1)
                    if part:
                        split_o(g, part)

        @block.vector
        def _(dve):
            def use(g, n):
                dve.wait_ge(proj_done, g * proj + n + 1)
                return ps_p[:, n % 2, :]

            def query_key(g, i):
                dve.wait_ge(scores_done, g)
                if rectified:
                    dve.tensor_scalar(qk[:, i, :], use(g, i), bqk_sb[:, g, i:i + 1], None,
                                      ALU.add).then_inc(proj_free[i], 1)
                    dve.wait_ge(proj_free[i], freed(g, i))
                    dve.scalar_tensor_tensor(out=qk[:, i, :], in0=qk[:, i, :], scalar=0.01, in1=qk[:, i, :],
                                             op0=ALU.mult, op1=ALU.max).then_inc(qk_ready, 1)
                else:
                    dve.tensor_scalar(qk[:, i, :], use(g, i), bqk_sb[:, g, i:i + 1], None,
                                      ALU.add).then_inc(proj_free[i], 1)

            def values(g, part, t):
                u = v_use(part, t)
                full = use(g, u)
                dve.wait_ge(v_ready, (g * parts + part) * NT + (t - 1 if t >= 2 else 0))
                dve.tensor_tensor(v_sum[:, t % 2, :], full[:, 0:vc], bv_sb[:, part, :], ALU.add)\
                   .then_inc(proj_free[u % 2], 1)
                if rectified:
                    dve.wait_ge(proj_free[u % 2], freed(g, u))
                    dve.scalar_tensor_tensor(out=v_sum[:, t % 2, :], in0=v_sum[:, t % 2, :], scalar=0.01,
                                             in1=v_sum[:, t % 2, :], op0=ALU.mult, op1=ALU.max).then_inc(v_sum_ready, 1)

            def turned_low(g, h):
                dve.wait_ge(pT_hi_ready, g * HG + h + 1)
                dve.tensor_tensor(pT_lo[:, h % 2, :], ps_s[:, h, :], as_f32(pT_hi[:, h % 2, :]),
                                  ALU.subtract).then_inc(pT_ready, 1)

            def outputs_low(g, part):
                for i in range(n_o):
                    n = part * n_o + i
                    dve.wait_ge(o_hi_ready, g * parts * n_o + n + 1)
                    k, rows = (i, slice(0, P)) if dv >= P else (0, slice(dv * i, dv * i + dv))
                    dve.tensor_tensor(o_lo[rows, k, :], ps_o[rows, n % 2, :], as_f32(o_hi[rows, k, :]),
                                      ALU.subtract).then_inc(o_ready, 1)

            def add_y(g, part, t):
                u = y_use(part, t)
                full = use(g, u)
                if part:
                    before = y_use(part - 1, t)
                    dve.wait_ge(proj_free[before % 2], freed(g, before))
                else:
                    before = y_use(parts - 1, t)
                    dve.wait_ge(proj_free[before % 2], g * (proj // 2))
                dve.tensor_tensor(y[:, t, :], y[:, t, :], full, ALU.add).then_inc(proj_free[u % 2], 1)

            dve.wait_ge(start_loaded, 16 * (NT + 1))
            dve.wait_ge(zero_ready, 1)
            with dve.Fori(0, NG) as g:
                query_key(g, 0)
                query_key(g, 1)
                dve.wait_ge(bv_loaded, 16 * (g + 1))
                dve.wait_ge(scores_done, g + 1)
                for_scores = ps_s[:, :, 0:NT * S].rearrange("p h (t k) -> p h t k", k=S)
                dve.tensor_reduce(smax[:, :, :], for_scores, AX_X, ALU.max).then_inc(smax_ready, 1)
                dve.wait_ge(smax_ready, g + 1)
                for h in range(HG):
                    dve.tensor_tensor(sc[:, h, :, :], for_scores[:, h, :, :],
                                      smax[:, h, :].unsqueeze(2).to_broadcast([P, NT, S]), ALU.subtract).then_inc(sub_ready, 1)
                for t in range(2):
                    values(g, 0, t)
                dve.wait_ge(exp_ready, g + 1)
                dve.tensor_reduce(rsum[:, :, :], sc[:, :, :, :], AX_X, ALU.add).then_inc(rsum_ready, 1)
                dve.wait_ge(rsum_ready, g + 1)
                dve.reciprocal(rinv[:, :, :], rsum[:, :, :]).then_inc(rinv_ready, 1)
                dve.wait_ge(rinv_ready, g + 1)
                dve.wait_ge(turned, g * HG)
                for half in range(2):
                    q = slice(S * half, S * half + S)
                    for h in range(HG):
                        dve.tensor_tensor(probs[q, h, :, S * half:S * half + S], sc[q, h, :, :],
                                          rinv[q, h, :].unsqueeze(2).to_broadcast([S, NT, S]), ALU.mult).then_inc(probs_ready, 1)
                for t in range(2, NT):
                    values(g, 0, t)
                for part in range(parts):
                    for h in range(part * hp, (part + 1) * hp):
                        turned_low(g, h)
                    outputs_low(g, part)
                    if part < parts - 1:
                        for t in range(NT):
                            values(g, part + 1, t)
                    for t in range(NT):
                        add_y(g, part, t)
            for bank in range(2):
                dve.wait_ge(proj_free[bank], NG * (proj // 2))
            for t in range(NT):
                if rectified:
                    dve.scalar_tensor_tensor(out=y[:, t, :], in0=y[:, t, :], scalar=0.01, in1=y[:, t, :],
                                             op0=ALU.mult, op1=ALU.max).then_inc(x_ready, 1)
                    dve.tensor_tensor(x[:, t, :], x[:, t, :], xn[:, t, :], ALU.add).then_inc(x_ready, 1)
                    dve.wait_ge(x_ready, 3 * t + 2)
                    dve.tensor_tensor(x[:, t, :], x[:, t, :], y[:, t, :], ALU.add).then_inc(x_ready, 1)
                else:
                    dve.tensor_tensor(x[:, t, :], x[:, t, :], y[:, t, :], ALU.add).then_inc(x_ready, 1)

        @block.tensor
        def _(pe):
            def bank(g, n):
                pe.wait_ge(proj_free[n % 2], g * (proj // 2) + n // 2)
                return ps_p[:, n % 2, :]

            def query_key(g, i):
                full = bank(g, i)
                for k in range(KT):
                    cols = slice(P * i, P * i + P)
                    for n, (w, a) in enumerate(three(qk_hi[:, k, cols], qk_lo[:, k, cols], xT_hi[:, k, :], xT_lo[:, k, :])):
                        mm = pe.matmul(full, w, a, start=(k == 0 and n == 0), stop=(k == KT - 1 and n == 2))
                mm.then_inc(proj_done, 1)

            def scores(g):
                if rectified:
                    pe.wait_ge(qk_ready, 2 * g + 2)
                else:
                    for i in range(2):
                        pe.wait_ge(proj_free[i], g * (proj // 2) + 1)
                pe.wait_ge(pT_ready, g * HG)
                for t in range(NT):
                    for half in range(2):
                        for h in range(HG):
                            r = slice(DH * h, DH * h + DH)
                            tok = slice(t * P + half * S, t * P + half * S + S)
                            mm = pe.matmul(ps_s[half * S:half * S + S, h, t * S:t * S + S], qk[r, 0, tok], qk[r, 1, tok],
                                           start=True, stop=True)
                mm.then_inc(scores_done, 1)

            def values(g, part, t):
                full = bank(g, v_use(part, t))
                for k in range(KT):
                    tok = slice(t * P, t * P + P)
                    for n, (a, w) in enumerate(three(xT_hi[:, k, tok], xT_lo[:, k, tok], wv_hi[:, k, :], wv_lo[:, k, :])):
                        mm = pe.matmul(full[:, 0:vc], a, w, start=(k == 0 and n == 0), stop=(k == KT - 1 and n == 2))
                mm.then_inc(proj_done, 1)

            def turn(g, h):
                for t in range(NT):
                    mm = pe.transpose(ps_s[:, h, t * P:(t + 1) * P], probs[:, h, t, :], ident[:, :])
                mm.then_inc(turned, 1)

            def outputs(g, part, h):
                pe.wait_ge(pT_ready, g * HG + h + 1)
                for c in range(kc):
                    n = part * n_o + (h - part * hp) * kc + c
                    if n >= 2:
                        pe.wait_ge(o_ready, g * parts * n_o + n - 1)
                    else:
                        pe.wait_ge(o_ready, g * parts * n_o)
                    v0 = (h - part * hp) * dv + c * P if dv >= P else 0
                    for t in range(NT):
                        tok = slice(t * P, t * P + P)
                        for i, (v, p) in enumerate(three(v_hi[:, t, v0:v0 + P], v_lo[:, t, v0:v0 + P],
                                                         pT_hi[:, h % 2, tok], pT_lo[:, h % 2, tok])):
                            mm = pe.matmul(ps_o[:, n % 2, tok], v, p, start=(i == 0), stop=(i == 2))
                    mm.then_inc(o_done, 1)

            def project(g, part, t):
                full = bank(g, y_use(part, t))
                for k in range(ko):
                    tok = slice(t * P, t * P + P)
                    for n, (o, w) in enumerate(three(o_hi[:, k, tok], o_lo[:, k, tok], wo_hi[:, k, :], wo_lo[:, k, :])):
                        mm = pe.matmul(full, o, w, start=(k == 0 and n == 0), stop=(k == ko - 1 and n == 2))
                mm.then_inc(proj_done, 1)

            with pe.Fori(0, NG) as g:
                pe.wait_ge(wqk_ready, g + 1)
                query_key(g, 0)
                query_key(g, 1)
                scores(g)
                pe.wait_ge(wv_ready, g * parts + 1)
                for t in range(NT):
                    values(g, 0, t)
                pe.wait_ge(probs_ready, 2 * HG * (g + 1))
                for part in range(parts):
                    pe.wait_ge(v_ready, (g * parts + part + 1) * NT)
                    heads = range(part * hp, (part + 1) * hp)
                    for h in heads[:2]:
                        turn(g, h)
                    for h in heads:
                        outputs(g, part, h)
                        if h + 2 in heads:
                            turn(g, h + 2)
                    if part < parts - 1:
                        pe.wait_ge(wv_ready, g * parts + part + 2)
                        for t in range(NT):
                            values(g, part + 1, t)
                    pe.wait_ge(wo_ready, g * parts + part + 1)
                    pe.wait_ge(o_ready, (g * parts + part + 1) * n_o)
                    for t in range(NT):
                        project(g, part, t)


def experts(nc, stage, x, xT_hi, xT_lo, ident, before, gate, w1, w3, w2, b1, b3, b2):
    NR = NE - 1
    with ExitStack() as ctx:
        m = Memory(nc, ctx, stage)
        raw = [m.sb(f"raw{i}", [P, KT, D]) for i in range(3)]
        w_hi = [m.sb(f"w_hi{i}", [P, KT, D], F32R) for i in range(3)]
        w_lo = [m.sb(f"w_lo{i}", [P, KT, D], F32R) for i in range(3)]
        b1_sb, b3_sb, b2_sb = m.sb("b1", [P, NE, KT]), m.sb("b3", [P, NE, KT]), m.sb("b2", [NE, D])
        gate_sb = m.sb("gate", [P, KT, NR])
        gate_hi, gate_lo = m.sb("gate_hi", [P, KT, NR], F32R), m.sb("gate_lo", [P, KT, NR], F32R)
        before_sb = m.sb("before", [P, NR, NR])
        lg, pr = m.sb("lg", [P, NT, NR]), m.sb("pr", [P, NT, NR])
        rmax, rsum, rinv = m.sb("rmax", [P, NT]), m.sb("rsum", [P, NT]), m.sb("rinv", [P, NT])
        beats, ties = m.sb("beats", [P, NT, NR, NR]), m.sb("ties", [P, NT, NR, NR])
        rank, chosen = m.sb("rank", [P, NT, NR]), m.sb("chosen", [P, NT, NR])
        weight = m.sb("weight", [P, NE, NT])
        weightT = m.sb("weightT", [NE, TOK])
        gated = m.sb("gated", [P, 2, TOK])
        h32 = m.sb("h32", [P, KT, TOK])
        h_hi, h_lo = m.sb("h_hi", [P, KT, TOK], F32R), m.sb("h_lo", [P, KT, TOK], F32R)
        ps_1, ps_3, ps_y = m.pb("ps_1", [P, 2, TOK]), m.pb("ps_3", [P, 2, TOK]), m.pb("ps_y", [P, 2, D])
        ps_g = m.pb("ps_g", [P, NT, NR])
        ps_w = m.pb("ps_w", [NE, TOK])

        small_loaded, gate_hi_ready, gate_ready, logits_done, router, weight_ready = (m.sem(n) for n in (
            "small_loaded", "gate_hi_ready", "gate_ready", "logits_done", "router", "weight_ready"))
        router_exp, weight_turned, weightT_ready, bias_done = (m.sem(n) for n in ("router_exp", "weight_turned", "weightT_ready", "bias_done"))
        loaded, hi_ready, lo_ready = m.sems("loaded", 3), m.sems("hi_ready", 3), m.sems("lo_ready", 3)
        up_done, down_done = m.sem("up_done"), m.sem("down_done")
        gated_ready, h_ready, h_hi_ready, h_lo_ready = (m.sem(n) for n in ("gated_ready", "h_ready", "h_hi_ready", "h_lo_ready"))
        bias_added, x_ready = m.sem("bias_added"), m.sem("x_ready")
        block = ctx.enter_context(nc.Block())
        weights = (w1, w3, w2)

        @block.sync
        def _(sp):
            for to, of in ((gate_sb[:, :, :], gate), (before_sb[:, :, :], before.to_broadcast([P, NR * NR]).rearrange("p (a b) -> p a b", b=NR)),
                           (b1_sb[:, :, :], b1), (b3_sb[:, :, :], b3), (b2_sb[:, :], b2)):
                sp.dma_start(to, of).then_inc(small_loaded, 16)
            with sp.Fori(0, NE) as e:
                for i in range(3):
                    sp.wait_ge(lo_ready[i], e)
                    sp.dma_start(raw[i][:, :, :], weights[i][e]).then_inc(loaded[i], 16)

        @block.scalar
        def _(act):
            act.wait_ge(small_loaded, 16 * 5)
            act.activation(gate_hi[:, :, :], gate_sb[:, :, :], ACT.Copy).then_inc(gate_hi_ready, 1)
            act.wait_ge(router, 2)
            act.activation(pr[:, :, :], lg[:, :, :], ACT.Exp).then_inc(router_exp, 1)

            def split(e, i):
                act.wait_ge(loaded[i], 16 * (e + 1))
                if i < 2:
                    act.wait_ge(up_done, KT * e)
                else:
                    act.wait_ge(down_done, NT * e)
                act.activation(w_hi[i][:, :, :], raw[i][:, :, :], ACT.Copy).then_inc(hi_ready[i], 1)

            def gate_slice(e, k):
                act.wait_ge(up_done, KT * e + k + 1)
                act.wait_ge(h_ready, KT * e + max(0, k - 1))
                act.activation(gated[:, k % 2, :], ps_1[:, k % 2, :], ACT.Silu,
                               bias=b1_sb[:, e, k:k + 1]).then_inc(gated_ready, 1)

            def high_slice(e, k):
                act.wait_ge(h_ready, KT * e + k + 1)
                act.wait_ge(down_done, NT * e)
                act.activation(h_hi[:, k, :], h32[:, k, :], ACT.Copy).then_inc(h_hi_ready, 1)

            with act.Fori(0, NE) as e:
                split(e, 0)
                split(e, 1)
                gate_slice(e, 0)
                split(e, 2)
                for k in range(1, KT):
                    gate_slice(e, k)
                    high_slice(e, k - 1)
                high_slice(e, KT - 1)

        @block.gpsimd
        def _(pool):
            with pool.Fori(0, NE) as e:
                for i in range(3):
                    pool.wait_ge(hi_ready[i], e + 1)
                    pool.tensor_tensor(w_lo[i][:, :, :], raw[i][:, :, :], as_f32(w_hi[i][:, :, :]),
                                       ALU.subtract).then_inc(lo_ready[i], 1)
                for k in range(KT):
                    pool.wait_ge(h_hi_ready, KT * e + k + 1)
                    pool.tensor_tensor(h_lo[:, k, :], h32[:, k, :], as_f32(h_hi[:, k, :]), ALU.subtract).then_inc(h_lo_ready, 1)

        @block.vector
        def _(dve):
            steps = [0]

            def step(ins):
                ins.then_inc(router, 1)
                steps[0] += 1
                dve.wait_ge(router, steps[0])

            def each(ap):
                return ap.unsqueeze(2).to_broadcast([P, NT, NR])

            dve.wait_ge(gate_hi_ready, 1)
            dve.tensor_tensor(gate_lo[:, :, :], gate_sb[:, :, :], as_f32(gate_hi[:, :, :]), ALU.subtract).then_inc(gate_ready, 1)
            dve.wait_ge(small_loaded, 16 * 5)
            dve.wait_ge(logits_done, 1)
            step(dve.tensor_reduce(rmax[:, :], ps_g[:, :, :], AX_X, ALU.max))
            step(dve.tensor_tensor(lg[:, :, :], ps_g[:, :, :], each(rmax[:, :]), ALU.subtract))
            dve.wait_ge(router_exp, 1)
            step(dve.tensor_reduce(rsum[:, :], pr[:, :, :], AX_X, ALU.add))
            step(dve.reciprocal(rinv[:, :], rsum[:, :]))
            step(dve.tensor_tensor(pr[:, :, :], pr[:, :, :], each(rinv[:, :]), ALU.mult))
            for t in range(NT):
                other = pr[:, t, :].unsqueeze(1).to_broadcast([P, NR, NR])
                own = pr[:, t, :].unsqueeze(2).to_broadcast([P, NR, NR])
                step(dve.tensor_tensor(beats[:, t, :, :], other, own, ALU.is_gt))
                step(dve.tensor_tensor(ties[:, t, :, :], other, own, ALU.is_equal))
                step(dve.tensor_tensor(ties[:, t, :, :], ties[:, t, :, :], before_sb[:, :, :], ALU.mult))
            step(dve.tensor_tensor(beats[:, :, :, :], beats[:, :, :, :], ties[:, :, :, :], ALU.add))
            step(dve.tensor_reduce(rank[:, :, :], beats[:, :, :, :], AX_X, ALU.add))
            step(dve.tensor_scalar(chosen[:, :, :], rank[:, :, :], 2.0, None, ALU.is_lt))
            step(dve.memset(weight[:, NR, :], 1.0))
            dve.tensor_tensor(weight[:, 0:NR, :].rearrange("p e t -> p t e"), pr[:, :, :], chosen[:, :, :],
                              ALU.mult).then_inc(weight_ready, 1)
            dve.wait_ge(weight_turned, 1)
            dve.tensor_copy(weightT[:, :], ps_w[:, :]).then_inc(weightT_ready, 1)

            for t in range(NT):
                dve.wait_ge(bias_done, t + 1)
                dve.tensor_tensor(x[:, t, :], x[:, t, :], ps_y[:, t % 2, :], ALU.add).then_inc(bias_added, 1)
            dve.wait_ge(bias_added, NT)
            with dve.Fori(0, NE) as e:
                for k in range(KT):
                    dve.wait_ge(gated_ready, KT * e + k + 1)
                    dve.wait_ge(h_lo_ready, KT * e)
                    dve.scalar_tensor_tensor(out=h32[:, k, :], in0=ps_3[:, k % 2, :], scalar=b3_sb[:, e, k:k + 1],
                                             in1=gated[:, k % 2, :], op0=ALU.add, op1=ALU.mult).then_inc(h_ready, 1)
                for t in range(NT):
                    dve.wait_ge(down_done, NT * e + t + 1)
                    dve.wait_ge(x_ready, NT * e)
                    dve.scalar_tensor_tensor(out=x[:, t, :], in0=ps_y[:, t % 2, :], scalar=weight[:, e, t:t + 1],
                                             in1=x[:, t, :], op0=ALU.mult, op1=ALU.add).then_inc(x_ready, 1)

        @block.tensor
        def _(pe):
            pe.wait_ge(gate_ready, 1)
            for t in range(NT):
                for k in range(KT):
                    tok = slice(t * P, t * P + P)
                    for n, (a, w) in enumerate(three(xT_hi[:, k, tok], xT_lo[:, k, tok], gate_hi[:, k, :], gate_lo[:, k, :])):
                        mm = pe.matmul(ps_g[:, t, :], a, w, start=(k == 0 and n == 0), stop=(k == KT - 1 and n == 2))
            mm.then_inc(logits_done, 1)
            pe.wait_ge(weight_ready, 1)
            for t in range(NT):
                mm = pe.transpose(ps_w[:, t * P:(t + 1) * P], weight[:, :, t], ident[:, :])
            mm.then_inc(weight_turned, 1)
            pe.wait_ge(weightT_ready, 1)
            for t in range(NT):
                if t >= 2:
                    pe.wait_ge(bias_added, t - 1)
                pe.matmul(ps_y[:, t % 2, :], weightT[:, t * P:(t + 1) * P], b2_sb[:, :], start=True, stop=True).then_inc(bias_done, 1)
            pe.wait_ge(bias_added, NT)
            with pe.Fori(0, NE) as e:
                for i in range(2):
                    pe.wait_ge(lo_ready[i], e + 1)
                for k in range(KT):
                    pe.wait_ge(h_ready, KT * e + max(0, k - 1))
                    cols = slice(P * k, P * k + P)
                    for i, ps in ((0, ps_1), (1, ps_3)):
                        for j in range(KT):
                            for n, (w, a) in enumerate(three(w_hi[i][:, j, cols], w_lo[i][:, j, cols], xT_hi[:, j, :], xT_lo[:, j, :])):
                                mm = pe.matmul(ps[:, k % 2, :], w, a, start=(j == 0 and n == 0), stop=(j == KT - 1 and n == 2))
                    mm.then_inc(up_done, 1)
                pe.wait_ge(lo_ready[2], e + 1)
                for t in range(NT):
                    pe.wait_ge(x_ready, NT * e + max(0, t - 1))
                    tok = slice(t * P, t * P + P)
                    for j in range(KT):
                        if t == 0:
                            pe.wait_ge(h_lo_ready, KT * e + j + 1)
                        for n, (a, w) in enumerate(three(h_hi[:, j, tok], h_lo[:, j, tok], w_hi[2][:, j, :], w_lo[2][:, j, :])):
                            mm = pe.matmul(ps_y[:, t % 2, :], a, w, start=(j == 0 and n == 0), stop=(j == KT - 1 and n == 2))
                    mm.then_inc(down_done, 1)


def split_weight(nc, stage, chunks, raw_slots):
    with ExitStack() as ctx:
        m = Memory(nc, ctx, stage)
        n_slots = len(raw_slots)
        loaded, hi_ready, lo_ready = m.sems("loaded", n_slots), m.sem("hi_ready"), m.sem("lo_ready")
        block = ctx.enter_context(nc.Block())

        @block.sync
        def _(sp):
            for i, (of, _, _) in enumerate(chunks):
                if i >= n_slots:
                    sp.wait_ge(lo_ready, i - n_slots + 1)
                sp.dma_start(raw_slots[i % n_slots], of).then_inc(loaded[i % n_slots], 16)

        @block.scalar
        def _(act):
            for i, (_, hi, _) in enumerate(chunks):
                act.wait_ge(loaded[i % n_slots], 16 * (i // n_slots + 1))
                act.activation(hi, raw_slots[i % n_slots], ACT.Copy).then_inc(hi_ready, 1)

        @block.vector
        def _(dve):
            for i, (_, hi, lo) in enumerate(chunks):
                dve.wait_ge(hi_ready, i + 1)
                dve.tensor_tensor(lo, raw_slots[i % n_slots], as_f32(hi), ALU.subtract).then_inc(lo_ready, 1)


def project_queries(nc, stage, q, xT_hi, xT_lo, w_hi, w_lo, bias):
    with ExitStack() as ctx:
        m = Memory(nc, ctx, stage)
        ps = m.pb("ps", [P, NG, TOK])
        done, q_ready = m.sem("done"), m.sem("q_ready")
        block = ctx.enter_context(nc.Block())

        @block.tensor
        def _(pe):
            for g in range(NG):
                for k in range(KT):
                    cols = slice(P * g, P * g + P)
                    for n, (w, a) in enumerate(three(w_hi[:, k, cols], w_lo[:, k, cols], xT_hi[:, k, :], xT_lo[:, k, :])):
                        mm = pe.matmul(ps[:, g, :], w, a, start=(k == 0 and n == 0), stop=(k == KT - 1 and n == 2))
                mm.then_inc(done, 1)

        @block.vector
        def _(dve):
            for g in range(NG):
                dve.wait_ge(done, g + 1)
                dve.tensor_scalar(q[:, g, :], ps[:, g, :], bias[:, g:g + 1], 1.0 / sqrt(DH), ALU.add, ALU.mult).then_inc(q_ready, 1)


def masked_context_attention(nc, stage, q, att, ident, wk, wv, bk, bv, ctxT, mask, gain):
    with ExitStack() as ctx:
        m = Memory(nc, ctx, stage)
        (wk_hi, wk_lo), (wv_hi, wv_lo) = wk, wv
        HV = 2
        VC = D // HV
        raw_T = m.sb("raw_T", [P, 2, S2P])
        T_hi, T_lo = m.sb("T_hi", [P, KT, S2P], F32R), m.sb("T_lo", [P, KT, S2P], F32R)
        k_hi, k_lo = m.sb("k_hi", [P, S2P], F32R), m.sb("k_lo", [P, S2P], F32R)
        v_sum = m.sb("v_sum", [P, 2, VC])
        v_pair = m.sb("v_pair", [P, NJ, 4, P], F32R)
        qb_hi, qb_lo = m.sb("qb_hi", [P, NG, P], F32R), m.sb("qb_lo", [P, NG, P], F32R)
        pr = m.sb("pr", [P, 2, S2P])
        neg = m.sb("neg", [P, S2P], I32)
        gn = m.sb("gn", [P, S2P])
        cmax = m.sb("cmax", [P, 2, 4])
        rmax, nmax, rsum, rinv = m.sb("rmax", [P, 2]), m.sb("nmax", [P, 2]), m.sb("rsum", [P, 2]), m.sb("rinv", [P, 2])
        pT = m.sb("pT", [P, 2, 4, 2 * P], F32R)
        o_low = m.sb("o_low", [S, 2, S])
        o_part = m.sb("o_part", [S, 2, S])
        ps_p = m.pb("ps_p", [P, 3, 512])
        ps_s = m.pb("ps_s", [P, 2, 512])
        ps_t = m.pb("ps_t", [P, 2, 512])
        ps_o = m.pb("ps_o", [P, 2, 2 * P])
        negf = neg[:, :].bitcast(F32)

        n_p = NG * 4 + HV * NJ
        assert n_p % 3 == 0
        T_loaded, T_split, mask_loaded, gain_loaded = m.sems("T_loaded", 2), m.sem("T_split"), m.sem("mask_loaded"), m.sem("gain_loaded")
        T_hi_ready = m.sem("T_hi_ready")
        zero_ready, neg_shifted, neg_ready, qb_hi_ready, qb_ready = (m.sem(n) for n in ("zero_ready", "neg_shifted", "neg_ready", "qb_hi_ready", "qb_ready"))
        proj_done, proj_free, k_hi_ready, k_ready = m.sem("proj_done"), m.sems("proj_free", 3), m.sem("k_hi_ready"), m.sem("k_ready")
        v_hi_ready, v_ready = m.sem("v_hi_ready"), m.sem("v_ready")
        scores_done, masked, rmax_ready, nmax_ready, exp_ready, rinv_ready, share_ready = (
            m.sems(n, 2) for n in ("scores_done", "masked", "rmax_ready", "nmax_ready", "exp_ready", "rinv_ready", "share_ready"))
        turned, pT_hi_ready, pT_ready, pT_used = m.sem("turned"), m.sem("pT_hi_ready"), m.sem("pT_ready"), m.sem("pT_used")
        waited = m.sems("waited", 2)
        o_low_ready, o_part_ready, att_ready = (m.sem(n) for n in ("o_low_ready", "o_part_ready", "att_ready"))
        block = ctx.enter_context(nc.Block())

        order = [("k", 0, c) for c in range(4)] + [("v", 0, j) for j in range(NJ)]
        order += [("k", 1, c) for c in range(4)] + [("k", 2, c) for c in range(4)]
        order += [("v", 1, j) for j in range(NJ)] + [("k", 3, c) for c in range(4)]
        use_of = {what: n for n, what in enumerate(order)}

        def freed(b, u):
            return b * (n_p // 3) + u // 3 + 1

        def tiles(n):
            j0, j1 = JG[n]
            return j0, j1, JR[j0]

        @block.sync
        def _(sp):
            def load_T(b):
                for k in range(KT):
                    sp.wait_ge(T_split, 4 * b + max(0, k - 1))
                    sp.dma_start(raw_T[:, k % 2, :], ctxT[b, :, k, :]).then_inc(T_loaded[k % 2], 16)

            def load_mask(b):
                for i in range(2):
                    sp.wait_ge(masked[i], 4 * NG * b)
                sp.dma_start(neg[0:S, 0:S2], mask[b]).then_inc(mask_loaded, 16)
                sp.dma_start(neg[S:P, 0:S2], mask[b]).then_inc(mask_loaded, 16)
                for i in range(2):
                    sp.wait_ge(share_ready[i], NG * b)
                sp.dma_start(gn[0:S, 0:S2], gain[b]).then_inc(gain_loaded, 16)
                sp.dma_start(gn[S:P, 0:S2], gain[b]).then_inc(gain_loaded, 16)

            load_T(0)
            load_mask(0)
            with sp.Fori(0, B - 1) as b:
                load_T(b + 1)
                load_mask(b + 1)

        @block.scalar
        def _(act):
            def split_T(b, k):
                act.wait_ge(T_loaded[k % 2], 16 * (2 * b + k // 2 + 1))
                act.wait_ge(proj_done, n_p * b)
                act.activation(T_hi[:, k, :], raw_T[:, k % 2, :], ACT.Copy).then_inc(T_hi_ready, 1)

            def keys_high(b, g):
                for i in range(2):
                    act.wait_ge(scores_done[i], 4 * (NG * b + g))
                for c in range(4):
                    u = use_of["k", g, c]
                    act.wait_ge(proj_done, n_p * b + u + 1)
                    act.activation(k_hi[:, CH0[c]:CH0[c] + CHW[c]], ps_p[:, u % 3, 0:CHW[c]], ACT.Identity,
                                   bias=bk[:, g:g + 1]).then_inc(k_hi_ready, 1)

            def values_high(b, half):
                act.wait_ge(pT_used, 32 * b + 16 * half)
                for j in range(NJ):
                    u, r = use_of["v", half, j], JR[j]
                    act.wait_ge(proj_free[u % 3], freed(b, u))
                    act.activation(v_pair[0:r, j, :, 0:S], v_sum[0:r, j % 2, :].rearrange("p (a c) -> p a c", c=S),
                                   ACT.Copy).then_inc(v_hi_ready, 1)

            def exps(b, g):
                for i in range(2):
                    act.wait_ge(nmax_ready[i], NG * b + g + 1)
                    act.activation(pr[:, i, 0:S2], pr[:, i, 0:S2], ACT.Exp, bias=nmax[:, i:i + 1],
                                   accum_out=rsum[:, i:i + 1]).then_inc(exp_ready[i], 1)

            def turned_high(b, g, i):
                for n in range(4):
                    j0, j1, r = tiles(n)
                    u = 8 * g + 4 * i + n
                    act.wait_ge(turned, 32 * b + u + 1)
                    act.wait_ge(pT_used, 32 * b + max(0, u - 1))
                    act.activation(pT[0:r, u % 2, 0:j1 - j0, 0:P],
                                   ps_t[0:r, u % 2, 0:(j1 - j0) * P].rearrange("p (j c) -> p j c", c=P),
                                   ACT.Copy).then_inc(pT_hi_ready, 1)

            def out_low(b, g):
                act.wait_ge(pT_used, 32 * b + 8 * (g + 1))
                for h in range(2):
                    rows = slice(DH * h, DH * h + DH)
                    act.activation(o_low[rows, :, :], ps_o[S + DH * h:S + DH * h + DH, :, S * h:S * h + S],
                                   ACT.Copy).then_inc(o_low_ready, 1)

            def batch(b, last):
                keys_high(b, 0)
                exps(b, 0)
                values_high(b, 0)
                for g in range(NG):
                    if g == 2:
                        values_high(b, 1)
                    if g < NG - 1:
                        keys_high(b, g + 1)
                    for i in range(2):
                        turned_high(b, g, i)
                        if g >= 2 and not last:
                            split_T(b + 1, 2 * (g - 2) + i)
                    out_low(b, g)
                    if g < NG - 1:
                        exps(b, g + 1)

            for k in range(KT):
                split_T(0, k)
            with act.Fori(0, B - 1) as b:
                batch(b, False)
            batch(B - 1, True)

        @block.gpsimd
        def _(pool):
            def values_low(b, half):
                for j in range(NJ):
                    r = JR[j]
                    pool.wait_ge(v_hi_ready, 2 * NJ * b + NJ * half + j + 1)
                    pool.tensor_tensor(v_pair[0:r, j, :, S:P], v_sum[0:r, j % 2, :].rearrange("p (a c) -> p a c", c=S),
                                       as_f32(v_pair[0:r, j, :, 0:S]), ALU.subtract).then_inc(v_ready, 1)

            with pool.Fori(0, B) as b:
                pool.wait_ge(mask_loaded, 32 * (b + 1))
                pool.sem_inc(waited[0], 1)
                pool.tensor_scalar(negf[:, 0:S2], neg[:, 0:S2], -1.0, 1.0e9, ALU.add, ALU.mult).then_inc(neg_ready, 1)
                values_low(b, 0)
                values_low(b, 1)

        @block.vector
        def _(dve):
            dve.memset(as_f32(qb_hi[:, :, :]), 0.0).then_inc(zero_ready, 1)
            dve.memset(as_f32(qb_lo[:, :, :]), 0.0).then_inc(zero_ready, 1)
            dve.wait_ge(zero_ready, 2)

            def stage_queries(b):
                for i in range(2):
                    dve.wait_ge(scores_done[i], 4 * NG * b)
                for h in range(HG):
                    rows, cols = slice(DH * h, DH * h + DH), slice(S * (h % 2), S * (h % 2) + S)
                    dve.tensor_copy(qb_hi[rows, :, cols], q[rows, :, bass.ts(b, S)]).then_inc(qb_hi_ready, 1)
                dve.wait_ge(qb_hi_ready, HG * (b + 1))
                for h in range(HG):
                    rows, cols = slice(DH * h, DH * h + DH), slice(S * (h % 2), S * (h % 2) + S)
                    dve.tensor_tensor(qb_lo[rows, :, cols], q[rows, :, bass.ts(b, S)], as_f32(qb_hi[rows, :, cols]),
                                      ALU.subtract).then_inc(qb_ready, 1)

            def split_T(b, k):
                dve.wait_ge(T_hi_ready, 4 * b + k + 1)
                dve.tensor_tensor(T_lo[:, k, :], raw_T[:, k % 2, :], as_f32(T_hi[:, k, :]), ALU.subtract).then_inc(T_split, 1)

            def keys_low(b, g):
                for c in range(4):
                    u = use_of["k", g, c]
                    cols = slice(CH0[c], CH0[c] + CHW[c])
                    dve.wait_ge(k_hi_ready, 4 * (NG * b + g) + c + 1)
                    dve.scalar_tensor_tensor(out=k_lo[:, cols], in0=ps_p[:, u % 3, 0:CHW[c]], scalar=bk[:, g:g + 1],
                                             in1=as_f32(k_hi[:, cols]), op0=ALU.add, op1=ALU.subtract).then_inc(proj_free[u % 3], 1)

            def values(b, half):
                for j in range(NJ):
                    u, r = use_of["v", half, j], JR[j]
                    dve.wait_ge(proj_done, n_p * b + u + 1)
                    dve.wait_ge(v_ready, 2 * NJ * b + NJ * half + max(0, j - 1))
                    dve.tensor_tensor(v_sum[0:r, j % 2, :], ps_p[0:r, u % 3, 0:VC], bv[0:r, VC * half:VC * half + VC],
                                      ALU.add).then_inc(proj_free[u % 3], 1)

            def mask_scores(b, g):
                dve.wait_ge(neg_ready, b + 1)
                dve.wait_ge(turned, 32 * b + 8 * g)
                for c in range(4):
                    for i in range(2):
                        w = CHV[c]
                        dve.wait_ge(scores_done[i], 4 * (NG * b + g) + c + 1)
                        dve.sem_inc(waited[1], 1)
                        dve.tensor_tensor_reduce(pr[:, i, CH0[c]:CH0[c] + w], ps_s[:, i, 0:w], negf[:, CH0[c]:CH0[c] + w],
                                                 1.0, LOW, ALU.add, ALU.max, cmax[:, i, c:c + 1]).then_inc(masked[i], 1)
                for i in range(2):
                    dve.wait_ge(masked[i], 4 * (NG * b + g + 1))
                    dve.tensor_reduce(rmax[:, i:i + 1], cmax[:, i, :], AX_X, ALU.max).then_inc(rmax_ready[i], 1)
                for i in range(2):
                    dve.wait_ge(rmax_ready[i], NG * b + g + 1)
                    dve.tensor_scalar(nmax[:, i:i + 1], rmax[:, i:i + 1], -1.0, None, ALU.mult).then_inc(nmax_ready[i], 1)

            def shares(b, g):
                dve.wait_ge(gain_loaded, 32 * (b + 1))
                for i in range(2):
                    dve.wait_ge(exp_ready[i], NG * b + g + 1)
                    dve.reciprocal(rinv[:, i:i + 1], rsum[:, i:i + 1]).then_inc(rinv_ready[i], 1)
                    dve.wait_ge(rinv_ready[i], NG * b + g + 1)
                    dve.scalar_tensor_tensor(out=pr[:, i, 0:S2], in0=pr[:, i, 0:S2], scalar=rinv[:, i:i + 1],
                                             in1=gn[:, 0:S2], op0=ALU.mult, op1=ALU.mult).then_inc(share_ready[i], 1)

            def turned_low(b, g, i):
                for n in range(4):
                    j0, j1, r = tiles(n)
                    u = 8 * g + 4 * i + n
                    dve.wait_ge(pT_hi_ready, 32 * b + u + 1)
                    dve.tensor_tensor(pT[0:r, u % 2, 0:j1 - j0, P:2 * P],
                                      ps_t[0:r, u % 2, 0:(j1 - j0) * P].rearrange("p (j c) -> p j c", c=P),
                                      as_f32(pT[0:r, u % 2, 0:j1 - j0, 0:P]), ALU.subtract).then_inc(pT_ready, 1)

            def outputs(b, g):
                n = NG * b + g
                dve.wait_ge(o_low_ready, 2 * n + 2)
                for h in range(2):
                    rows, own = slice(DH * h, DH * h + DH), slice(S * h, S * h + S)
                    dve.tensor_tensor(o_part[rows, :, :], ps_o[rows, :, own], o_low[rows, :, :], ALU.add).then_inc(o_part_ready, 1)
                dve.wait_ge(o_part_ready, 2 * n + 2)
                for i in range(2):
                    for h in range(2):
                        rows = slice(DH * h, DH * h + DH)
                        to = slice(S * i + DH * h, S * i + DH * h + DH)
                        dve.tensor_tensor(att[to, g, bass.ts(b, S)], ps_o[rows, i, P + S * h:P + S * h + S],
                                          o_part[rows, i, :], ALU.add).then_inc(att_ready, 1)

            def batch(b, last):
                stage_queries(b)
                keys_low(b, 0)
                mask_scores(b, 0)
                values(b, 0)
                shares(b, 0)
                for g in range(NG):
                    if g == 2:
                        values(b, 1)
                    if g < NG - 1:
                        keys_low(b, g + 1)
                    for i in range(2):
                        turned_low(b, g, i)
                        if g >= 2 and not last:
                            split_T(b + 1, 2 * (g - 2) + i)
                    if g < NG - 1:
                        mask_scores(b, g + 1)
                    outputs(b, g)
                    if g < NG - 1:
                        shares(b, g + 1)

            for k in range(KT):
                split_T(0, k)
            with dve.Fori(0, B - 1) as b:
                batch(b, False)
            batch(B - 1, True)

        @block.tensor
        def _(pe):
            def bank(b, u):
                pe.wait_ge(proj_free[u % 3], b * (n_p // 3) + u // 3)
                return ps_p[:, u % 3, :]

            def keys(b, g):
                for c in range(4):
                    full = bank(b, use_of["k", g, c])
                    for k in range(KT):
                        if g == 0 and c == 0:
                            pe.wait_ge(T_split, 4 * b + k + 1)
                        cols, w = slice(P * g, P * g + P), slice(CH0[c], CH0[c] + CHW[c])
                        for n, (a, t) in enumerate(three(wk_hi[:, k, cols], wk_lo[:, k, cols], T_hi[:, k, w], T_lo[:, k, w])):
                            mm = pe.matmul(full[:, 0:CHW[c]], a, t, start=(k == 0 and n == 0), stop=(k == KT - 1 and n == 2))
                    mm.then_inc(proj_done, 1)

            def values(b, half):
                for j in range(NJ):
                    full = bank(b, use_of["v", half, j])
                    r = JR[j]
                    for k in range(KT):
                        rows, cols = slice(P * j, P * j + r), slice(VC * half, VC * half + VC)
                        for n, (t, w) in enumerate(three(T_hi[:, k, rows], T_lo[:, k, rows], wv_hi[:, k, cols], wv_lo[:, k, cols])):
                            mm = pe.matmul(full[0:r, 0:VC], t, w, start=(k == 0 and n == 0), stop=(k == KT - 1 and n == 2))
                    mm.then_inc(proj_done, 1)

            def scores(b, g):
                if g == 0:
                    pe.wait_ge(qb_ready, HG * (b + 1))
                for c in range(4):
                    cols = slice(CH0[c], CH0[c] + CHW[c])
                    u = use_of["k", g, c]
                    pe.wait_ge(proj_free[u % 3], freed(b, u))
                    for i in range(2):
                        pe.wait_ge(masked[i], 4 * (NG * b + g) + c)
                        r = slice(S * i, S * i + S)
                        for n, (a, t) in enumerate(three(qb_hi[r, g, :], qb_lo[r, g, :], k_hi[r, cols], k_lo[r, cols])):
                            mm = pe.matmul(ps_s[:, i, 0:CHW[c]], a, t, start=(n == 0), stop=(n == 2))
                        mm.then_inc(scores_done[i], 1)

            def outputs(b, g):
                pe.wait_ge(v_ready, 2 * NJ * b + NJ * (g // 2 + 1))
                pe.wait_ge(att_ready, HG * (NG * b + g))

                def turn(i, n):
                    j0, j1, r = tiles(n)
                    u = 8 * g + 4 * i + n
                    pe.wait_ge(pT_ready, 32 * b + max(0, u - 1))
                    for j in range(j0, j1):
                        mm = pe.transpose(ps_t[0:r, u % 2, (j - j0) * P:(j - j0 + 1) * P], pr[:, i, j * P:j * P + r], ident[:, :])
                    mm.then_inc(turned, 1)

                def multiply(i, n):
                    j0, j1, r = tiles(n)
                    u = 8 * g + 4 * i + n
                    pe.wait_ge(pT_ready, 32 * b + u + 1)
                    for j in range(j0, j1):
                        mm = pe.matmul(ps_o[:, i, :], v_pair[0:r, j, 2 * (g % 2) + i, :], pT[0:r, u % 2, j - j0, :],
                                       start=(j == 0), stop=(j == NJ - 1))
                    mm.then_inc(pT_used, 1)

                steps = [(i, n) for i in range(2) for n in range(4)]
                for s, (i, n) in enumerate(steps):
                    if n == 0:
                        pe.wait_ge(share_ready[i], NG * b + g + 1)
                    turn(i, n)
                    if s:
                        multiply(*steps[s - 1])
                multiply(*steps[-1])

            with pe.Fori(0, B) as b:
                keys(b, 0)
                scores(b, 0)
                values(b, 0)
                for g in range(NG):
                    if g == 2:
                        values(b, 1)
                    if g < NG - 1:
                        keys(b, g + 1)
                    outputs(b, g)
                    if g < NG - 1:
                        scores(b, g + 1)


def project_attended(nc, stage, x, att, w_hi, w_lo, bo):
    with ExitStack() as ctx:
        m = Memory(nc, ctx, stage)
        a_hi, a_lo = m.sb("a_hi", [P, KT, TOK], F32R), m.sb("a_lo", [P, KT, TOK], F32R)
        ps = m.pb("ps", [P, NT, D])
        hi_ready, lo_ready, done, bias_added, x_ready = (m.sem(n) for n in ("hi_ready", "lo_ready", "done", "bias_added", "x_ready"))
        block = ctx.enter_context(nc.Block())

        @block.scalar
        def _(act):
            for k in range(KT):
                act.activation(a_hi[:, k, :], att[:, k, :], ACT.Copy).then_inc(hi_ready, 1)

        @block.vector
        def _(dve):
            for k in range(KT):
                dve.wait_ge(hi_ready, k + 1)
                dve.tensor_tensor(a_lo[:, k, :], att[:, k, :], as_f32(a_hi[:, k, :]), ALU.subtract).then_inc(lo_ready, 1)
            for t in range(NT):
                dve.tensor_tensor(x[:, t, :], x[:, t, :], bo[:, :], ALU.add).then_inc(bias_added, 1)
            for t in range(NT):
                dve.wait_ge(done, t + 1)
                dve.wait_ge(bias_added, t + 1)
                dve.tensor_tensor(x[:, t, :], x[:, t, :], ps[:, t, :], ALU.add).then_inc(x_ready, 1)

        @block.tensor
        def _(pe):
            for t in range(NT):
                tok = slice(t * P, t * P + P)
                for k in range(KT):
                    pe.wait_ge(lo_ready, k + 1)
                    for n, (a, w) in enumerate(three(a_hi[:, k, tok], a_lo[:, k, tok], w_hi[:, k, :], w_lo[:, k, :])):
                        mm = pe.matmul(ps[:, t, :], a, w, start=(k == 0 and n == 0), stop=(k == KT - 1 and n == 2))
                mm.then_inc(done, 1)


def quantized_blocks(nc, stage, x, h, hT_hi, hT_lo, ident, codes, scales, la, lb, bias, gamma, beta):
    RANK = 32
    NBK = 3
    GROUP = 16
    GP = P // GROUP
    with ExitStack() as ctx:
        m = Memory(nc, ctx, stage)
        code = m.sb("code", [P, 2, KT, D], I32)
        scale = m.sb("scale", [P, 2, KT, D])
        la_sb, lb_sb = m.sb("la", [RANK, 2, D]), m.sb("lb", [RANK, 2, D])
        w = m.sb("w", [P, 2, KT, D])
        w_hi, w_lo = m.sb("w_hi", [P, 2, KT, D], F32R), m.sb("w_lo", [P, 2, KT, D], F32R)
        bias_sb = m.sb("bias", [P, 2, D])
        gamma_sb, beta_sb = m.sb("gamma", [P, D]), m.sb("beta", [P, D])
        z = m.sb("z", [P, NT, D])
        zT_hi, zT_lo = m.sb("zT_hi", [P, KT, TOK], F32R), m.sb("zT_lo", [P, KT, TOK], F32R)
        stats, mv = m.sb("stats", [P, NT, 6]), m.sb("mv", [P, NT, 2])
        var, std, rstd = m.sb("var", [P, NT]), m.sb("std", [P, NT]), m.sb("rstd", [P, NT])
        ps_l, ps_y, ps_t = m.pb("ps_l", [P, 2, D]), m.pb("ps_y", [P, 2, D]), m.pb("ps_t", [P, KT, TOK])

        loaded, rank_loaded, small_loaded = m.sems("loaded", 2), m.sems("rank_loaded", 2), m.sem("small_loaded")
        w_coded, w_scaled, rank_done, w_summed, w_hi_ready, w_ready = (m.sems(n, 2) for n in (
            "w_coded", "w_scaled", "rank_done", "w_summed", "w_hi_ready", "w_ready"))
        y_done, y_read = m.sems("y_done", 2), m.sems("y_read", 2)
        stats_ready, mv_ready, var_ready, std_ready, rstd_ready = (m.sem(n) for n in ("stats_ready", "mv_ready", "var_ready", "std_ready", "rstd_ready"))
        z_ready, z_scaled, z_shifted, gelu_ready = (m.sem(n) for n in ("z_ready", "z_scaled", "z_shifted", "gelu_ready"))
        turned, hi_ready, lo_ready = m.sems("turned", 2), m.sems("hi_ready", 2), m.sems("lo_ready", 2)
        waited = m.sem("waited")
        h_biased, x_ready = m.sem("h_biased"), m.sem("x_ready")
        block = ctx.enter_context(nc.Block())

        @block.sync
        def _(sp):
            def load(b):
                for s in range(2):
                    sp.wait_ge(w_ready[s], b)
                    sp.dma_start(code[:, s, :, :], codes[2 * b + s]).then_inc(loaded[s], 16)
                    for k in range(KT):
                        rows = scales[2 * b + s, GP * k:GP * k + GP, :].unsqueeze(1).to_broadcast([GP, GROUP, D])
                        sp.dma_start(scale[:, s, k, :], rows).then_inc(loaded[s], 16)
                    sp.dma_start(la_sb[:, s, :], la[2 * b + s]).then_inc(rank_loaded[s], 16)
                    sp.dma_start(lb_sb[:, s, :], lb[2 * b + s]).then_inc(rank_loaded[s], 16)
                    if s == 0:
                        sp.wait_ge(y_read[1], NT * b)
                        for to, of in ((bias_sb[:, 0, :], bias[2 * b]), (bias_sb[:, 1, :], bias[2 * b + 1]),
                                       (gamma_sb[:, :], gamma[b]), (beta_sb[:, :], beta[b])):
                            sp.dma_start(to, of.to_broadcast([P, D])).then_inc(small_loaded, 16)

            with sp.Fori(0, NBK) as b:
                load(b)

        @block.gpsimd
        def _(pool):
            def from_codes(b, s):
                pool.wait_ge(loaded[s], 16 * (KT + 1) * (b + 1))
                pool.wait_ge(w_ready[s], b)
                pool.sem_inc(waited, 1)
                pool.tensor_scalar(w[:, s, :, :], code[:, s, :, :], 1.0 / 7.5, -1.0, ALU.mult, ALU.add).then_inc(w_coded[s], 1)

            def low(b, s):
                pool.wait_ge(w_hi_ready[s], b + 1)
                pool.tensor_tensor(w_lo[:, s, :, :], w[:, s, :, :], as_f32(w_hi[:, s, :, :]), ALU.subtract).then_inc(w_ready[s], 1)

            with pool.Fori(0, NBK) as b:
                from_codes(b, 0)
                low(b, 0)
                from_codes(b, 1)
                low(b, 1)

        @block.scalar
        def _(act):
            def high(b, s):
                act.wait_ge(w_summed[s], KT * (b + 1))
                act.wait_ge(y_done[s], NT * b)
                act.activation(w_hi[:, s, :, :], w[:, s, :, :], ACT.Copy).then_inc(w_hi_ready[s], 1)

            def turned_high(b, s, to):
                for k in range(KT):
                    act.wait_ge(turned[s], KT * b + k + 1)
                    act.activation(to[:, k, :], ps_t[:, k, :], ACT.Copy).then_inc(hi_ready[s], 1)

            def blk(b, last):
                high(b, 0)
                high(b, 1)
                act.wait_ge(var_ready, b + 1)
                act.activation(std[:, :], var[:, :], ACT.Sqrt).then_inc(std_ready, 1)
                for t in range(NT):
                    act.wait_ge(z_shifted, NT * b + t + 1)
                    act.activation(z[:, t, :], z[:, t, :], ACT.Gelu).then_inc(gelu_ready, 1)
                turned_high(b, 0, zT_hi)
                if not last:
                    turned_high(b, 1, hT_hi)

            with act.Fori(0, NBK - 1) as b:
                blk(b, False)
            blk(NBK - 1, True)

        @block.vector
        def _(dve):
            def matrix(b, s):
                dve.wait_ge(w_coded[s], b + 1)
                dve.tensor_tensor(w[:, s, :, :], w[:, s, :, :], scale[:, s, :, :], ALU.mult).then_inc(w_scaled[s], 1)
                dve.wait_ge(w_scaled[s], b + 1)
                for k in range(KT):
                    dve.wait_ge(rank_done[s], KT * b + k + 1)
                    dve.tensor_tensor(w[:, s, k, :], w[:, s, k, :], ps_l[:, k % 2, :], ALU.add).then_inc(w_summed[s], 1)

            def turned_low(b, s, hi, lo):
                for k in range(KT):
                    dve.wait_ge(hi_ready[s], KT * b + k + 1)
                    dve.tensor_tensor(lo[:, k, :], ps_t[:, k, :], as_f32(hi[:, k, :]), ALU.subtract).then_inc(lo_ready[s], 1)

            def blk(b, last):
                matrix(b, 0)
                matrix(b, 1)
                dve.wait_ge(small_loaded, 64 * (b + 1))
                for t in range(NT):
                    dve.wait_ge(y_done[0], NT * b + t + 1)
                    dve.wait_ge(turned[0], KT * b)
                    dve.tensor_tensor(z[:, t, :], ps_y[:, t % 2, :], bias_sb[:, 0, :], ALU.add).then_inc(y_read[0], 1)
                    dve.wait_ge(y_read[0], NT * b + t + 1)
                    dve.bn_stats(stats[:, t, :], z[:, t, :]).then_inc(stats_ready, 1)
                dve.wait_ge(stats_ready, NT * (b + 1))
                for t in range(NT):
                    dve.tensor_tensor(h[:, t, :], h[:, t, :], bias_sb[:, 1, :], ALU.add).then_inc(h_biased, 1)
                for t in range(NT):
                    dve.bn_aggr(mv[:, t, :], stats[:, t, :]).then_inc(mv_ready, 1)
                dve.wait_ge(mv_ready, NT * (b + 1))
                dve.tensor_scalar(var[:, :], mv[:, :, 1], EPS, None, ALU.add).then_inc(var_ready, 1)
                dve.wait_ge(std_ready, b + 1)
                dve.reciprocal(rstd[:, :], std[:, :]).then_inc(rstd_ready, 1)
                dve.wait_ge(rstd_ready, b + 1)
                for t in range(NT):
                    dve.tensor_scalar(z[:, t, :], z[:, t, :], mv[:, t, 0:1], rstd[:, t:t + 1],
                                      ALU.subtract, ALU.mult).then_inc(z_ready, 1)
                    dve.wait_ge(z_ready, NT * b + t + 1)
                    dve.tensor_tensor(z[:, t, :], z[:, t, :], gamma_sb[:, :], ALU.mult).then_inc(z_scaled, 1)
                    dve.wait_ge(z_scaled, NT * b + t + 1)
                    dve.tensor_tensor(z[:, t, :], z[:, t, :], beta_sb[:, :], ALU.add).then_inc(z_shifted, 1)
                turned_low(b, 0, zT_hi, zT_lo)
                for t in range(NT):
                    dve.wait_ge(y_done[1], NT * b + t + 1)
                    dve.wait_ge(h_biased, NT * b + t + 1)
                    dve.tensor_tensor(h[:, t, :], h[:, t, :], ps_y[:, t % 2, :], ALU.add).then_inc(y_read[1], 1)
                if not last:
                    turned_low(b, 1, hT_hi, hT_lo)

            with dve.Fori(0, NBK - 1) as b:
                blk(b, False)
            blk(NBK - 1, True)
            dve.wait_ge(y_read[1], NT * NBK)
            for t in range(NT):
                dve.tensor_tensor(x[:, t, :], x[:, t, :], h[:, t, :], ALU.add).then_inc(x_ready, 1)

        @block.tensor
        def _(pe):
            def rank_product(b, s):
                pe.wait_ge(rank_loaded[s], 32 * (b + 1))
                for k in range(KT):
                    if k >= 2:
                        pe.wait_ge(w_summed[s], KT * b + k - 1)
                    elif s:
                        pe.wait_ge(w_summed[0], KT * (b + 1))
                    else:
                        pe.wait_ge(w_summed[1], KT * b)
                    pe.matmul(ps_l[:, k % 2, :], la_sb[:, s, P * k:P * k + P], lb_sb[:, s, :],
                              start=True, stop=True).then_inc(rank_done[s], 1)

            def linear(b, s, hi, lo):
                pe.wait_ge(w_ready[s], b + 1)
                for t in range(NT):
                    if t >= 2:
                        pe.wait_ge(y_read[s], NT * b + t - 1)
                    elif s:
                        pe.wait_ge(y_read[0], NT * (b + 1))
                    else:
                        pe.wait_ge(y_read[1], NT * b)
                    tok = slice(t * P, t * P + P)
                    for k in range(KT):
                        for n, (a, v) in enumerate(three(hi[:, k, tok], lo[:, k, tok], w_hi[:, s, k, :], w_lo[:, s, k, :])):
                            mm = pe.matmul(ps_y[:, t % 2, :], a, v, start=(k == 0 and n == 0), stop=(k == KT - 1 and n == 2))
                    mm.then_inc(y_done[s], 1)

            def turn(b, s, of):
                for t in range(NT):
                    if s == 0:
                        pe.wait_ge(gelu_ready, NT * b + t + 1)
                        pe.wait_ge(lo_ready[1], KT * b)
                    else:
                        pe.wait_ge(y_read[1], NT * b + t + 1)
                    for k in range(KT):
                        mm = pe.transpose(ps_t[:, k, t * P:(t + 1) * P], of[:, t, P * k:P * k + P], ident[:, :])
                        if t == NT - 1:
                            mm.then_inc(turned[s], 1)

            def blk(b, last):
                rank_product(b, 0)
                rank_product(b, 1)
                pe.wait_ge(lo_ready[1], KT * b)
                linear(b, 0, hT_hi, hT_lo)
                turn(b, 0, z)
                pe.wait_ge(lo_ready[0], KT * (b + 1))
                linear(b, 1, zT_hi, zT_lo)
                if not last:
                    turn(b, 1, h)

            with pe.Fori(0, NBK - 1) as b:
                blk(b, False)
            blk(NBK - 1, True)


def perceiver(nc, a, out):
    with ExitStack() as ctx:
        m = Memory(nc, ctx, "all")
        x, ident = m.sb("x", [P, NT, D]), m.sb("ident", [P, P])
        loaded, stored = m.sem("loaded"), m.sem("stored")
        with nc.Block() as block:
            @block.sync
            def _(sp):
                sp.dma_start(x[:, :, :], a["x"].rearrange("(t p) d -> p t d", p=P)).then_inc(loaded, 16)
                sp.dma_start(ident[:, :], a["ident"]).then_inc(loaded, 16)
                sp.wait_ge(loaded, 32)

        with ExitStack() as first:
            m = Memory(nc, first, "first")
            xT_hi, xT_lo = m.sb("xT_hi", [P, KT, TOK], F32R), m.sb("xT_lo", [P, KT, TOK], F32R)

            with ExitStack() as stage:
                xn = Memory(nc, stage, "n0").sb("xn", [P, NT, D])
                layernorm(nc, "ln0", x, xn, xT_hi, xT_lo, ident)
            context_attention(nc, "ctx", x, xT_hi, xT_lo, ident, a["ctxT"], a["ctxN"])

            xn = m.sb("xn", [P, NT, D])
            layernorm(nc, "ln1", x, xn, xT_hi, xT_lo, ident)
            head_attention(nc, "att0", x, xn, xT_hi, xT_lo, ident, a["a0_wqk"], a["a0_wv"], a["a0_wo"], a["a0_bqk"],
                           a["a0_bv"], a["a0_bo"], DH, False)
            layernorm(nc, "ln2", x, xn, xT_hi, xT_lo, ident)
            experts(nc, "moe", x, xT_hi, xT_lo, ident, a["before"], a["gate"], a["w1"], a["w3"], a["w2"],
                    a["b1"], a["b3"], a["b2"])

        with ExitStack() as cross:
            m = Memory(nc, cross, "cross")
            bq, bk, bv, bo = m.sb("bq", [P, NG]), m.sb("bk", [P, NG]), m.sb("bv", [P, D]), m.sb("bo", [P, D])
            q, att = m.sb("q", [P, NG, TOK]), m.sb("att", [P, NG, TOK])
            b_loaded = m.sem("b_loaded")
            with nc.Block() as block:
                @block.sync
                def _(sp):
                    sp.dma_start(bq[:, :], a["bq"]).then_inc(b_loaded, 16)
                    sp.dma_start(bk[:, :], a["bk"]).then_inc(b_loaded, 16)
                    sp.dma_start(bv[:, :], a["bv"].to_broadcast([P, D])).then_inc(b_loaded, 16)
                    sp.dma_start(bo[:, :], a["bo"].to_broadcast([P, D])).then_inc(b_loaded, 16)
                    sp.wait_ge(b_loaded, 64)
            with ExitStack() as stage:
                m = Memory(nc, stage, "query")
                xn = m.sb("xn", [P, NT, D])
                xT_hi, xT_lo = m.sb("xT_hi", [P, KT, TOK], F32R), m.sb("xT_lo", [P, KT, TOK], F32R)
                raw, w_hi, w_lo = m.sb("raw", [P, KT, D]), m.sb("w_hi", [P, KT, D], F32R), m.sb("w_lo", [P, KT, D], F32R)
                layernorm(nc, "ln3", x, xn, xT_hi, xT_lo, ident)
                split_weight(nc, "wq", [(a["wq"], w_hi[:, :, :], w_lo[:, :, :])], [raw[:, :, :]])
                project_queries(nc, "pq", q, xT_hi, xT_lo, w_hi, w_lo, bq)
            with ExitStack() as stage:
                m = Memory(nc, stage, "kv")
                wk = m.sb("wk_hi", [P, KT, D], F32R), m.sb("wk_lo", [P, KT, D], F32R)
                wv = m.sb("wv_hi", [P, KT, D], F32R), m.sb("wv_lo", [P, KT, D], F32R)
                with ExitStack() as loading:
                    raw = Memory(nc, loading, "kv_raw").sb("raw", [P, 2, KT, D])
                    split_weight(nc, "wkv", [(a["wk"], wk[0][:, :, :], wk[1][:, :, :]), (a["wv"], wv[0][:, :, :], wv[1][:, :, :])],
                                 [raw[:, 0, :, :], raw[:, 1, :, :]])
                masked_context_attention(nc, "cross", q, att, ident, wk, wv, bk, bv, a["ctxT"], a["mask"], a["gain"])
            with ExitStack() as stage:
                m = Memory(nc, stage, "after")
                raw, w_hi, w_lo = m.sb("raw", [P, KT, D]), m.sb("w_hi", [P, KT, D], F32R), m.sb("w_lo", [P, KT, D], F32R)
                split_weight(nc, "wo", [(a["wo"], w_hi[:, :, :], w_lo[:, :, :])], [raw[:, :, :]])
                project_attended(nc, "po", x, att, w_hi, w_lo, bo)

        with ExitStack() as last:
            m = Memory(nc, last, "last")
            xn = m.sb("xn", [P, NT, D])
            xT_hi, xT_lo = m.sb("xT_hi", [P, KT, TOK], F32R), m.sb("xT_lo", [P, KT, TOK], F32R)
            layernorm(nc, "ln4", x, xn, xT_hi, xT_lo, ident)
            head_attention(nc, "att1", x, xn, xT_hi, xT_lo, ident, a["a1_wqk"], a["a1_wv"], a["a1_wo"], a["a1_bqk"],
                           a["a1_bv"], a["a1_bo"], D // 2, True)
            layernorm(nc, "ln5", x, xn, xT_hi, xT_lo, ident)
            quantized_blocks(nc, "quant", x, xn, xT_hi, xT_lo, ident, a["codes"], a["scales"], a["la"], a["lb"],
                             a["bias"], a["gamma"], a["beta"])

        with nc.Block() as block:
            @block.sync
            def _(sp):
                sp.dma_start(out.rearrange("(t p) d -> p t d", p=P), x[:, :, :]).then_inc(stored, 16)
                sp.wait_ge(stored, 16)




def _slices(w):
    return w.reshape(w.shape[0] // P, P, -1).transpose(1, 0, 2)


def _head_groups(np, wq, wk, wv, wo, bq, bk, bv, bo, dv):
    parts = max(1, HG * dv // 512)
    vc = HG * dv // parts
    both = [np.concatenate([wq[:, g * P:g * P + P], wk[:, g * P:g * P + P]], 1) for g in range(NG)]
    return {
        "wqk": np.stack([_slices(w) for w in both]),
        "wv": np.stack([_slices(wv[:, i * vc:i * vc + vc]) for i in range(NG * parts)]).reshape(NG, parts, P, KT, vc),
        "wo": np.stack([_slices(wo[i * vc:i * vc + vc]) for i in range(NG * parts)]).reshape(NG, parts, P, vc // P, D),
        "bqk": np.stack([bq.reshape(NG, P), bk.reshape(NG, P)], -1).transpose(1, 0, 2),
        "bv": bv.reshape(NG, 1, HG * dv),
        "bo": bo.reshape(1, D),
    }


def kernel(**inputs):
    import numpy as np
    import concourse.bacc as bacc
    from concourse.bass_utils import run_bass_kernel_spmd

    i = {name: np.asarray(v) for name, v in inputs.items()}
    ctx = i["ctx_1024"]
    padded = np.concatenate([ctx.transpose(0, 2, 1), np.zeros((B, D, S2P - S2), ctx.dtype)], 2)
    a = {
        "x": i["x"].reshape(TOK, D),
        "ident": np.eye(P, dtype=np.float32),
        "before": np.tril(np.ones((NE - 1, NE - 1), np.float32), -1).reshape(1, -1),
        "ctxN": ctx,
        "ctxT": padded.reshape(B, KT, P, S2P).transpose(0, 2, 1, 3),
        "mask": i["mask_BxSxS2_ik1"],
        "gain": i["fside_BxSxS2_0"],
    }
    w, b = i["L0_attn_Wqkv"], i["L0_attn_bqkv"]
    layer = _head_groups(np, w[:, 0:D], w[:, D:2 * D], w[:, 2 * D:], i["L0_attn_Wo"], b[0:D], b[D:2 * D], b[2 * D:],
                         i["L0_attn_bo"], DH)
    a.update({f"a0_{n}": v for n, v in layer.items()})
    w, b = i["L1_attn_Wc"].T, i["L1_attn_bc"]
    layer = _head_groups(np, w[:, 0:D], w[:, D:2 * D], w[:, 2 * D:], i["L1_attn_Wo"].T, b[0:D], b[D:2 * D], b[2 * D:],
                         i["L1_attn_bo"], D // 2)
    a.update({f"a1_{n}": v for n, v in layer.items()})
    a["gate"] = _slices(i["L0_ffn_gate_w"].T)
    for n in "132":
        a[f"w{n}"] = np.stack([_slices(v) for v in [*i[f"L0_ffn_w{n}"], i[f"L0_ffn_sw{n}"]]])
        bias = np.concatenate([i[f"L0_ffn_b{n}"], i[f"L0_ffn_sb{n}"][None]])
        a[f"b{n}"] = bias if n == "2" else bias.reshape(NE, KT, P).transpose(2, 0, 1)
    for n in "qkvo":
        a[f"w{n}"] = _slices(i[f"L1_xattn_w{n}_k"])
        bias = i[f"L1_xattn_w{n}_b"]
        a[f"b{n}"] = bias.reshape(NG, P).T if n in "qk" else bias.reshape(1, D)
    a["codes"] = np.stack([_slices(c.T) for c in i["L1_ffn_qweights"]])
    a["scales"] = i["L1_ffn_scales"].transpose(0, 2, 1)
    a["la"] = i["L1_ffn_lora_a"]
    a["lb"] = i["L1_ffn_lora_b"].transpose(0, 2, 1)
    a["bias"] = i["L1_ffn_biases"].reshape(-1, 1, D)
    a["gamma"] = i["L1_ffn_ln_gamma"].reshape(-1, 1, D)
    a["beta"] = i["L1_ffn_ln_beta"].reshape(-1, 1, D)

    nc = bacc.Bacc("TRN2", target_bir_lowering=False, num_devices=1)
    arrays = {f"in_{n}": np.ascontiguousarray(v) for n, v in a.items()}
    aps = {n: nc.dram_tensor(f"in_{n}", arrays[f"in_{n}"].shape, mybir.dt.from_np(arrays[f"in_{n}"].dtype),
                             kind="ExternalInput").ap() for n in a}
    out = nc.dram_tensor("out", (TOK, D), F32, kind="ExternalOutput").ap()
    perceiver(nc, aps, out)
    r = run_bass_kernel_spmd(nc, [arrays], core_ids=[0])
    return r.results[0]["out"].reshape(B, S, D)
```

```python
from contextlib import ExitStack
from math import sqrt

import concourse.bass as bass
from concourse import mybir

F32 = mybir.dt.float32
F32R = mybir.dt.float32r
I32 = mybir.dt.int32
ALU = mybir.AluOpType
ACT = mybir.ActivationFunctionType
AX_X = mybir.AxisListType.X

P = 128
B, S, D = 8, 64, 512
TOK = B * S
NT = TOK // P
KT = D // P
S2 = 1601
S2P = S2 + 1
CH0 = [0, 402, 802, 1202]
CHW = [402, 400, 400, 400]
CHV = [402, 400, 400, 399]
NJ = 13
JR = [P] * 12 + [S2 - 12 * P]
JG = [(0, 4), (4, 8), (8, 12), (12, 13)]
H = 16
HG = 4
NG = H // HG
DH = D // H
NE = 9
EPS = 1e-5
LOW = -3.0e38


def as_f32(ap):
    return ap.bitcast(F32)


def three(hi_a, lo_a, hi_b, lo_b):
    return ((hi_a, hi_b), (hi_a, lo_b), (lo_a, hi_b))


class Memory:

    def __init__(self, nc, ctx, stage):
        self.nc, self.ctx, self.stage = nc, ctx, stage
        self.used = []
        ctx.callback(self.clear)

    def sb(self, name, shape, dt=F32):
        return self.ctx.enter_context(self.nc.sbuf_tensor(f"{self.stage}_{name}", shape, dt))

    def pb(self, name, shape, dt=F32):
        return self.ctx.enter_context(self.nc.psum_tensor(f"{self.stage}_{name}", shape, dt))

    def sem(self, name):
        self.used.append(self.nc.alloc_semaphore(f"{self.stage}_{name}"))
        return self.used[-1]

    def clear(self):
        if self.used:
            self.nc.clear_and_free_semaphores(self.used)
            self.nc.all_engine_barrier()

    def sems(self, name, n):
        return [self.sem(f"{name}{i}") for i in range(n)]


def layernorm(nc, stage, x, xn, xT_hi, xT_lo, ident, prefetch=None, x_loaded=None):
    with ExitStack() as ctx:
        m = Memory(nc, ctx, stage)
        stats = m.sb("stats", [P, NT, 6])
        mv = m.sb("mv", [P, NT, 2])
        var = m.sb("var", [P, NT])
        std = m.sb("std", [P, NT])
        rstd = m.sb("rstd", [P, NT])
        turned = m.pb("turned", [P, NT, KT, P])
        stats_ready, mv_ready, var_ready = m.sem("stats_ready"), m.sem("mv_ready"), m.sem("var_ready")
        std_ready, rstd_ready, xn_ready = m.sem("std_ready"), m.sem("rstd_ready"), m.sem("xn_ready")
        turned_ready, hi_ready, lo_ready = m.sem("turned_ready"), m.sem("hi_ready"), m.sem("lo_ready")
        block = ctx.enter_context(nc.Block())

        if prefetch is not None:
            @block.sync
            def _(sp):
                prefetch(sp)

        @block.vector
        def _(dve):
            for t in range(NT):
                if x_loaded is not None:
                    dve.wait_ge(x_loaded[t], 16)
                dve.bn_stats(stats[:, t, :], x[:, t, :]).then_inc(stats_ready, 1)
            for t in range(NT):
                dve.wait_ge(stats_ready, t + 1)
                dve.bn_aggr(mv[:, t, :], stats[:, t, :]).then_inc(mv_ready, 1)
            dve.wait_ge(mv_ready, NT)
            dve.tensor_scalar(var[:, :], mv[:, :, 1], EPS, None, ALU.add).then_inc(var_ready, 1)
            dve.wait_ge(std_ready, 1)
            dve.reciprocal(rstd[:, :], std[:, :]).then_inc(rstd_ready, 1)
            dve.wait_ge(rstd_ready, 1)
            for t in range(NT):
                dve.tensor_scalar(xn[:, t, :], x[:, t, :], mv[:, t, 0:1], rstd[:, t:t + 1],
                                  ALU.subtract, ALU.mult).then_inc(xn_ready, 1)
            if xT_lo is not None:
                for t in range(NT):
                    tok = slice(t * P, t * P + P)
                    dve.wait_ge(hi_ready, t + 1)
                    dve.tensor_tensor(xT_lo[:, :, tok], turned[:, t, :, :], as_f32(xT_hi[:, :, tok]),
                                      ALU.subtract).then_inc(lo_ready, 1)

        @block.scalar
        def _(act):
            act.wait_ge(var_ready, 1)
            act.activation(std[:, :], var[:, :], ACT.Sqrt).then_inc(std_ready, 1)
            for t in range(NT):
                act.wait_ge(turned_ready, t + 1)
                act.activation(xT_hi[:, :, t * P:(t + 1) * P], turned[:, t, :, :], ACT.Copy).then_inc(hi_ready, 1)

        @block.tensor
        def _(pe):
            if x_loaded is not None:
                pe.wait_ge(x_loaded[NT], 16)
            for t in range(NT):
                pe.wait_ge(xn_ready, t + 1)
                for k in range(KT):
                    turn = pe.transpose(turned[:, t, k, :], xn[:, t, k * P:(k + 1) * P], ident[:, :])
                turn.then_inc(turned_ready, 1)


def context_attention(nc, stage, norm, x, xT, ident, ctxT, ctxN):
    with ExitStack() as ctx:
        m = Memory(nc, ctx, stage)
        raw_T = m.sb("raw_T", [P, 2, KT, S2P])
        raw_N = m.sb("raw_N", [P, NJ, D])
        N_hi, N_lo = m.sb("N_hi", [P, NJ, D], F32R), m.sb("N_lo", [P, NJ, D], F32R)
        xs = m.sb("xs", [P, 2, KT, S])
        sc = m.sb("sc", [S, S2])
        pT = m.sb("pT", [P, NJ, 2 * S], F32R)
        cmax, csum = m.sb("cmax", [S, 4]), m.sb("csum", [S, 4])
        rmax, nmax, rsum, rinv = m.sb("rmax", [S, 1]), m.sb("nmax", [S, 1]), m.sb("rsum", [S, 1]), m.sb("rinv", [S, 1])
        o_below, o_sum = m.sb("o_below", [S, D]), m.sb("o_sum", [S, D])
        o_norm = m.sb("o_norm", [P, D])
        T_loaded = [m.sems(f"T_loaded{s}_", 4) for s in range(2)]
        N_loaded, N_hi_ready, N_split = (m.sems(n, len(JG)) for n in ("N_loaded", "N_hi_ready", "N_split"))
        xs_ready, scores_done, cmax_ready, rmax_ready, nmax_ready = (m.sem(n) for n in ("xs_ready", "scores_done", "cmax_ready", "rmax_ready", "nmax_ready"))
        exp_ready, rsum_ready, rinv_ready, turned, pT_hi_ready, pT_ready = (m.sem(n) for n in ("exp_ready", "rsum_ready", "rinv_ready", "turned", "pT_hi_ready", "pT_ready"))
        multiplied, o_below_ready, o_sum_ready, o_norm_ready, x_ready = (m.sem(n) for n in ("multiplied", "o_below_ready", "o_sum_ready", "o_norm_ready", "x_ready"))
        waited = m.sem("waited")
        pool_groups = (0, 3)
        turned_tiles = ((0, 8, P), (8, 12, P), (12, 13, JR[-1]))

        def steps(eng, batch):
            with eng.Fori(0, NT - 1) as t:
                batch(t, 0, False)
                batch(t, 1, False)
            batch(NT - 1, 0, True)
            batch(NT - 1, 1, True)

        def load_T(sp, b, t, s):
            for c in range(4):
                cols = slice(CH0[c], CH0[c] + CHW[c])
                sp.dma_start(raw_T[:, s, :, cols], ctxT[b, :, :, cols]).then_inc(T_loaded[s][c], 16)

        def load_N(sp, b, wait):
            for g, (j0, j1) in enumerate(JG):
                if wait:
                    sp.wait_ge(N_split[g], b)
                if g < 3:
                    rows = ctxN[b, j0 * P:j1 * P, :].rearrange("(j p) d -> p j d", p=P)
                    sp.dma_start(raw_N[:, j0:j1, :], rows).then_inc(N_loaded[g], 16)
                else:
                    sp.dma_start(raw_N[0:JR[-1], j0, :], ctxN[b, j0 * P:S2, :]).then_inc(N_loaded[g], 16)

        def prefetch(sp):
            load_T(sp, 0, 0, 0)
            load_N(sp, 0, False)
            load_T(sp, 1, 0, 1)

        norm(prefetch)
        ps_s = m.pb("ps_s", [P, 4, 512])
        ps_t = m.pb("ps_t", [P, 16, S])
        ps_o = m.pb("ps_o", [P, D])
        block = ctx.enter_context(nc.Block())

        @block.sync
        def _(sp):
            with sp.Fori(0, NT - 1) as t:
                for s in range(2):
                    sp.wait_ge(scores_done, 4 * (2 * t + s + 1))
                    load_T(sp, 2 * t + s + 2, t + 1, s)
                    load_N(sp, 2 * t + s + 1, True)
            load_N(sp, B - 1, True)

        @block.scalar
        def _(act):
            def split_N(b):
                for g, (j0, j1) in enumerate(JG):
                    r = JR[j0]
                    act.wait_ge(N_loaded[g], 16 * (b + 1))
                    act.wait_ge(multiplied, b)
                    act.activation(N_hi[0:r, j0:j1, :], raw_N[0:r, j0:j1, :], ACT.Copy).then_inc(N_hi_ready[g], 1)

            def exps(b):
                act.wait_ge(turned, b)
                act.wait_ge(nmax_ready, b + 1)
                for c in range(4):
                    act.activation(sc[:, CH0[c]:CH0[c] + CHV[c]], ps_s[0:S, c, 0:CHV[c]], ACT.Exp, bias=nmax[:, :],
                                   accum_out=csum[:, c:c + 1]).then_inc(exp_ready, 1)

            def turned_high(b):
                act.wait_ge(turned, b + 1)
                act.wait_ge(multiplied, b)
                for j0, j1, r in turned_tiles:
                    act.activation(pT[0:r, j0:j1, 0:S], ps_t[0:r, j0:j1, :], ACT.Copy).then_inc(pT_hi_ready, 1)

            def out_below(b):
                act.wait_ge(multiplied, b + 1)
                act.activation(o_below[:, :], ps_o[S:2 * S, :], ACT.Copy).then_inc(o_below_ready, 1)

            def batch(t, s, last):
                b = 2 * t + s
                split_N(b)
                if not (last and s == 1):
                    exps(b + 1)
                out_below(b)
                if not (last and s == 1):
                    turned_high(b + 1)

            exps(0)
            turned_high(0)
            steps(act, batch)

        @block.gpsimd
        def _(pool):
            with pool.Fori(0, B) as b:
                for g in pool_groups:
                    (j0, j1), r = JG[g], JR[JG[g][0]]
                    pool.wait_ge(N_hi_ready[g], b + 1)
                    pool.tensor_tensor(N_lo[0:r, j0:j1, :], raw_N[0:r, j0:j1, :], as_f32(N_hi[0:r, j0:j1, :]),
                                       ALU.subtract).then_inc(N_split[g], 1)

        @block.vector
        def _(dve):
            def stage_x(b, s):
                dve.tensor_copy(xs[:, s, :, :], xT[:, :, bass.ts(b, S)]).then_inc(xs_ready, 1)

            def split_N(b):
                for g, (j0, j1) in enumerate(JG):
                    if g not in pool_groups:
                        dve.wait_ge(N_hi_ready[g], b + 1)
                        dve.tensor_tensor(N_lo[:, j0:j1, :], raw_N[:, j0:j1, :], as_f32(N_hi[:, j0:j1, :]),
                                          ALU.subtract).then_inc(N_split[g], 1)

            def maxima(b):
                for c in range(4):
                    dve.wait_ge(scores_done, 4 * b + c + 1)
                    dve.tensor_reduce(cmax[:, c:c + 1], ps_s[0:S, c, 0:CHV[c]], AX_X, ALU.max).then_inc(cmax_ready, 1)
                dve.wait_ge(cmax_ready, 4 * b + 4)
                dve.tensor_reduce(rmax[:, :], cmax[:, :], AX_X, ALU.max).then_inc(rmax_ready, 1)
                dve.wait_ge(rmax_ready, b + 1)
                dve.tensor_scalar(nmax[:, :], rmax[:, :], -1.0, None, ALU.mult).then_inc(nmax_ready, 1)

            def turned_low(b):
                for i, (j0, j1, r) in enumerate(turned_tiles):
                    dve.wait_ge(pT_hi_ready, 3 * b + (1 if i == 0 else 3))
                    dve.tensor_tensor(pT[0:r, j0:j1, S:2 * S], ps_t[0:r, j0:j1, :], as_f32(pT[0:r, j0:j1, 0:S]),
                                      ALU.subtract).then_inc(pT_ready, 1)

            def sums(b):
                dve.wait_ge(exp_ready, 4 * (b + 1))
                dve.tensor_reduce(rsum[:, :], csum[:, :], AX_X, ALU.add).then_inc(rsum_ready, 1)
                dve.wait_ge(rsum_ready, b + 1)
                dve.reciprocal(rinv[:, :], rsum[:, :]).then_inc(rinv_ready, 1)

            def add_out(b, t, s):
                q = slice(S * s, S * s + S)
                dve.wait_ge(o_below_ready, b + 1)
                dve.tensor_tensor(o_sum[:, :], ps_o[0:S, :], o_below[:, :], ALU.add).then_inc(o_sum_ready, 1)
                dve.wait_ge(rinv_ready, b + 1)
                dve.wait_ge(o_sum_ready, b + 1)
                dve.tensor_scalar(o_norm[q, :], o_sum[:, :], rinv[:, 0:1], None, ALU.mult).then_inc(o_norm_ready, 1)
                dve.wait_ge(o_norm_ready, b + 1)
                dve.tensor_tensor(x[q, t, :], x[q, t, :], o_norm[q, :], ALU.add).then_inc(x_ready, 1)

            def batch(t, s, last):
                b = 2 * t + s
                split_N(b)
                if not (last and s == 1):
                    maxima(b + 1)
                if not last:
                    stage_x(b + 2, s)
                add_out(b, t, s)
                if not (last and s == 1):
                    sums(b + 1)
                    turned_low(b + 1)

            stage_x(0, 0)
            stage_x(1, 1)
            maxima(0)
            sums(0)
            turned_low(0)
            steps(dve, batch)

        @block.tensor
        def _(pe):
            def scores(b, t, s):
                pe.wait_ge(xs_ready, b + 1)
                for c in range(4):
                    pe.wait_ge(T_loaded[s][c], 16 * (t + 1))
                    for k in range(KT):
                        mm = pe.matmul(ps_s[0:S, c, 0:CHW[c]], xs[:, s, k, :], raw_T[:, s, k, CH0[c]:CH0[c] + CHW[c]],
                                       start=(k == 0), stop=(k == KT - 1))
                    mm.then_inc(scores_done, 1)

            def turn(b):
                pe.wait_ge(pT_ready, 3 * b)
                pe.wait_ge(exp_ready, 4 * (b + 1))
                pe.sem_inc(waited, 1)
                for j in range(NJ):
                    last = pe.transpose(ps_t[0:JR[j], j, :], sc[:, j * P:j * P + JR[j]], ident[0:S, 0:S])
                last.then_inc(turned, 1)

            def values(b):
                pe.wait_ge(pT_ready, 3 * b + 3)
                pe.wait_ge(o_sum_ready, b)
                for g, (j0, j1) in enumerate(JG):
                    pe.wait_ge(N_split[g], b + 1)
                    for j in range(j0, j1):
                        r = JR[j]
                        pairs = [(2 * S, N_hi), (S, N_lo)] if j < NJ - 1 else [(S, N_lo), (2 * S, N_hi)]
                        for n, (rows, half) in enumerate(pairs):
                            mm = pe.matmul(ps_o[0:rows, :], pT[0:r, j, 0:rows], half[0:r, j, :],
                                           start=(j == 0 and n == 0), stop=(j == NJ - 1 and n == 1))
                mm.then_inc(multiplied, 1)

            def batch(t, s, last):
                b = 2 * t + s
                if not (last and s == 1):
                    scores(b + 1, t + s, 1 - s)
                values(b)
                if not (last and s == 1):
                    turn(b + 1)

            scores(0, 0, 0)
            turn(0)
            steps(pe, batch)


def head_attention(nc, stage, norm, x, xn, xT_hi, xT_lo, ident, wqk, wv, wo, bqk, bv, bo, dv, rectified):
    parts = max(1, HG * dv // 512)
    vc = HG * dv // parts
    hp = HG // parts
    ko = vc // P
    kc = max(1, dv // P)
    scale = 1.0 / sqrt(DH)
    with ExitStack() as ctx:
        m = Memory(nc, ctx, stage)
        raw_qk = m.sb("raw_qk", [P, KT, 2 * P])
        raw_v = m.sb("raw_v", [P, KT, vc])
        raw_o = m.sb("raw_o", [P, ko, D])
        qk_hi, qk_lo = m.sb("qk_hi", [P, KT, 2 * P], F32R), m.sb("qk_lo", [P, KT, 2 * P], F32R)
        wv_hi, wv_lo = m.sb("wv_hi", [P, KT, vc], F32R), m.sb("wv_lo", [P, KT, vc], F32R)
        wo_hi, wo_lo = m.sb("wo_hi", [P, ko, D], F32R), m.sb("wo_lo", [P, ko, D], F32R)
        bqk_sb = m.sb("bqk_sb", [P, NG, 2])
        bv_sb = m.sb("bv_sb", [P, parts, vc])
        qk = m.sb("qk", [P, 2, TOK])
        v_sum = m.sb("v_sum", [P, 2, vc])
        v_hi, v_lo = m.sb("v_hi", [P, NT, vc], F32R), m.sb("v_lo", [P, NT, vc], F32R)
        smax, rsum, rinv = m.sb("smax", [P, HG, NT]), m.sb("rsum", [P, HG, NT]), m.sb("rinv", [P, HG, NT])
        sc = m.sb("sc", [P, HG, NT, S])
        probs = m.sb("probs", [P, HG, NT, P])
        pT_hi, pT_lo = m.sb("pT_hi", [P, 2, TOK], F32R), m.sb("pT_lo", [P, 2, TOK], F32R)
        o_hi, o_lo = m.sb("o_hi", [P, ko, TOK], F32R), m.sb("o_lo", [P, ko, TOK], F32R)
        y = m.sb("y", [P, NT, D])

        start_loaded, y_loaded, qk_loaded, v_loaded, o_loaded, bv_loaded = (m.sem(n) for n in ("start_loaded", "y_loaded", "qk_loaded", "v_loaded", "o_loaded", "bv_loaded"))
        wqk_hi_ready, wqk_ready, wv_hi_ready, wv_ready, wo_hi_ready, wo_ready = (m.sem(n) for n in (
            "wqk_hi_ready", "wqk_ready", "wv_hi_ready", "wv_ready", "wo_hi_ready", "wo_ready"))
        qk_done, v_done, y_done = m.sem("qk_done"), m.sem("v_done"), m.sem("y_done")
        qk_added, v_added, y_added = m.sem("qk_added"), m.sem("v_added"), m.sem("y_added")
        qk_sum_ready, qk_ready, scores_done, smax_ready, sub_ready = (m.sem(n) for n in ("qk_sum_ready", "qk_ready", "scores_done", "smax_ready", "sub_ready"))
        exp_ready, rsum_ready, rinv_ready, zero_ready, probs_ready = (m.sem(n) for n in ("exp_ready", "rsum_ready", "rinv_ready", "zero_ready", "probs_ready"))
        turned, pT_hi_ready, pT_ready = (m.sem(n) for n in ("turned", "pT_hi_ready", "pT_ready"))
        v_sum_ready, v_hi_ready, v_ready = (m.sem(n) for n in ("v_sum_ready", "v_hi_ready", "v_ready"))
        o_done, o_hi_ready, o_ready, x_ready = (m.sem(n) for n in ("o_done", "o_hi_ready", "o_ready", "x_ready"))

        n_o = ko if dv >= P else HG

        def uses(g, part, t=0):
            return (g * parts + part) * NT + t

        v_sum_stands = v_sum_ready if rectified else v_added

        def outputs_of(g, h):
            return g * parts * n_o + h * kc

        def load_qk(sp, g, first=False):
            if not first:
                sp.wait_ge(wqk_ready, g)
            sp.dma_start(raw_qk[:, :, :], wqk[g]).then_inc(qk_loaded, 16)

        def load_v(sp, g, part, first=False):
            if not first:
                sp.wait_ge(wv_ready, g * parts + part)
            sp.dma_start(raw_v[:, :, :], wv[g, part]).then_inc(v_loaded, 16)

        def load_o(sp, g, part, first=False):
            if not first:
                sp.wait_ge(wo_ready, g * parts + part)
            sp.dma_start(raw_o[:, :, :], wo[g, part]).then_inc(o_loaded, 16)

        def load_bv(sp, g, first=False):
            if not first:
                sp.wait_ge(v_ready, uses(g, 0))
            sp.dma_start(bv_sb[:, :, :].rearrange("p a c -> p (a c)"),
                         bv[g].to_broadcast([P, HG * dv])).then_inc(bv_loaded, 16)

        def prefetch(sp):
            load_qk(sp, 0, True)
            sp.dma_start(bqk_sb[:, :, :], bqk).then_inc(start_loaded, 16)
            load_v(sp, 0, 0, True)
            load_bv(sp, 0, True)
            load_o(sp, 0, 0, True)
            for t in range(NT):
                sp.dma_start(y[:, t, :], bo.to_broadcast([P, D])).then_inc(y_loaded, 16)

        norm(prefetch)
        ps_p = m.pb("ps_p", [P, 2, 512])
        ps_s = m.pb("ps_s", [P, HG, 512])
        ps_o = m.pb("ps_o", [P, 2, 512])
        block = ctx.enter_context(nc.Block())

        @block.sync
        def _(sp):
            if parts == 2:
                load_v(sp, 0, 1)
            with sp.Fori(0, NG - 1) as g:
                load_qk(sp, g + 1)
                load_v(sp, g + 1, 0)
                if parts == 2:
                    load_o(sp, g, 1)
                load_bv(sp, g + 1)
                if parts == 2:
                    load_v(sp, g + 1, 1)
                load_o(sp, g + 1, 0)
            if parts == 2:
                load_o(sp, NG - 1, 1)

        @block.scalar
        def _(act):
            def split_qk(g):
                act.wait_ge(qk_loaded, 16 * (g + 1))
                act.wait_ge(qk_done, 2 * g)
                act.activation(qk_hi[:, :, :], raw_qk[:, :, :], ACT.Copy).then_inc(wqk_hi_ready, 1)

            def split_v(g, part):
                act.wait_ge(v_loaded, 16 * (g * parts + part + 1))
                act.wait_ge(v_done, uses(g, part))
                act.activation(wv_hi[:, :, :], raw_v[:, :, :], ACT.Copy).then_inc(wv_hi_ready, 1)

            def split_o(g, part):
                act.wait_ge(o_loaded, 16 * (g * parts + part + 1))
                act.wait_ge(y_done, uses(g, part))
                act.activation(wo_hi[:, :, :], raw_o[:, :, :], ACT.Copy).then_inc(wo_hi_ready, 1)

            def exps(g):
                act.wait_ge(sub_ready, HG * (g + 1))
                act.activation(sc[:, :, :, :], sc[:, :, :, :], ACT.Exp, scale=scale).then_inc(exp_ready, 1)

            def values_high(g, part):
                act.wait_ge(o_done, outputs_of(g, part * hp))
                for t in range(NT):
                    act.wait_ge(v_sum_stands, uses(g, part, t + 1))
                    act.activation(v_hi[:, t, :], v_sum[:, t % 2, :], ACT.Copy).then_inc(v_hi_ready, 1)

            def turned_high(g, h):
                act.wait_ge(turned, g * HG + h + 1)
                act.wait_ge(o_done, outputs_of(g, max(0, h - 1)))
                act.activation(pT_hi[:, h % 2, :], ps_s[:, h, :], ACT.Copy).then_inc(pT_hi_ready, 1)

            def output_high(g, n):
                act.wait_ge(y_done, uses(g, n // n_o))
                act.wait_ge(o_done, g * parts * n_o + n + 1)
                k, rows = (n % n_o, slice(0, P)) if dv >= P else (0, slice(dv * n, dv * n + dv))
                act.activation(o_hi[rows, k, :], ps_o[rows, n % 2, :], ACT.Copy).then_inc(o_hi_ready, 1)

            def group(g, last):
                if parts == 1:
                    if not last:
                        split_qk(g + 1)
                    output_high(g, 0)
                    turned_high(g, 2)
                    output_high(g, 1)
                    turned_high(g, 3)
                    split_o(g, 0)
                    output_high(g, 2)
                    output_high(g, 3)
                    if not last:
                        split_v(g + 1, 0)
                        exps(g + 1)
                        values_high(g + 1, 0)
                else:
                    for n in range(n_o):
                        output_high(g, n)
                    split_o(g, 0)
                    if not last:
                        split_qk(g + 1)
                    values_high(g, 1)
                    turned_high(g, 2)
                    turned_high(g, 3)
                    if last:
                        split_o(g, 1)
                    else:
                        split_v(g + 1, 0)
                    for n in range(n_o, 2 * n_o):
                        output_high(g, n)
                    if not last:
                        split_o(g, 1)
                        exps(g + 1)
                        values_high(g + 1, 0)
                if not last:
                    turned_high(g + 1, 0)
                    turned_high(g + 1, 1)
                    if parts == 2:
                        split_v(g + 1, 1)

            split_qk(0)
            split_v(0, 0)
            exps(0)
            values_high(0, 0)
            turned_high(0, 0)
            turned_high(0, 1)
            if parts == 2:
                split_v(0, 1)
            with act.Fori(0, NG - 1) as g:
                group(g, False)
            group(NG - 1, True)

        @block.gpsimd
        def _(pool):
            def qk_low(g):
                pool.wait_ge(wqk_hi_ready, g + 1)
                pool.tensor_tensor(qk_lo[:, :, :], raw_qk[:, :, :], as_f32(qk_hi[:, :, :]), ALU.subtract).then_inc(wqk_ready, 1)

            def wv_low(g, part):
                pool.wait_ge(wv_hi_ready, g * parts + part + 1)
                pool.tensor_tensor(wv_lo[:, :, :], raw_v[:, :, :], as_f32(wv_hi[:, :, :]), ALU.subtract).then_inc(wv_ready, 1)

            def wo_low(g, part):
                pool.wait_ge(wo_hi_ready, g * parts + part + 1)
                pool.tensor_tensor(wo_lo[:, :, :], raw_o[:, :, :], as_f32(wo_hi[:, :, :]), ALU.subtract).then_inc(wo_ready, 1)

            def values_low(g, part):
                for t in range(NT):
                    pool.wait_ge(v_hi_ready, uses(g, part, t + 1))
                    pool.tensor_tensor(v_lo[:, t, :], v_sum[:, t % 2, :], as_f32(v_hi[:, t, :]), ALU.subtract).then_inc(v_ready, 1)

            def group(g, last):
                if parts == 1:
                    if not last:
                        qk_low(g + 1)
                    wo_low(g, 0)
                    if not last:
                        wv_low(g + 1, 0)
                        values_low(g + 1, 0)
                else:
                    wo_low(g, 0)
                    if not last:
                        qk_low(g + 1)
                    values_low(g, 1)
                    if last:
                        wo_low(g, 1)
                    else:
                        wv_low(g + 1, 0)
                        wo_low(g, 1)
                        values_low(g + 1, 0)
                        wv_low(g + 1, 1)

            pool.memset(probs[:, :, :, :], 0.0).then_inc(zero_ready, 1)
            qk_low(0)
            wv_low(0, 0)
            values_low(0, 0)
            if parts == 2:
                wv_low(0, 1)
            with pool.Fori(0, NG - 1) as g:
                group(g, False)
            group(NG - 1, True)

        @block.vector
        def _(dve):
            def query_key(g, i):
                dve.wait_ge(scores_done, g)
                dve.wait_ge(qk_done, 2 * g + i + 1)
                dve.tensor_scalar(qk[:, i, :], ps_p[:, i, :], bqk_sb[:, g, i:i + 1], None, ALU.add).then_inc(qk_added, 1)
                if rectified:
                    dve.wait_ge(qk_added, 2 * g + i + 1)
                    dve.scalar_tensor_tensor(out=qk[:, i, :], in0=qk[:, i, :], scalar=0.01, in1=qk[:, i, :],
                                             op0=ALU.mult, op1=ALU.max).then_inc(qk_ready, 1)

            def values(g, part, t):
                dve.wait_ge(v_done, uses(g, part, t + 1))
                dve.wait_ge(v_ready, uses(g, part, max(0, t - 1)))
                dve.tensor_tensor(v_sum[:, t % 2, :], ps_p[:, t % 2, 0:vc], bv_sb[:, part, :], ALU.add).then_inc(v_added, 1)
                if rectified:
                    dve.wait_ge(v_added, uses(g, part, t + 1))
                    dve.scalar_tensor_tensor(out=v_sum[:, t % 2, :], in0=v_sum[:, t % 2, :], scalar=0.01,
                                             in1=v_sum[:, t % 2, :], op0=ALU.mult, op1=ALU.max).then_inc(v_sum_ready, 1)

            def softmax_and_values(g):
                dve.wait_ge(scores_done, g + 1)
                for_scores = ps_s[:, :, 0:NT * S].rearrange("p h (t k) -> p h t k", k=S)
                dve.tensor_reduce(smax[:, :, :], for_scores, AX_X, ALU.max).then_inc(smax_ready, 1)
                dve.wait_ge(smax_ready, g + 1)
                for h in range(HG):
                    dve.tensor_tensor(sc[:, h, :, :], for_scores[:, h, :, :],
                                      smax[:, h, :].unsqueeze(2).to_broadcast([P, NT, S]), ALU.subtract).then_inc(sub_ready, 1)
                dve.wait_ge(bv_loaded, 16 * (g + 1))
                values(g, 0, 0)
                dve.wait_ge(exp_ready, g + 1)
                dve.tensor_reduce(rsum[:, :, :], sc[:, :, :, :], AX_X, ALU.add).then_inc(rsum_ready, 1)
                dve.wait_ge(rsum_ready, g + 1)
                dve.reciprocal(rinv[:, :, :], rsum[:, :, :]).then_inc(rinv_ready, 1)
                dve.wait_ge(rinv_ready, g + 1)
                dve.wait_ge(turned, g * HG)
                for half in range(2):
                    q = slice(S * half, S * half + S)
                    own = probs[q, :, :, S * half:S * half + S].rearrange("p h t k -> p (h t) k")
                    dve.tensor_tensor(own, sc[q, :, :, :].rearrange("p h t k -> p (h t) k"),
                                      rinv[q, :, :].rearrange("p h t -> p (h t)").unsqueeze(2).to_broadcast([S, HG * NT, S]),
                                      ALU.mult).then_inc(probs_ready, 1)
                for t in range(1, NT):
                    values(g, 0, t)

            def turned_low(g, h):
                dve.wait_ge(pT_hi_ready, g * HG + h + 1)
                dve.tensor_tensor(pT_lo[:, h % 2, :], ps_s[:, h, :], as_f32(pT_hi[:, h % 2, :]),
                                  ALU.subtract).then_inc(pT_ready, 1)

            def output_low(g, n):
                dve.wait_ge(o_hi_ready, g * parts * n_o + n + 1)
                k, rows = (n % n_o, slice(0, P)) if dv >= P else (0, slice(dv * n, dv * n + dv))
                dve.tensor_tensor(o_lo[rows, k, :], ps_o[rows, n % 2, :], as_f32(o_hi[rows, k, :]),
                                  ALU.subtract).then_inc(o_ready, 1)

            def add_y(g, part, t):
                dve.wait_ge(y_done, uses(g, part, t + 1))
                dve.wait_ge(y_added, uses(g, part))
                dve.tensor_tensor(y[:, t, :], y[:, t, :], ps_p[:, t % 2, :], ALU.add).then_inc(y_added, 1)

            def group(g, last):
                if parts == 1:
                    output_low(g, 0)
                    turned_low(g, 2)
                    output_low(g, 1)
                    turned_low(g, 3)
                    if not last:
                        query_key(g + 1, 0)
                        query_key(g + 1, 1)
                    output_low(g, 2)
                    output_low(g, 3)
                else:
                    for n in range(n_o):
                        output_low(g, n)
                    for t in range(NT):
                        values(g, 1, t)
                    for t in range(NT):
                        add_y(g, 0, t)
                    turned_low(g, 2)
                    turned_low(g, 3)
                    if not last:
                        query_key(g + 1, 0)
                        query_key(g + 1, 1)
                    for n in range(n_o, 2 * n_o):
                        output_low(g, n)
                if not last:
                    softmax_and_values(g + 1)
                for t in range(NT):
                    if t == 2 and not last:
                        turned_low(g + 1, 0)
                        turned_low(g + 1, 1)
                    add_y(g, parts - 1, t)

            dve.wait_ge(start_loaded, 16)
            dve.wait_ge(zero_ready, 1)
            query_key(0, 0)
            query_key(0, 1)
            softmax_and_values(0)
            turned_low(0, 0)
            turned_low(0, 1)
            dve.wait_ge(y_loaded, 16 * NT)
            with dve.Fori(0, NG - 1) as g:
                group(g, False)
            group(NG - 1, True)
            dve.wait_ge(y_added, uses(NG, 0))
            for t in range(NT):
                if rectified:
                    dve.scalar_tensor_tensor(out=y[:, t, :], in0=y[:, t, :], scalar=0.01, in1=y[:, t, :],
                                             op0=ALU.mult, op1=ALU.max).then_inc(x_ready, 1)
                    dve.tensor_tensor(x[:, t, :], x[:, t, :], xn[:, t, :], ALU.add).then_inc(x_ready, 1)
                    dve.wait_ge(x_ready, 3 * t + 2)
                    dve.tensor_tensor(x[:, t, :], x[:, t, :], y[:, t, :], ALU.add).then_inc(x_ready, 1)
                else:
                    dve.tensor_tensor(x[:, t, :], x[:, t, :], y[:, t, :], ALU.add).then_inc(x_ready, 1)

        @block.tensor
        def _(pe):

            def query_key(g, first):
                pe.wait_ge(wqk_ready, g + 1)
                for i in range(2):
                    if not first:
                        if parts == 2:
                            pe.wait_ge(y_added, uses(g - 1, 0, i + 3))
                        else:
                            pe.wait_ge(y_added, uses(g - 1, 0))
                            pe.wait_ge(v_added, uses(g, 0))
                    for k in range(KT):
                        cols = slice(P * i, P * i + P)
                        for n, (w, a) in enumerate(three(qk_hi[:, k, cols], qk_lo[:, k, cols], xT_hi[:, k, :], xT_lo[:, k, :])):
                            mm = pe.matmul(ps_p[:, i, :], w, a, start=(k == 0 and n == 0), stop=(k == KT - 1 and n == 2))
                    mm.then_inc(qk_done, 1)

            def scores(g):
                pe.wait_ge(qk_ready if rectified else qk_added, 2 * g + 2)
                pe.wait_ge(pT_ready, g * HG)
                for t in range(NT):
                    for half in range(2):
                        for h in range(HG):
                            r = slice(DH * h, DH * h + DH)
                            tok = slice(t * P + half * S, t * P + half * S + S)
                            mm = pe.matmul(ps_s[half * S:half * S + S, h, t * S:t * S + S], qk[r, 0, tok], qk[r, 1, tok],
                                           start=True, stop=True)
                mm.then_inc(scores_done, 1)

            def values(g, part):
                pe.wait_ge(wv_ready, g * parts + part + 1)
                for t in range(NT):
                    if t >= 2:
                        pe.wait_ge(v_added, uses(g, part, t - 1))
                    elif part:
                        pe.wait_ge(y_added, uses(g, 0))
                        pe.wait_ge(v_added, uses(g, 1))
                    for k in range(KT):
                        tok = slice(t * P, t * P + P)
                        for n, (a, w) in enumerate(three(xT_hi[:, k, tok], xT_lo[:, k, tok], wv_hi[:, k, :], wv_lo[:, k, :])):
                            mm = pe.matmul(ps_p[:, t % 2, 0:vc], a, w, start=(k == 0 and n == 0), stop=(k == KT - 1 and n == 2))
                    mm.then_inc(v_done, 1)

            def turn(g, h):
                if h % hp == 0:
                    pe.wait_ge(probs_ready, 2 * (g + 1))
                for t in range(NT):
                    mm = pe.transpose(ps_s[:, h, t * P:(t + 1) * P], probs[:, h, t, :], ident[:, :])
                mm.then_inc(turned, 1)

            def outputs(g, h):
                part = h // hp
                pe.wait_ge(pT_ready, g * HG + h + 1)
                for c in range(kc):
                    n = h * kc + c
                    pe.wait_ge(o_ready, g * parts * n_o + max(0, n - 1))
                    v0 = (h - part * hp) * dv + c * P if dv >= P else 0
                    for t in range(NT):
                        if h % hp == 0 and c == 0:
                            pe.wait_ge(v_ready, uses(g, part, t + 1))
                        tok = slice(t * P, t * P + P)
                        for i, (v, p) in enumerate(three(v_hi[:, t, v0:v0 + P], v_lo[:, t, v0:v0 + P],
                                                         pT_hi[:, h % 2, tok], pT_lo[:, h % 2, tok])):
                            mm = pe.matmul(ps_o[:, n % 2, tok], v, p, start=(i == 0), stop=(i == 2))
                    mm.then_inc(o_done, 1)

            def project(g, part, t, last):
                if t == 0:
                    pe.wait_ge(wo_ready, g * parts + part + 1)
                    pe.wait_ge(o_ready, (g * parts + part + 1) * n_o)
                if t >= 2:
                    pe.wait_ge(y_added, uses(g, part, t - 1))
                elif part < parts - 1:
                    pe.wait_ge(v_added, uses(g, part + 1, t + 3))
                elif last:
                    pe.wait_ge(y_added, uses(g, part))
                else:
                    pe.wait_ge(v_added, uses(g + 1, 0, t + 3))
                for k in range(ko):
                    tok = slice(t * P, t * P + P)
                    for n, (o, w) in enumerate(three(o_hi[:, k, tok], o_lo[:, k, tok], wo_hi[:, k, :], wo_lo[:, k, :])):
                        mm = pe.matmul(ps_p[:, t % 2, :], o, w, start=(k == 0 and n == 0), stop=(k == ko - 1 and n == 2))
                mm.then_inc(y_done, 1)

            def group(g, last):
                if parts == 1:
                    outputs(g, 0)
                    turn(g, 2)
                    outputs(g, 1)
                    turn(g, 3)
                else:
                    outputs(g, 0)
                    outputs(g, 1)
                    values(g, 1)
                    for t in range(NT):
                        project(g, 0, t, last)
                    turn(g, 2)
                    turn(g, 3)
                if not last:
                    query_key(g + 1, False)
                outputs(g, 2)
                outputs(g, 3)
                if not last:
                    scores(g + 1)
                    values(g + 1, 0)
                for t in range(NT):
                    if t == 2 and not last:
                        turn(g + 1, 0)
                        turn(g + 1, 1)
                    project(g, parts - 1, t, last)

            query_key(0, True)
            scores(0)
            values(0, 0)
            turn(0, 0)
            turn(0, 1)
            with pe.Fori(0, NG - 1) as g:
                group(g, False)
            group(NG - 1, True)




def experts(nc, stage, norm, x, xT_hi, xT_lo, ident, before, gate, w1, w3, w2, b1, b3, b2):
    NR = NE - 1
    with ExitStack() as ctx:
        m = Memory(nc, ctx, stage)
        raw = [m.sb(f"raw{i}", [P, KT, D]) for i in range(3)]
        w_hi = [m.sb(f"w_hi{i}", [P, KT, D], F32R) for i in range(3)]
        w_lo = [m.sb(f"w_lo{i}", [P, KT, D], F32R) for i in range(3)]
        b1_sb, b3_sb, b2_sb = m.sb("b1", [P, NE, KT]), m.sb("b3", [P, NE, KT]), m.sb("b2", [NE, D])
        gate_sb = m.sb("gate", [P, KT, NR])
        gate_hi, gate_lo = m.sb("gate_hi", [P, KT, NR], F32R), m.sb("gate_lo", [P, KT, NR], F32R)
        before_sb = m.sb("before", [P, NR, NR])
        lg, pr = m.sb("lg", [P, NT, NR]), m.sb("pr", [P, NT, NR])
        rmax, rsum, rinv = m.sb("rmax", [P, NT]), m.sb("rsum", [P, NT]), m.sb("rinv", [P, NT])
        beats, ties = m.sb("beats", [P, NT, NR, NR]), m.sb("ties", [P, NT, NR, NR])
        rank, chosen = m.sb("rank", [P, NT, NR]), m.sb("chosen", [P, NT, NR])
        weight = m.sb("weight", [P, NE, NT])
        weightT = m.sb("weightT", [NE, TOK])
        gated = m.sb("gated", [P, 2, TOK])
        h32 = m.sb("h32", [P, KT, TOK])
        h_hi, h_lo = m.sb("h_hi", [P, KT, TOK], F32R), m.sb("h_lo", [P, KT, TOK], F32R)

        small_loaded, gate_hi_ready, gate_ready, logits_done, router, weight_ready = (m.sem(n) for n in (
            "small_loaded", "gate_hi_ready", "gate_ready", "logits_done", "router", "weight_ready"))
        router_exp, weight_turned, weightT_ready, bias_done = (m.sem(n) for n in ("router_exp", "weight_turned", "weightT_ready", "bias_done"))
        loaded, hi_ready, lo_ready = m.sems("loaded", 3), m.sems("hi_ready", 3), m.sems("lo_ready", 3)
        up_done, down_done = m.sem("up_done"), m.sem("down_done")
        gated_ready, h_ready, h_hi_ready, h_lo_ready = (m.sem(n) for n in ("gated_ready", "h_ready", "h_hi_ready", "h_lo_ready"))
        bias_added, x_ready = m.sem("bias_added"), m.sem("x_ready")
        weights = (w1, w3, w2)

        def load(sp, e, i):
            sp.dma_start(raw[i][:, :, :], weights[i][e]).then_inc(loaded[i], 16)

        def prefetch(sp):
            for to, of in ((gate_sb[:, :, :], gate), (before_sb[:, :, :], before.to_broadcast([P, NR * NR]).rearrange("p (a b) -> p a b", b=NR)),
                           (b1_sb[:, :, :], b1), (b3_sb[:, :, :], b3), (b2_sb[:, :], b2)):
                sp.dma_start(to, of).then_inc(small_loaded, 16)
            for i in range(3):
                load(sp, 0, i)

        norm(prefetch)
        ps_1, ps_3, ps_y = m.pb("ps_1", [P, 2, TOK]), m.pb("ps_3", [P, 2, TOK]), m.pb("ps_y", [P, 2, D])
        ps_g = m.pb("ps_g", [P, NT, NR])
        ps_w = m.pb("ps_w", [NE, TOK])
        block = ctx.enter_context(nc.Block())

        @block.sync
        def _(sp):
            with sp.Fori(0, NE - 1) as e:
                for i in range(3):
                    sp.wait_ge(lo_ready[i], e + 1)
                    load(sp, e + 1, i)

        @block.scalar
        def _(act):
            act.wait_ge(small_loaded, 16 * 5)
            act.activation(gate_hi[:, :, :], gate_sb[:, :, :], ACT.Copy).then_inc(gate_hi_ready, 1)
            act.wait_ge(router, 2)
            act.activation(pr[:, :, :], lg[:, :, :], ACT.Exp).then_inc(router_exp, 1)

            def split(e, i):
                act.wait_ge(loaded[i], 16 * (e + 1))
                if i < 2:
                    act.wait_ge(up_done, KT * e)
                else:
                    act.wait_ge(down_done, NT * e)
                act.activation(w_hi[i][:, :, :], raw[i][:, :, :], ACT.Copy).then_inc(hi_ready[i], 1)

            def gate_slice(e, k):
                act.wait_ge(up_done, KT * e + k + 1)
                act.wait_ge(h_ready, KT * e + max(0, k - 1))
                act.activation(gated[:, k % 2, :], ps_1[:, k % 2, :], ACT.Silu,
                               bias=b1_sb[:, e, k:k + 1]).then_inc(gated_ready, 1)

            def high_slice(e, k):
                act.wait_ge(h_ready, KT * e + k + 1)
                act.wait_ge(down_done, NT * e)
                act.activation(h_hi[:, k, :], h32[:, k, :], ACT.Copy).then_inc(h_hi_ready, 1)

            with act.Fori(0, NE) as e:
                split(e, 0)
                split(e, 1)
                gate_slice(e, 0)
                split(e, 2)
                for k in range(1, KT):
                    gate_slice(e, k)
                    high_slice(e, k - 1)
                high_slice(e, KT - 1)

        @block.gpsimd
        def _(pool):
            with pool.Fori(0, NE) as e:
                for i in range(3):
                    pool.wait_ge(hi_ready[i], e + 1)
                    pool.tensor_tensor(w_lo[i][:, :, :], raw[i][:, :, :], as_f32(w_hi[i][:, :, :]),
                                       ALU.subtract).then_inc(lo_ready[i], 1)
                for k in range(KT):
                    pool.wait_ge(h_hi_ready, KT * e + k + 1)
                    pool.tensor_tensor(h_lo[:, k, :], h32[:, k, :], as_f32(h_hi[:, k, :]), ALU.subtract).then_inc(h_lo_ready, 1)

        @block.vector
        def _(dve):
            steps = [0]

            def step(ins):
                ins.then_inc(router, 1)
                steps[0] += 1
                dve.wait_ge(router, steps[0])

            def each(ap):
                return ap.unsqueeze(2).to_broadcast([P, NT, NR])

            dve.wait_ge(gate_hi_ready, 1)
            dve.tensor_tensor(gate_lo[:, :, :], gate_sb[:, :, :], as_f32(gate_hi[:, :, :]), ALU.subtract).then_inc(gate_ready, 1)
            dve.wait_ge(small_loaded, 16 * 5)
            dve.wait_ge(logits_done, 1)
            step(dve.tensor_reduce(rmax[:, :], ps_g[:, :, :], AX_X, ALU.max))
            step(dve.tensor_tensor(lg[:, :, :], ps_g[:, :, :], each(rmax[:, :]), ALU.subtract))
            dve.wait_ge(router_exp, 1)
            step(dve.tensor_reduce(rsum[:, :], pr[:, :, :], AX_X, ALU.add))
            step(dve.reciprocal(rinv[:, :], rsum[:, :]))
            step(dve.tensor_tensor(pr[:, :, :], pr[:, :, :], each(rinv[:, :]), ALU.mult))
            for t in range(NT):
                other = pr[:, t, :].unsqueeze(1).to_broadcast([P, NR, NR])
                own = pr[:, t, :].unsqueeze(2).to_broadcast([P, NR, NR])
                step(dve.tensor_tensor(beats[:, t, :, :], other, own, ALU.is_gt))
                step(dve.tensor_tensor(ties[:, t, :, :], other, own, ALU.is_equal))
                step(dve.tensor_tensor(ties[:, t, :, :], ties[:, t, :, :], before_sb[:, :, :], ALU.mult))
            step(dve.tensor_tensor(beats[:, :, :, :], beats[:, :, :, :], ties[:, :, :, :], ALU.add))
            step(dve.tensor_reduce(rank[:, :, :], beats[:, :, :, :], AX_X, ALU.add))
            step(dve.tensor_scalar(chosen[:, :, :], rank[:, :, :], 2.0, None, ALU.is_lt))
            step(dve.memset(weight[:, NR, :], 1.0))
            dve.tensor_tensor(weight[:, 0:NR, :].rearrange("p e t -> p t e"), pr[:, :, :], chosen[:, :, :],
                              ALU.mult).then_inc(weight_ready, 1)
            dve.wait_ge(weight_turned, 1)
            dve.tensor_copy(weightT[:, :], ps_w[:, :]).then_inc(weightT_ready, 1)

            for t in range(NT):
                dve.wait_ge(bias_done, t + 1)
                dve.tensor_tensor(x[:, t, :], x[:, t, :], ps_y[:, t % 2, :], ALU.add).then_inc(bias_added, 1)
            dve.wait_ge(bias_added, NT)
            with dve.Fori(0, NE) as e:
                for k in range(KT):
                    dve.wait_ge(gated_ready, KT * e + k + 1)
                    dve.wait_ge(h_lo_ready, KT * e)
                    dve.scalar_tensor_tensor(out=h32[:, k, :], in0=ps_3[:, k % 2, :], scalar=b3_sb[:, e, k:k + 1],
                                             in1=gated[:, k % 2, :], op0=ALU.add, op1=ALU.mult).then_inc(h_ready, 1)
                for t in range(NT):
                    dve.wait_ge(down_done, NT * e + t + 1)
                    dve.wait_ge(x_ready, NT * e)
                    dve.scalar_tensor_tensor(out=x[:, t, :], in0=ps_y[:, t % 2, :], scalar=weight[:, e, t:t + 1],
                                             in1=x[:, t, :], op0=ALU.mult, op1=ALU.add).then_inc(x_ready, 1)

        @block.tensor
        def _(pe):
            pe.wait_ge(gate_ready, 1)
            for t in range(NT):
                for k in range(KT):
                    tok = slice(t * P, t * P + P)
                    for n, (a, w) in enumerate(three(xT_hi[:, k, tok], xT_lo[:, k, tok], gate_hi[:, k, :], gate_lo[:, k, :])):
                        mm = pe.matmul(ps_g[:, t, :], a, w, start=(k == 0 and n == 0), stop=(k == KT - 1 and n == 2))
            mm.then_inc(logits_done, 1)
            pe.wait_ge(weight_ready, 1)
            for t in range(NT):
                mm = pe.transpose(ps_w[:, t * P:(t + 1) * P], weight[:, :, t], ident[:, :])
            mm.then_inc(weight_turned, 1)
            pe.wait_ge(weightT_ready, 1)
            for t in range(NT):
                if t >= 2:
                    pe.wait_ge(bias_added, t - 1)
                pe.matmul(ps_y[:, t % 2, :], weightT[:, t * P:(t + 1) * P], b2_sb[:, :], start=True, stop=True).then_inc(bias_done, 1)
            pe.wait_ge(bias_added, NT)
            with pe.Fori(0, NE) as e:
                for i in range(2):
                    pe.wait_ge(lo_ready[i], e + 1)
                for k in range(KT):
                    pe.wait_ge(h_ready, KT * e + max(0, k - 1))
                    cols = slice(P * k, P * k + P)
                    for i, ps in ((0, ps_1), (1, ps_3)):
                        for j in range(KT):
                            for n, (w, a) in enumerate(three(w_hi[i][:, j, cols], w_lo[i][:, j, cols], xT_hi[:, j, :], xT_lo[:, j, :])):
                                mm = pe.matmul(ps[:, k % 2, :], w, a, start=(j == 0 and n == 0), stop=(j == KT - 1 and n == 2))
                    mm.then_inc(up_done, 1)
                pe.wait_ge(lo_ready[2], e + 1)
                for t in range(NT):
                    pe.wait_ge(x_ready, NT * e + max(0, t - 1))
                    tok = slice(t * P, t * P + P)
                    for j in range(KT):
                        if t == 0:
                            pe.wait_ge(h_lo_ready, KT * e + j + 1)
                        for n, (a, w) in enumerate(three(h_hi[:, j, tok], h_lo[:, j, tok], w_hi[2][:, j, :], w_lo[2][:, j, :])):
                            mm = pe.matmul(ps_y[:, t % 2, :], a, w, start=(j == 0 and n == 0), stop=(j == KT - 1 and n == 2))
                    mm.then_inc(down_done, 1)


def project_queries(nc, stage, norm, q, xT_hi, xT_lo, weights, sources, wq_hi, wq_lo, biases):
    with ExitStack() as ctx:
        m = Memory(nc, ctx, stage)
        halves = [(wq_hi, wq_lo), *weights]
        raw = [m.sb(f"raw{i}", [P, KT, D]) for i in range(3)]
        loaded, hi_ready, lo_ready = m.sems("loaded", 3), m.sems("hi_ready", 3), m.sems("lo_ready", 3)
        bias_loaded, done, q_ready = m.sem("bias_loaded"), m.sem("done"), m.sem("q_ready")

        def prefetch(sp):
            for i in range(3):
                sp.dma_start(raw[i][:, :, :], sources[i]).then_inc(loaded[i], 16)
            for to, of in biases:
                sp.dma_start(to, of).then_inc(bias_loaded, 16)

        norm(prefetch)
        ps = m.pb("ps", [P, NG, TOK])
        block = ctx.enter_context(nc.Block())

        @block.scalar
        def _(act):
            for i, (hi, _) in enumerate(halves):
                act.wait_ge(loaded[i], 16)
                act.activation(hi[:, :, :], raw[i][:, :, :], ACT.Copy).then_inc(hi_ready[i], 1)

        @block.gpsimd
        def _(pool):
            pool.wait_ge(hi_ready[2], 1)
            pool.tensor_tensor(halves[2][1][:, :, :], raw[2][:, :, :], as_f32(halves[2][0][:, :, :]), ALU.subtract).then_inc(lo_ready[2], 1)

        @block.tensor
        def _(pe):
            pe.wait_ge(lo_ready[0], 1)
            for g in range(NG):
                for k in range(KT):
                    cols = slice(P * g, P * g + P)
                    for n, (w, a) in enumerate(three(wq_hi[:, k, cols], wq_lo[:, k, cols], xT_hi[:, k, :], xT_lo[:, k, :])):
                        mm = pe.matmul(ps[:, g, :], w, a, start=(k == 0 and n == 0), stop=(k == KT - 1 and n == 2))
                mm.then_inc(done, 1)

        @block.vector
        def _(dve):
            for i in range(2):
                dve.wait_ge(hi_ready[i], 1)
                dve.tensor_tensor(halves[i][1][:, :, :], raw[i][:, :, :], as_f32(halves[i][0][:, :, :]), ALU.subtract).then_inc(lo_ready[i], 1)
            dve.wait_ge(bias_loaded, 16 * len(biases))
            for g in range(NG):
                dve.wait_ge(done, g + 1)
                dve.tensor_scalar(q[:, g, :], ps[:, g, :], biases[0][0][:, g:g + 1], 1.0 / sqrt(DH), ALU.add, ALU.mult).then_inc(q_ready, 1)


def masked_context_attention(nc, stage, q, ident, wk, wv, bk, bv, ctxT, mask, gain):
    with ExitStack() as ctx:
        m = Memory(nc, ctx, stage)
        (wk_hi, wk_lo), (wv_hi, wv_lo) = wk, wv
        HV = 2
        VC = D // HV
        VSLOTS = 3
        RING = 4
        raw_T = m.sb("raw_T", [P, 2, KT, CHW[0]])
        T_hi, T_lo = m.sb("T_hi", [P, KT, S2P], F32R), m.sb("T_lo", [P, KT, S2P], F32R)
        k_hi, k_lo = m.sb("k_hi", [P, S2P], F32R), m.sb("k_lo", [P, S2P], F32R)
        v_sum = m.sb("v_sum", [P, VSLOTS, VC])
        v_pair = m.sb("v_pair", [P, NJ, 4, P], F32R)
        qb_hi, qb_lo = m.sb("qb_hi", [P, NG, P], F32R), m.sb("qb_lo", [P, NG, P], F32R)
        pr = m.sb("pr", [P, 2, S2])
        mask_sb = m.sb("mask", [P, S2], I32)
        neg = m.sb("neg", [P, S2])
        gn = m.sb("gn", [P, S2])
        cmax = m.sb("cmax", [P, 2, 4])
        rmax, nmax, rsum, rinv = m.sb("rmax", [P, 2]), m.sb("nmax", [P, 2]), m.sb("rsum", [P, 2]), m.sb("rinv", [P, 2])
        pT = m.sb("pT", [P, RING, 4, 2 * P], F32R)
        o_low = m.sb("o_low", [S, 2, S])
        o_part = m.sb("o_part", [S, 2, S])
        ps_p = m.pb("ps_p", [P, 3, 512])
        ps_r = m.pb("ps_r", [P, RING, 512])
        ps_o = m.pb("ps_o", [P, 2, 2 * P])

        n_p = NG * 4 + HV * NJ
        assert n_p % 3 == 0
        T_loaded, T_hi_ready, T_split = m.sems("T_loaded", 2), m.sem("T_hi_ready"), m.sems("T_split", 4)
        mask_loaded, gain_loaded, neg_ready = m.sem("mask_loaded"), m.sem("gain_loaded"), m.sem("neg_ready")
        zero_ready, qb_hi_ready, qb_ready = m.sem("zero_ready"), m.sem("qb_hi_ready"), m.sem("qb_ready")
        proj_done, proj_free, k_hi_ready = m.sem("proj_done"), m.sems("proj_free", 3), m.sem("k_hi_ready")
        v_hi_ready, v_ready = m.sem("v_hi_ready"), m.sem("v_ready")
        scores_done, masked, rmax_ready, nmax_ready, exp_ready, rinv_ready, share_ready = (
            m.sems(n, 2) for n in ("scores_done", "masked", "rmax_ready", "nmax_ready", "exp_ready", "rinv_ready", "share_ready"))
        turned, pT_hi_ready, pT_ready, pT_used = m.sem("turned"), m.sem("pT_hi_ready"), m.sem("pT_ready"), m.sem("pT_used")
        o_low_ready, o_part_ready, att_ready = (m.sem(n) for n in ("o_low_ready", "o_part_ready", "att_ready"))
        waited = m.sems("waited", 3)
        block = ctx.enter_context(nc.Block())

        order = [("k", 0, c) for c in range(4)] + [("v", 0, j) for j in range(NJ)]
        order += [("k", g, c) for g in range(1, NG) for c in range(4)] + [("v", 1, j) for j in range(NJ)]
        use_of = {what: n for n, what in enumerate(order)}
        last_of = [(CH0[c] + CHV[c] - 1) // P for c in range(4)]

        def freed(b, u):
            return b * (n_p // 3) + u // 3 + 1

        def tiles(n):
            j0, j1 = JG[n % 4]
            return j0, j1, JR[j0]

        def chunk(c):
            return slice(CH0[c], CH0[c] + CHW[c])

        @block.sync
        def _(sp):
            def load_T(b, c):
                sp.dma_start(raw_T[:, c % 2, :, 0:CHW[c]], ctxT[b, :, :, chunk(c)]).then_inc(T_loaded[c % 2], 16)

            def load_mask(b):
                sp.dma_start(mask_sb[0:S, :], mask[b]).then_inc(mask_loaded, 16)
                sp.dma_start(mask_sb[S:P, :], mask[b]).then_inc(mask_loaded, 16)

            def load_gain(b):
                sp.dma_start(gn[0:S, :], gain[b]).then_inc(gain_loaded, 16)
                sp.dma_start(gn[S:P, :], gain[b]).then_inc(gain_loaded, 16)

            for c in range(4):
                if c == 2:
                    load_mask(0)
                if c >= 2:
                    sp.wait_ge(T_split[c - 2], 1)
                load_T(0, c)
            load_gain(0)
            with sp.Fori(0, B - 1) as b:
                for c in range(4):
                    if c == 2:
                        sp.wait_ge(neg_ready, b + 1)
                        load_mask(b + 1)
                    sp.wait_ge(T_split[(c + 2) % 4], b + 1 + c // 2)
                    load_T(b + 1, c)
                for i in range(2):
                    sp.wait_ge(share_ready[i], NG * (b + 1))
                load_gain(b + 1)

        @block.scalar
        def _(act):
            def split_T(b, c):
                act.wait_ge(T_loaded[c % 2], 16 * (2 * b + c // 2 + 1))
                act.activation(T_hi[:, :, chunk(c)], raw_T[:, c % 2, :, 0:CHW[c]], ACT.Copy).then_inc(T_hi_ready, 1)

            def queries_high(b):
                for i in range(2):
                    act.wait_ge(scores_done[i], 4 * NG * b)
                for h in range(HG):
                    rows, cols = slice(DH * h, DH * h + DH), slice(S * (h % 2), S * (h % 2) + S)
                    if h == 0:
                        act.sem_inc(waited[0], 1)
                    act.activation(qb_hi[rows, :, cols], q[rows, :, bass.ts(b, S)], ACT.Copy).then_inc(qb_hi_ready, 1)

            def keys_high(b, g, c):
                u = use_of["k", g, c]
                for i in range(2):
                    act.wait_ge(scores_done[i], 4 * (NG * b + g))
                act.wait_ge(proj_done, n_p * b + u + 1)
                act.activation(k_hi[:, chunk(c)], ps_p[:, u % 3, 0:CHW[c]], ACT.Identity,
                               bias=bk[:, g:g + 1]).then_inc(k_hi_ready, 1)

            def values_high(b, half, j):
                u, r = use_of["v", half, j], JR[j]
                if j == 0:
                    act.wait_ge(pT_used, 32 * b + 16 * half)
                act.wait_ge(proj_free[u % 3], freed(b, u))
                act.activation(v_pair[0:r, j, :, 0:S], v_sum[0:r, j % VSLOTS, :].rearrange("p (a c) -> p a c", c=S),
                               ACT.Copy).then_inc(v_hi_ready, 1)

            def exps(b, g):
                for i in range(2):
                    act.wait_ge(nmax_ready[i], NG * b + g + 1)
                    act.activation(pr[:, i, :], pr[:, i, :], ACT.Exp, bias=nmax[:, i:i + 1],
                                   accum_out=rsum[:, i:i + 1]).then_inc(exp_ready[i], 1)

            def turned_high(b, g):
                for n in range(8):
                    j0, j1, r = tiles(n)
                    act.wait_ge(turned, 32 * b + 8 * g + n + 1)
                    act.wait_ge(pT_used, 32 * b + 8 * g + max(0, n - RING + 1))
                    act.activation(pT[0:r, n % RING, 0:j1 - j0, 0:P],
                                   ps_r[0:r, n % RING, 0:(j1 - j0) * P].rearrange("p (j c) -> p j c", c=P),
                                   ACT.Copy).then_inc(pT_hi_ready, 1)

            def out_low(b, g):
                act.wait_ge(pT_used, 32 * b + 8 * (g + 1))
                for h in range(2):
                    rows = slice(DH * h, DH * h + DH)
                    act.activation(o_low[rows, :, :], ps_o[S + DH * h:S + DH * h + DH, :, S * h:S * h + S],
                                   ACT.Copy).then_inc(o_low_ready, 1)

            def batch(b, last):
                exps(b, 0)
                for j in range(NJ):
                    values_high(b, 0, j)
                for c in range(4):
                    keys_high(b, 1, c)
                turned_high(b, 0)
                out_low(b, 0)
                for g in (1, 2):
                    exps(b, g)
                    for c in range(4):
                        keys_high(b, g + 1, c)
                    if g == 2:
                        for j in range(NJ):
                            values_high(b, 1, j)
                            if j in last_of[:3] and not last:
                                act.wait_ge(proj_done, n_p * b + use_of["v", 1, j] + 1)
                                split_T(b + 1, last_of.index(j))
                    turned_high(b, g)
                    out_low(b, g)
                if not last:
                    act.wait_ge(proj_done, n_p * (b + 1))
                    split_T(b + 1, 3)
                exps(b, 3)
                if not last:
                    for c in range(4):
                        keys_high(b + 1, 0, c)
                        if c == 1:
                            queries_high(b + 1)
                turned_high(b, 3)
                out_low(b, 3)

            act.wait_ge(zero_ready, 2)
            for c in range(4):
                split_T(0, c)
            queries_high(0)
            for c in range(4):
                keys_high(0, 0, c)
            with act.Fori(0, B - 1) as b:
                batch(b, False)
            batch(B - 1, True)

        @block.gpsimd
        def _(pool):
            def added_mask(b):
                for i in range(2):
                    pool.wait_ge(masked[i], 4 * NG * b)
                pool.wait_ge(mask_loaded, 32 * (b + 1))
                pool.wait_ge(v_ready, 2 * NJ * b)
                pool.sem_inc(waited[1], 1)
                pool.tensor_scalar(neg[:, :], mask_sb[:, :], -1.0, 1.0e9, ALU.add, ALU.mult).then_inc(neg_ready, 1)

            def queries_low(b):
                pool.wait_ge(qb_hi_ready, HG * (b + 1))
                pool.wait_ge(neg_ready, b + 1)
                for h in range(HG):
                    rows, cols = slice(DH * h, DH * h + DH), slice(S * (h % 2), S * (h % 2) + S)
                    if h:
                        pool.wait_ge(qb_ready, HG * b + h)
                    pool.sem_inc(waited[1], 1)
                    pool.tensor_tensor(qb_lo[rows, :, cols], q[rows, :, bass.ts(b, S)], as_f32(qb_hi[rows, :, cols]),
                                       ALU.subtract).then_inc(qb_ready, 1)

            def values_low(b, half):
                if half == 0:
                    pool.wait_ge(qb_ready, HG * (b + 1))
                for j in range(NJ):
                    r = JR[j]
                    pool.wait_ge(v_hi_ready, 2 * NJ * b + NJ * half + j + 1)
                    pool.tensor_tensor(v_pair[0:r, j, :, S:P], v_sum[0:r, j % VSLOTS, :].rearrange("p (a c) -> p a c", c=S),
                                       as_f32(v_pair[0:r, j, :, 0:S]), ALU.subtract).then_inc(v_ready, 1)

            pool.memset(as_f32(qb_hi[:, :, :]), 0.0).then_inc(zero_ready, 1)
            pool.memset(as_f32(qb_lo[:, :, :]), 0.0).then_inc(zero_ready, 1)
            pool.wait_ge(zero_ready, 2)
            def split_T(b):
                for c in range(2, 4):
                    pool.wait_ge(T_hi_ready, 4 * b + c + 1)
                    pool.tensor_tensor(T_lo[:, :, chunk(c)], raw_T[:, c % 2, :, 0:CHW[c]], as_f32(T_hi[:, :, chunk(c)]),
                                       ALU.subtract).then_inc(T_split[c], 1)

            def batch(b, last):
                added_mask(b)
                queries_low(b)
                values_low(b, 0)
                values_low(b, 1)
                if not last:
                    split_T(b + 1)

            split_T(0)
            with pool.Fori(0, B - 1) as b:
                batch(b, False)
            batch(B - 1, True)

        @block.vector
        def _(dve):
            def split_T(b, c):
                dve.wait_ge(T_hi_ready, 4 * b + c + 1)
                dve.tensor_tensor(T_lo[:, :, chunk(c)], raw_T[:, c % 2, :, 0:CHW[c]], as_f32(T_hi[:, :, chunk(c)]),
                                  ALU.subtract).then_inc(T_split[c], 1)

            def keys_low(b, g, c):
                u = use_of["k", g, c]
                dve.wait_ge(k_hi_ready, 4 * (NG * b + g) + c + 1)
                dve.scalar_tensor_tensor(out=k_lo[:, chunk(c)], in0=ps_p[:, u % 3, 0:CHW[c]], scalar=bk[:, g:g + 1],
                                         in1=as_f32(k_hi[:, chunk(c)]), op0=ALU.add, op1=ALU.subtract).then_inc(proj_free[u % 3], 1)

            def values(b, half, j):
                u, r = use_of["v", half, j], JR[j]
                dve.wait_ge(proj_done, n_p * b + u + 1)
                dve.wait_ge(v_ready, 2 * NJ * b + NJ * half + max(0, j - VSLOTS + 1))
                dve.tensor_tensor(v_sum[0:r, j % VSLOTS, :], ps_p[0:r, u % 3, 0:VC], bv[0:r, VC * half:VC * half + VC],
                                  ALU.add).then_inc(proj_free[u % 3], 1)

            def mask_scores(b, g):
                dve.wait_ge(neg_ready, b + 1)
                dve.wait_ge(turned, 32 * b + 8 * g)
                for c in range(4):
                    for i in range(2):
                        cols = slice(CH0[c], CH0[c] + CHV[c])
                        dve.wait_ge(scores_done[i], 4 * (NG * b + g) + c + 1)
                        dve.sem_inc(waited[2], 1)
                        dve.tensor_tensor_reduce(pr[:, i, cols], ps_r[:, (2 * c + i) % RING, 0:CHV[c]], neg[:, cols],
                                                 1.0, LOW, ALU.add, ALU.max, cmax[:, i, c:c + 1]).then_inc(masked[i], 1)
                for i in range(2):
                    dve.wait_ge(masked[i], 4 * (NG * b + g + 1))
                    dve.tensor_reduce(rmax[:, i:i + 1], cmax[:, i, :], AX_X, ALU.max).then_inc(rmax_ready[i], 1)
                for i in range(2):
                    dve.wait_ge(rmax_ready[i], NG * b + g + 1)
                    dve.tensor_scalar(nmax[:, i:i + 1], rmax[:, i:i + 1], -1.0, None, ALU.mult).then_inc(nmax_ready[i], 1)

            def shares(b, g, i):
                dve.wait_ge(exp_ready[i], NG * b + g + 1)
                dve.reciprocal(rinv[:, i:i + 1], rsum[:, i:i + 1]).then_inc(rinv_ready[i], 1)
                dve.wait_ge(gain_loaded, 32 * (b + 1))
                dve.wait_ge(rinv_ready[i], NG * b + g + 1)
                dve.scalar_tensor_tensor(out=pr[:, i, :], in0=pr[:, i, :], scalar=rinv[:, i:i + 1],
                                         in1=gn[:, :], op0=ALU.mult, op1=ALU.mult).then_inc(share_ready[i], 1)

            def turned_low(b, g):
                for n in range(8):
                    j0, j1, r = tiles(n)
                    dve.wait_ge(pT_hi_ready, 32 * b + 8 * g + n + 1)
                    dve.tensor_tensor(pT[0:r, n % RING, 0:j1 - j0, P:2 * P],
                                      ps_r[0:r, n % RING, 0:(j1 - j0) * P].rearrange("p (j c) -> p j c", c=P),
                                      as_f32(pT[0:r, n % RING, 0:j1 - j0, 0:P]), ALU.subtract).then_inc(pT_ready, 1)

            def outputs(b, g):
                n = NG * b + g
                dve.wait_ge(o_low_ready, 2 * n + 2)
                for h in range(2):
                    rows, own = slice(DH * h, DH * h + DH), slice(S * h, S * h + S)
                    dve.tensor_tensor(o_part[rows, :, :], ps_o[rows, :, own], o_low[rows, :, :], ALU.add).then_inc(o_part_ready, 1)
                dve.wait_ge(o_part_ready, 2 * n + 2)
                for i in range(2):
                    for h in range(2):
                        rows = slice(DH * h, DH * h + DH)
                        to = slice(S * i + DH * h, S * i + DH * h + DH)
                        dve.tensor_tensor(q[to, g, bass.ts(b, S)], ps_o[rows, i, P + S * h:P + S * h + S],
                                          o_part[rows, i, :], ALU.add).then_inc(att_ready, 1)

            def shares_and_keys(b, g, next_b, next_g):
                shares(b, g, 0)
                keys_low(next_b, next_g, 0)
                shares(b, g, 1)
                for c in range(1, 4):
                    keys_low(next_b, next_g, c)

            def batch(b, last):
                values(b, 0, 0)
                values(b, 0, 1)
                shares(b, 0, 0)
                values(b, 0, 2)
                shares(b, 0, 1)
                for j in range(3, NJ):
                    values(b, 0, j)
                for c in range(4):
                    keys_low(b, 1, c)
                turned_low(b, 0)
                mask_scores(b, 1)
                outputs(b, 0)
                for g in (1, 2):
                    shares_and_keys(b, g, b, g + 1)
                    if g == 2:
                        for j in range(NJ):
                            values(b, 1, j)
                            if j - 2 in last_of[:2] and not last:
                                split_T(b + 1, last_of.index(j - 2))
                    turned_low(b, g)
                    mask_scores(b, g + 1)
                    outputs(b, g)
                if last:
                    shares(b, 3, 0)
                    shares(b, 3, 1)
                    turned_low(b, 3)
                else:
                    shares_and_keys(b, 3, b + 1, 0)
                    turned_low(b, 3)
                    mask_scores(b + 1, 0)
                outputs(b, 3)

            for c in range(2):
                split_T(0, c)
            for c in range(4):
                keys_low(0, 0, c)
            mask_scores(0, 0)
            with dve.Fori(0, B - 1) as b:
                batch(b, False)
            batch(B - 1, True)

        @block.tensor
        def _(pe):
            def bank(b, u):
                pe.wait_ge(proj_free[u % 3], b * (n_p // 3) + u // 3)
                return ps_p[:, u % 3, :]

            def keys(b, g):
                for c in range(4):
                    full = bank(b, use_of["k", g, c])
                    if g == 0:
                        pe.wait_ge(T_split[c], b + 1)
                    for k in range(KT):
                        cols = slice(P * g, P * g + P)
                        for n, (a, t) in enumerate(three(wk_hi[:, k, cols], wk_lo[:, k, cols], T_hi[:, k, chunk(c)], T_lo[:, k, chunk(c)])):
                            mm = pe.matmul(full[:, 0:CHW[c]], a, t, start=(k == 0 and n == 0), stop=(k == KT - 1 and n == 2))
                    mm.then_inc(proj_done, 1)

            def values(b, half):
                for j in range(NJ):
                    full = bank(b, use_of["v", half, j])
                    r = JR[j]
                    for k in range(KT):
                        rows, cols = slice(P * j, P * j + r), slice(VC * half, VC * half + VC)
                        for n, (t, w) in enumerate(three(T_hi[:, k, rows], T_lo[:, k, rows], wv_hi[:, k, cols], wv_lo[:, k, cols])):
                            mm = pe.matmul(full[0:r, 0:VC], t, w, start=(k == 0 and n == 0), stop=(k == KT - 1 and n == 2))
                    mm.then_inc(proj_done, 1)

            def scores(b, g, c):
                if g == 0 and c == 0:
                    pe.wait_ge(qb_ready, HG * (b + 1))
                u = use_of["k", g, c]
                pe.wait_ge(proj_free[u % 3], freed(b, u))
                for i in range(2):
                    if 2 * c + i >= RING:
                        pe.wait_ge(masked[i], 4 * (NG * b + g) + c - RING // 2 + 1)
                    r = slice(S * i, S * i + S)
                    for n, (a, t) in enumerate(three(qb_hi[r, g, :], qb_lo[r, g, :], k_hi[r, chunk(c)], k_lo[r, chunk(c)])):
                        mm = pe.matmul(ps_r[:, (2 * c + i) % RING, 0:CHW[c]], a, t, start=(n == 0), stop=(n == 2))
                    mm.then_inc(scores_done[i], 1)

            def turn(b, g, n):
                j0, j1, r = tiles(n)
                if n >= RING:
                    pe.wait_ge(pT_ready, 32 * b + 8 * g + n - RING + 1)
                for j in range(j0, j1):
                    mm = pe.transpose(ps_r[0:r, n % RING, (j - j0) * P:(j - j0 + 1) * P], pr[:, n // 4, j * P:j * P + r], ident[:, :])
                mm.then_inc(turned, 1)

            def multiply(b, g, n):
                j0, j1, r = tiles(n)
                pe.wait_ge(pT_ready, 32 * b + 8 * g + n + 1)
                if n < 4:
                    pe.wait_ge(v_ready, 2 * NJ * b + NJ * (g // 2) + j1)
                for j in range(j0, j1):
                    mm = pe.matmul(ps_o[:, n // 4, :], v_pair[0:r, j, 2 * (g % 2) + n // 4, :], pT[0:r, n % RING, j - j0, :],
                                   start=(j == 0), stop=(j == NJ - 1))
                mm.then_inc(pT_used, 1)

            def outputs_and_scores(b, g, after):
                pe.wait_ge(att_ready, HG * (NG * b + g))
                for n in range(8):
                    if n % 4 == 0:
                        pe.wait_ge(share_ready[n // 4], NG * b + g + 1)
                    if n >= RING:
                        multiply(b, g, n - RING)
                    turn(b, g, n)
                multiply(b, g, 4)
                multiply(b, g, 5)
                if after:
                    scores(*after, 0)
                multiply(b, g, 6)
                multiply(b, g, 7)
                if after:
                    for c in range(1, 4):
                        scores(*after, c)

            keys(0, 0)
            for c in range(4):
                scores(0, 0, c)

            def batch(b, last):
                values(b, 0)
                keys(b, 1)
                outputs_and_scores(b, 0, (b, 1))
                keys(b, 2)
                outputs_and_scores(b, 1, (b, 2))
                keys(b, 3)
                values(b, 1)
                outputs_and_scores(b, 2, (b, 3))
                if not last:
                    keys(b + 1, 0)
                outputs_and_scores(b, 3, None if last else (b + 1, 0))

            with pe.Fori(0, B - 1) as b:
                batch(b, False)
            batch(B - 1, True)


def project_attended(nc, stage, x, att, weight, bias):
    with ExitStack() as ctx:
        m = Memory(nc, ctx, stage)
        a_hi, a_lo = m.sb("a_hi", [P, KT, TOK], F32R), m.sb("a_lo", [P, KT, TOK], F32R)
        raw, w_hi, w_lo = m.sb("raw", [P, KT, D]), m.sb("w_hi", [P, KT, D], F32R), m.sb("w_lo", [P, KT, D], F32R)
        bo = m.sb("bo", [P, D])
        ps = m.pb("ps", [P, NT, D])
        loaded, bo_loaded, a_hi_ready, a_lo_ready, w_hi_ready, w_lo_ready = m.sems("loaded", KT), *(m.sem(n) for n in (
            "bo_loaded", "a_hi_ready", "a_lo_ready", "w_hi_ready", "w_lo_ready"))
        done, bias_added, x_ready = m.sem("done"), m.sem("bias_added"), m.sem("x_ready")
        block = ctx.enter_context(nc.Block())

        @block.sync
        def _(sp):
            for k in range(KT):
                sp.dma_start(raw[:, k, :], weight[:, k, :]).then_inc(loaded[k], 16)
            sp.dma_start(bo[:, :], bias.to_broadcast([P, D])).then_inc(bo_loaded, 16)

        @block.scalar
        def _(act):
            for k in range(KT):
                act.activation(a_hi[:, k, :], att[:, k, :], ACT.Copy).then_inc(a_hi_ready, 1)
            for k in range(KT):
                act.wait_ge(loaded[k], 16)
                act.activation(w_hi[:, k, :], raw[:, k, :], ACT.Copy).then_inc(w_hi_ready, 1)

        @block.vector
        def _(dve):
            for k in range(KT):
                dve.wait_ge(a_hi_ready, k + 1)
                dve.tensor_tensor(a_lo[:, k, :], att[:, k, :], as_f32(a_hi[:, k, :]), ALU.subtract).then_inc(a_lo_ready, 1)
            for k in range(KT):
                dve.wait_ge(w_hi_ready, k + 1)
                dve.tensor_tensor(w_lo[:, k, :], raw[:, k, :], as_f32(w_hi[:, k, :]), ALU.subtract).then_inc(w_lo_ready, 1)
            dve.wait_ge(bo_loaded, 16)
            for t in range(NT):
                dve.tensor_tensor(x[:, t, :], x[:, t, :], bo[:, :], ALU.add).then_inc(bias_added, 1)
            for t in range(NT):
                dve.wait_ge(done, t + 1)
                dve.wait_ge(bias_added, t + 1)
                dve.tensor_tensor(x[:, t, :], x[:, t, :], ps[:, t, :], ALU.add).then_inc(x_ready, 1)

        @block.tensor
        def _(pe):
            pe.wait_ge(a_lo_ready, KT)
            for t in range(NT):
                tok = slice(t * P, t * P + P)
                for k in range(KT):
                    if t == 0:
                        pe.wait_ge(w_lo_ready, k + 1)
                    for n, (a, w) in enumerate(three(a_hi[:, k, tok], a_lo[:, k, tok], w_hi[:, k, :], w_lo[:, k, :])):
                        mm = pe.matmul(ps[:, t, :], a, w, start=(k == 0 and n == 0), stop=(k == KT - 1 and n == 2))
                mm.then_inc(done, 1)


def quantized_blocks(nc, stage, norm, x, h, hT_hi, hT_lo, ident, codes, scales, la, lb, bias, gamma, beta):
    RANK = 32
    NBK = 3
    GROUP = 16
    GP = P // GROUP
    with ExitStack() as ctx:
        m = Memory(nc, ctx, stage)
        code = m.sb("code", [P, 2, KT, D], I32)
        scale = m.sb("scale", [P, 2, KT, D])
        la_sb, lb_sb = m.sb("la", [RANK, 2, D]), m.sb("lb", [RANK, 2, D])
        w = m.sb("w", [P, 2, KT, D])
        w_hi, w_lo = m.sb("w_hi", [P, 2, KT, D], F32R), m.sb("w_lo", [P, 2, KT, D], F32R)
        bias_sb = m.sb("bias", [P, 2, D])
        gamma_sb, beta_sb = m.sb("gamma", [P, D]), m.sb("beta", [P, D])
        z = m.sb("z", [P, NT, D])
        zT_hi, zT_lo = m.sb("zT_hi", [P, KT, TOK], F32R), m.sb("zT_lo", [P, KT, TOK], F32R)
        stats, mv = m.sb("stats", [P, NT, 6]), m.sb("mv", [P, NT, 2])
        var, std, rstd = m.sb("var", [P, NT]), m.sb("std", [P, NT]), m.sb("rstd", [P, NT])
        loaded, rank_loaded, small_loaded = m.sems("loaded", 2), m.sems("rank_loaded", 2), m.sem("small_loaded")
        w_coded, w_scaled, rank_done, w_summed, w_hi_ready, w_ready = (m.sems(n, 2) for n in (
            "w_coded", "w_scaled", "rank_done", "w_summed", "w_hi_ready", "w_ready"))
        y_done, y_read = m.sems("y_done", 2), m.sems("y_read", 2)
        stats_ready, mv_ready, var_ready, std_ready, rstd_ready = (m.sem(n) for n in ("stats_ready", "mv_ready", "var_ready", "std_ready", "rstd_ready"))
        z_ready, z_scaled, z_shifted, gelu_ready = (m.sem(n) for n in ("z_ready", "z_scaled", "z_shifted", "gelu_ready"))
        turned, hi_ready, lo_ready = m.sems("turned", 2), m.sems("hi_ready", 2), m.sems("lo_ready", 2)
        waited = m.sem("waited")
        h_biased, x_ready = m.sem("h_biased"), m.sem("x_ready")

        def load(sp, b, first):
            for s in range(2):
                if not first:
                    sp.wait_ge(w_ready[s], b)
                sp.dma_start(code[:, s, :, :], codes[2 * b + s]).then_inc(loaded[s], 16)
                for k in range(KT):
                    rows = scales[2 * b + s, GP * k:GP * k + GP, :].unsqueeze(1).to_broadcast([GP, GROUP, D])
                    sp.dma_start(scale[:, s, k, :], rows).then_inc(loaded[s], 16)
                sp.dma_start(la_sb[:, s, :], la[2 * b + s]).then_inc(rank_loaded[s], 16)
                sp.dma_start(lb_sb[:, s, :], lb[2 * b + s]).then_inc(rank_loaded[s], 16)
                if s == 0:
                    if not first:
                        sp.wait_ge(y_read[1], NT * b)
                    for to, of in ((bias_sb[:, 0, :], bias[2 * b]), (bias_sb[:, 1, :], bias[2 * b + 1]),
                                   (gamma_sb[:, :], gamma[b]), (beta_sb[:, :], beta[b])):
                        sp.dma_start(to, of.to_broadcast([P, D])).then_inc(small_loaded, 16)

        norm(lambda sp: load(sp, 0, True))
        ps_l, ps_y, ps_t = m.pb("ps_l", [P, 2, D]), m.pb("ps_y", [P, 2, D]), m.pb("ps_t", [P, KT, TOK])
        block = ctx.enter_context(nc.Block())

        @block.sync
        def _(sp):
            with sp.Fori(0, NBK - 1) as b:
                load(sp, b + 1, False)

        @block.gpsimd
        def _(pool):
            def from_codes(b, s):
                pool.wait_ge(loaded[s], 16 * (KT + 1) * (b + 1))
                pool.wait_ge(w_ready[s], b)
                pool.sem_inc(waited, 1)
                pool.tensor_scalar(w[:, s, :, :], code[:, s, :, :], 1.0 / 7.5, -1.0, ALU.mult, ALU.add).then_inc(w_coded[s], 1)

            def low(b, s):
                pool.wait_ge(w_hi_ready[s], b + 1)
                pool.tensor_tensor(w_lo[:, s, :, :], w[:, s, :, :], as_f32(w_hi[:, s, :, :]), ALU.subtract).then_inc(w_ready[s], 1)

            with pool.Fori(0, NBK) as b:
                from_codes(b, 0)
                low(b, 0)
                from_codes(b, 1)
                low(b, 1)

        @block.scalar
        def _(act):
            def high(b, s):
                act.wait_ge(w_summed[s], KT * (b + 1))
                act.wait_ge(y_done[s], NT * b)
                act.activation(w_hi[:, s, :, :], w[:, s, :, :], ACT.Copy).then_inc(w_hi_ready[s], 1)

            def turned_high(b, s, to):
                for k in range(KT):
                    act.wait_ge(turned[s], KT * b + k + 1)
                    act.activation(to[:, k, :], ps_t[:, k, :], ACT.Copy).then_inc(hi_ready[s], 1)

            def blk(b, last):
                high(b, 0)
                high(b, 1)
                act.wait_ge(var_ready, b + 1)
                act.activation(std[:, :], var[:, :], ACT.Sqrt).then_inc(std_ready, 1)
                for t in range(NT):
                    act.wait_ge(z_shifted, NT * b + t + 1)
                    act.activation(z[:, t, :], z[:, t, :], ACT.Gelu).then_inc(gelu_ready, 1)
                turned_high(b, 0, zT_hi)
                if not last:
                    turned_high(b, 1, hT_hi)

            with act.Fori(0, NBK - 1) as b:
                blk(b, False)
            blk(NBK - 1, True)

        @block.vector
        def _(dve):
            def matrix(b, s):
                dve.wait_ge(w_coded[s], b + 1)
                dve.tensor_tensor(w[:, s, :, :], w[:, s, :, :], scale[:, s, :, :], ALU.mult).then_inc(w_scaled[s], 1)
                dve.wait_ge(w_scaled[s], b + 1)
                for k in range(KT):
                    dve.wait_ge(rank_done[s], KT * b + k + 1)
                    dve.tensor_tensor(w[:, s, k, :], w[:, s, k, :], ps_l[:, k % 2, :], ALU.add).then_inc(w_summed[s], 1)

            def turned_low(b, s, hi, lo):
                for k in range(KT):
                    dve.wait_ge(hi_ready[s], KT * b + k + 1)
                    dve.tensor_tensor(lo[:, k, :], ps_t[:, k, :], as_f32(hi[:, k, :]), ALU.subtract).then_inc(lo_ready[s], 1)

            def blk(b, last):
                matrix(b, 0)
                matrix(b, 1)
                dve.wait_ge(small_loaded, 64 * (b + 1))
                for t in range(NT):
                    dve.wait_ge(y_done[0], NT * b + t + 1)
                    dve.wait_ge(turned[0], KT * b)
                    dve.tensor_tensor(z[:, t, :], ps_y[:, t % 2, :], bias_sb[:, 0, :], ALU.add).then_inc(y_read[0], 1)
                    dve.wait_ge(y_read[0], NT * b + t + 1)
                    dve.bn_stats(stats[:, t, :], z[:, t, :]).then_inc(stats_ready, 1)
                dve.wait_ge(stats_ready, NT * (b + 1))
                for t in range(NT):
                    dve.tensor_tensor(h[:, t, :], h[:, t, :], bias_sb[:, 1, :], ALU.add).then_inc(h_biased, 1)
                for t in range(NT):
                    dve.bn_aggr(mv[:, t, :], stats[:, t, :]).then_inc(mv_ready, 1)
                dve.wait_ge(mv_ready, NT * (b + 1))
                dve.tensor_scalar(var[:, :], mv[:, :, 1], EPS, None, ALU.add).then_inc(var_ready, 1)
                dve.wait_ge(std_ready, b + 1)
                dve.reciprocal(rstd[:, :], std[:, :]).then_inc(rstd_ready, 1)
                dve.wait_ge(rstd_ready, b + 1)
                for t in range(NT):
                    dve.tensor_scalar(z[:, t, :], z[:, t, :], mv[:, t, 0:1], rstd[:, t:t + 1],
                                      ALU.subtract, ALU.mult).then_inc(z_ready, 1)
                    dve.wait_ge(z_ready, NT * b + t + 1)
                    dve.tensor_tensor(z[:, t, :], z[:, t, :], gamma_sb[:, :], ALU.mult).then_inc(z_scaled, 1)
                    dve.wait_ge(z_scaled, NT * b + t + 1)
                    dve.tensor_tensor(z[:, t, :], z[:, t, :], beta_sb[:, :], ALU.add).then_inc(z_shifted, 1)
                turned_low(b, 0, zT_hi, zT_lo)
                for t in range(NT):
                    dve.wait_ge(y_done[1], NT * b + t + 1)
                    dve.wait_ge(h_biased, NT * b + t + 1)
                    dve.tensor_tensor(h[:, t, :], h[:, t, :], ps_y[:, t % 2, :], ALU.add).then_inc(y_read[1], 1)
                if not last:
                    turned_low(b, 1, hT_hi, hT_lo)

            with dve.Fori(0, NBK - 1) as b:
                blk(b, False)
            blk(NBK - 1, True)
            dve.wait_ge(y_read[1], NT * NBK)
            for t in range(NT):
                dve.tensor_tensor(x[:, t, :], x[:, t, :], h[:, t, :], ALU.add).then_inc(x_ready, 1)

        @block.tensor
        def _(pe):
            def rank_product(b, s):
                pe.wait_ge(rank_loaded[s], 32 * (b + 1))
                for k in range(KT):
                    if k >= 2:
                        pe.wait_ge(w_summed[s], KT * b + k - 1)
                    elif s:
                        pe.wait_ge(w_summed[0], KT * (b + 1))
                    else:
                        pe.wait_ge(w_summed[1], KT * b)
                    pe.matmul(ps_l[:, k % 2, :], la_sb[:, s, P * k:P * k + P], lb_sb[:, s, :],
                              start=True, stop=True).then_inc(rank_done[s], 1)

            def linear(b, s, hi, lo):
                pe.wait_ge(w_ready[s], b + 1)
                for t in range(NT):
                    if t >= 2:
                        pe.wait_ge(y_read[s], NT * b + t - 1)
                    elif s:
                        pe.wait_ge(y_read[0], NT * (b + 1))
                    else:
                        pe.wait_ge(y_read[1], NT * b)
                    tok = slice(t * P, t * P + P)
                    for k in range(KT):
                        for n, (a, v) in enumerate(three(hi[:, k, tok], lo[:, k, tok], w_hi[:, s, k, :], w_lo[:, s, k, :])):
                            mm = pe.matmul(ps_y[:, t % 2, :], a, v, start=(k == 0 and n == 0), stop=(k == KT - 1 and n == 2))
                    mm.then_inc(y_done[s], 1)

            def turn(b, s, of):
                for t in range(NT):
                    if s == 0:
                        pe.wait_ge(gelu_ready, NT * b + t + 1)
                        pe.wait_ge(lo_ready[1], KT * b)
                    else:
                        pe.wait_ge(y_read[1], NT * b + t + 1)
                    for k in range(KT):
                        mm = pe.transpose(ps_t[:, k, t * P:(t + 1) * P], of[:, t, P * k:P * k + P], ident[:, :])
                        if t == NT - 1:
                            mm.then_inc(turned[s], 1)

            def blk(b, last):
                rank_product(b, 0)
                rank_product(b, 1)
                pe.wait_ge(lo_ready[1], KT * b)
                linear(b, 0, hT_hi, hT_lo)
                turn(b, 0, z)
                pe.wait_ge(lo_ready[0], KT * (b + 1))
                linear(b, 1, zT_hi, zT_lo)
                if not last:
                    turn(b, 1, h)

            with pe.Fori(0, NBK - 1) as b:
                blk(b, False)
            blk(NBK - 1, True)


def perceiver(nc, a, out):
    with ExitStack() as ctx:
        m = Memory(nc, ctx, "all")
        x, ident = m.sb("x", [P, NT, D]), m.sb("ident", [P, P])
        x_loaded, stored = m.sems("x_loaded", NT + 1), m.sem("stored")

        with ExitStack() as first:
            m = Memory(nc, first, "first")
            xT = m.sb("xT", [P, KT, TOK])

            def norm(prefetch):
                def loads(sp):
                    for t in range(NT):
                        sp.dma_start(x[:, t, :], a["x"][t * P:(t + 1) * P, :]).then_inc(x_loaded[t], 16)
                    sp.dma_start(ident[:, :], a["ident"]).then_inc(x_loaded[NT], 16)
                    prefetch(sp)

                with ExitStack() as stage:
                    xn = Memory(nc, stage, "n0").sb("xn", [P, NT, D])
                    layernorm(nc, "ln0", x, xn, xT, None, ident, loads, x_loaded)
            context_attention(nc, "ctx", norm, x, xT, ident, a["ctxT"], a["ctxN"])

        with ExitStack() as second:
            m = Memory(nc, second, "second")
            xT_hi, xT_lo = m.sb("xT_hi", [P, KT, TOK], F32R), m.sb("xT_lo", [P, KT, TOK], F32R)
            xn = m.sb("xn", [P, NT, D])
            head_attention(nc, "att0", lambda prefetch: layernorm(nc, "ln1", x, xn, xT_hi, xT_lo, ident, prefetch),
                           x, xn, xT_hi, xT_lo, ident, a["a0_wqk"], a["a0_wv"], a["a0_wo"], a["a0_bqk"],
                           a["a0_bv"], a["a0_bo"], DH, False)
            experts(nc, "moe", lambda prefetch: layernorm(nc, "ln2", x, xn, xT_hi, xT_lo, ident, prefetch),
                    x, xT_hi, xT_lo, ident, a["before"], a["gate"], a["w1"], a["w3"], a["w2"], a["b1"], a["b3"], a["b2"])

        with ExitStack() as cross:
            m = Memory(nc, cross, "cross")
            bq, bk, bv = m.sb("bq", [P, NG]), m.sb("bk", [P, NG]), m.sb("bv", [P, D])
            q = m.sb("q", [P, NG, TOK])
            with ExitStack() as kv:
                m = Memory(nc, kv, "kv")
                wk = m.sb("wk_hi", [P, KT, D], F32R), m.sb("wk_lo", [P, KT, D], F32R)
                wv = m.sb("wv_hi", [P, KT, D], F32R), m.sb("wv_lo", [P, KT, D], F32R)
                with ExitStack() as stage:
                    m = Memory(nc, stage, "query")
                    xn = m.sb("xn", [P, NT, D])
                    xT_hi, xT_lo = m.sb("xT_hi", [P, KT, TOK], F32R), m.sb("xT_lo", [P, KT, TOK], F32R)
                    wq_hi, wq_lo = m.sb("wq_hi", [P, KT, D], F32R), m.sb("wq_lo", [P, KT, D], F32R)
                    project_queries(nc, "pq", lambda prefetch: layernorm(nc, "ln3", x, xn, xT_hi, xT_lo, ident, prefetch),
                                    q, xT_hi, xT_lo, (wk, wv), (a["wq"], a["wk"], a["wv"]), wq_hi, wq_lo,
                                    ((bq[:, :], a["bq"]), (bk[:, :], a["bk"]), (bv[:, :], a["bv"].to_broadcast([P, D]))))
                masked_context_attention(nc, "cross", q, ident, wk, wv, bk, bv, a["ctxT"], a["mask"], a["gain"])
            project_attended(nc, "po", x, q, a["wo"], a["bo"])

        with ExitStack() as last:
            m = Memory(nc, last, "last")
            xn = m.sb("xn", [P, NT, D])
            xT_hi, xT_lo = m.sb("xT_hi", [P, KT, TOK], F32R), m.sb("xT_lo", [P, KT, TOK], F32R)
            head_attention(nc, "att1", lambda prefetch: layernorm(nc, "ln4", x, xn, xT_hi, xT_lo, ident, prefetch),
                           x, xn, xT_hi, xT_lo, ident, a["a1_wqk"], a["a1_wv"], a["a1_wo"], a["a1_bqk"],
                           a["a1_bv"], a["a1_bo"], D // 2, True)
            quantized_blocks(nc, "quant", lambda prefetch: layernorm(nc, "ln5", x, xn, xT_hi, xT_lo, ident, prefetch),
                             x, xn, xT_hi, xT_lo, ident, a["codes"], a["scales"], a["la"], a["lb"],
                             a["bias"], a["gamma"], a["beta"])

        with nc.Block() as block:
            @block.sync
            def _(sp):
                sp.dma_start(out.rearrange("(t p) d -> p t d", p=P), x[:, :, :]).then_inc(stored, 16)
                sp.wait_ge(stored, 16)




def _slices(w):
    return w.reshape(w.shape[0] // P, P, -1).transpose(1, 0, 2)


def _head_groups(np, wq, wk, wv, wo, bq, bk, bv, bo, dv):
    parts = max(1, HG * dv // 512)
    vc = HG * dv // parts
    both = [np.concatenate([wq[:, g * P:g * P + P], wk[:, g * P:g * P + P]], 1) for g in range(NG)]
    return {
        "wqk": np.stack([_slices(w) for w in both]),
        "wv": np.stack([_slices(wv[:, i * vc:i * vc + vc]) for i in range(NG * parts)]).reshape(NG, parts, P, KT, vc),
        "wo": np.stack([_slices(wo[i * vc:i * vc + vc]) for i in range(NG * parts)]).reshape(NG, parts, P, vc // P, D),
        "bqk": np.stack([bq.reshape(NG, P), bk.reshape(NG, P)], -1).transpose(1, 0, 2),
        "bv": bv.reshape(NG, 1, HG * dv),
        "bo": bo.reshape(1, D),
    }


def kernel(**inputs):
    import numpy as np
    import concourse.bacc as bacc
    from concourse.bass_utils import run_bass_kernel_spmd

    i = {name: np.asarray(v) for name, v in inputs.items()}
    ctx = i["ctx_1024"]
    padded = np.concatenate([ctx.transpose(0, 2, 1), np.zeros((B, D, S2P - S2), ctx.dtype)], 2)
    a = {
        "x": i["x"].reshape(TOK, D),
        "ident": np.eye(P, dtype=np.float32),
        "before": np.tril(np.ones((NE - 1, NE - 1), np.float32), -1).reshape(1, -1),
        "ctxN": ctx,
        "ctxT": padded.reshape(B, KT, P, S2P).transpose(0, 2, 1, 3),
        "mask": i["mask_BxSxS2_ik1"],
        "gain": i["fside_BxSxS2_0"],
    }
    w, b = i["L0_attn_Wqkv"], i["L0_attn_bqkv"]
    layer = _head_groups(np, w[:, 0:D], w[:, D:2 * D], w[:, 2 * D:], i["L0_attn_Wo"], b[0:D], b[D:2 * D], b[2 * D:],
                         i["L0_attn_bo"], DH)
    a.update({f"a0_{n}": v for n, v in layer.items()})
    w, b = i["L1_attn_Wc"].T, i["L1_attn_bc"]
    layer = _head_groups(np, w[:, 0:D], w[:, D:2 * D], w[:, 2 * D:], i["L1_attn_Wo"].T, b[0:D], b[D:2 * D], b[2 * D:],
                         i["L1_attn_bo"], D // 2)
    a.update({f"a1_{n}": v for n, v in layer.items()})
    a["gate"] = _slices(i["L0_ffn_gate_w"].T)
    for n in "132":
        a[f"w{n}"] = np.stack([_slices(v) for v in [*i[f"L0_ffn_w{n}"], i[f"L0_ffn_sw{n}"]]])
        bias = np.concatenate([i[f"L0_ffn_b{n}"], i[f"L0_ffn_sb{n}"][None]])
        a[f"b{n}"] = bias if n == "2" else bias.reshape(NE, KT, P).transpose(2, 0, 1)
    for n in "qkvo":
        a[f"w{n}"] = _slices(i[f"L1_xattn_w{n}_k"])
        bias = i[f"L1_xattn_w{n}_b"]
        a[f"b{n}"] = bias.reshape(NG, P).T if n in "qk" else bias.reshape(1, D)
    a["codes"] = np.stack([_slices(c.T) for c in i["L1_ffn_qweights"]])
    a["scales"] = i["L1_ffn_scales"].transpose(0, 2, 1)
    a["la"] = i["L1_ffn_lora_a"]
    a["lb"] = i["L1_ffn_lora_b"].transpose(0, 2, 1)
    a["bias"] = i["L1_ffn_biases"].reshape(-1, 1, D)
    a["gamma"] = i["L1_ffn_ln_gamma"].reshape(-1, 1, D)
    a["beta"] = i["L1_ffn_ln_beta"].reshape(-1, 1, D)

    nc = bacc.Bacc("TRN2", target_bir_lowering=False, num_devices=1)
    arrays = {f"in_{n}": np.ascontiguousarray(v) for n, v in a.items()}
    aps = {n: nc.dram_tensor(f"in_{n}", arrays[f"in_{n}"].shape, mybir.dt.from_np(arrays[f"in_{n}"].dtype),
                             kind="ExternalInput").ap() for n in a}
    out = nc.dram_tensor("out", (TOK, D), F32, kind="ExternalOutput").ap()
    perceiver(nc, aps, out)
    r = run_bass_kernel_spmd(nc, [arrays], core_ids=[0])
    return r.results[0]["out"].reshape(B, S, D)
```

```python
from contextlib import ExitStack
from math import sqrt

import concourse.bass as bass
from concourse import mybir

F32 = mybir.dt.float32
F32R = mybir.dt.float32r
I32 = mybir.dt.int32
ALU = mybir.AluOpType
ACT = mybir.ActivationFunctionType
AX_X = mybir.AxisListType.X

P = 128
B, S, D = 8, 64, 512
TOK = B * S
NT = TOK // P
KT = D // P
S2 = 1601
S2P = S2 + 1
CH0 = [0, 402, 802, 1202]
CHW = [402, 400, 400, 400]
CHV = [402, 400, 400, 399]
NJ = 13
JR = [P] * 12 + [S2 - 12 * P]
JG = [(0, 4), (4, 8), (8, 12), (12, 13)]
H = 16
HG = 4
NG = H // HG
DH = D // H
NE = 9
EPS = 1e-5
LOW = -3.0e38


def as_f32(ap):
    return ap.bitcast(F32)


def three(hi_a, lo_a, hi_b, lo_b):
    return ((hi_a, hi_b), (hi_a, lo_b), (lo_a, hi_b))




class Memory:

    def __init__(self, nc, ctx, stage):
        self.nc, self.ctx, self.stage = nc, ctx, stage
        self.used = []
        ctx.callback(self.clear)

    def sb(self, name, shape, dt=F32):
        return self.ctx.enter_context(self.nc.sbuf_tensor(f"{self.stage}_{name}", shape, dt))

    def pb(self, name, shape, dt=F32):
        return self.ctx.enter_context(self.nc.psum_tensor(f"{self.stage}_{name}", shape, dt))

    def sem(self, name):
        self.used.append(self.nc.alloc_semaphore(f"{self.stage}_{name}"))
        return self.used[-1]

    def clear(self):
        if self.used:
            self.nc.clear_and_free_semaphores(self.used)
            self.nc.all_engine_barrier()

    def sems(self, name, n):
        return [self.sem(f"{name}{i}") for i in range(n)]


def layernorm(nc, stage, x, xn, xT_hi, xT_lo, ident, prefetch, on_act=None, on_pool=None, x_loaded=None):
    with ExitStack() as ctx:
        m = Memory(nc, ctx, stage)
        stats = m.sb("stats", [P, NT, 6])
        mv = m.sb("mv", [P, NT, 2])
        var = m.sb("var", [P, NT])
        std = m.sb("std", [P, NT])
        rstd = m.sb("rstd", [P, NT])
        turned = m.pb("turned", [P, NT, KT, P])
        stats_ready, mv_ready, var_ready = m.sem("stats_ready"), m.sem("mv_ready"), m.sem("var_ready")
        std_ready, rstd_ready, xn_ready = m.sem("std_ready"), m.sem("rstd_ready"), m.sem("xn_ready")
        turned_ready, hi_ready, lo_ready = m.sem("turned_ready"), m.sem("hi_ready"), m.sem("lo_ready")
        block = ctx.enter_context(nc.Block())

        @block.sync
        def _(sp):
            prefetch(sp)

        if on_pool is not None:
            @block.gpsimd
            def _(pool):
                on_pool(pool)

        @block.vector
        def _(dve):
            for t in range(NT):
                if x_loaded is not None:
                    dve.wait_ge(x_loaded[t], 16)
                dve.bn_stats(stats[:, t, :], x[:, t, :]).then_inc(stats_ready, 1)
            for t in range(NT):
                dve.wait_ge(stats_ready, t + 1)
                dve.bn_aggr(mv[:, t, :], stats[:, t, :]).then_inc(mv_ready, 1)
            dve.wait_ge(mv_ready, NT)
            dve.tensor_scalar(var[:, :], mv[:, :, 1], EPS, None, ALU.add).then_inc(var_ready, 1)
            dve.wait_ge(std_ready, 1)
            dve.reciprocal(rstd[:, :], std[:, :]).then_inc(rstd_ready, 1)
            dve.wait_ge(rstd_ready, 1)
            for t in range(NT):
                dve.tensor_scalar(xn[:, t, :], x[:, t, :], mv[:, t, 0:1], rstd[:, t:t + 1],
                                  ALU.subtract, ALU.mult).then_inc(xn_ready, 1)
            if xT_lo is not None:
                for t in range(NT):
                    tok = slice(t * P, t * P + P)
                    dve.wait_ge(hi_ready, t + 1)
                    dve.tensor_tensor(xT_lo[:, :, tok], turned[:, t, :, :], as_f32(xT_hi[:, :, tok]),
                                      ALU.subtract).then_inc(lo_ready, 1)

        @block.scalar
        def _(act):
            act.wait_ge(var_ready, 1)
            act.activation(std[:, :], var[:, :], ACT.Sqrt).then_inc(std_ready, 1)
            if on_act is not None:
                on_act(act)
            for t in range(NT):
                act.wait_ge(turned_ready, t + 1)
                act.activation(xT_hi[:, :, t * P:(t + 1) * P], turned[:, t, :, :], ACT.Copy).then_inc(hi_ready, 1)

        @block.tensor
        def _(pe):
            if x_loaded is not None:
                pe.wait_ge(x_loaded[NT], 16)
            for t in range(NT):
                pe.wait_ge(xn_ready, t + 1)
                for k in range(KT):
                    turn = pe.transpose(turned[:, t, k, :], xn[:, t, k * P:(k + 1) * P], ident[:, :])
                turn.then_inc(turned_ready, 1)


def context_attention(nc, stage, norm, x, xT, ident, ctxT, ctxN):
    with ExitStack() as ctx:
        m = Memory(nc, ctx, stage)
        raw_T = m.sb("raw_T", [P, 2, KT, S2P])
        raw_N = m.sb("raw_N", [P, NJ, D])
        N_hi, N_lo = m.sb("N_hi", [P, NJ, D], F32R), m.sb("N_lo", [P, NJ, D], F32R)
        xs = m.sb("xs", [P, 2, KT, S])
        sc = m.sb("sc", [S, S2])
        pT = m.sb("pT", [P, NJ, 2 * S], F32R)
        cmax, csum = m.sb("cmax", [S, 4]), m.sb("csum", [S, 4])
        rmax, nmax, rsum, rinv = m.sb("rmax", [S, 1]), m.sb("nmax", [S, 1]), m.sb("rsum", [S, 1]), m.sb("rinv", [S, 1])
        o_below, o_sum = m.sb("o_below", [S, D]), m.sb("o_sum", [S, D])
        o_norm = m.sb("o_norm", [P, D])
        T_loaded = [m.sems(f"T_loaded{s}_", 4) for s in range(2)]
        N_loaded, N_hi_ready, N_split = (m.sems(n, len(JG)) for n in ("N_loaded", "N_hi_ready", "N_split"))
        xs_ready, scores_done, cmax_ready, rmax_ready, nmax_ready = (m.sem(n) for n in ("xs_ready", "scores_done", "cmax_ready", "rmax_ready", "nmax_ready"))
        exp_ready, rsum_ready, rinv_ready, turned, pT_hi_ready, pT_ready = (m.sem(n) for n in ("exp_ready", "rsum_ready", "rinv_ready", "turned", "pT_hi_ready", "pT_ready"))
        multiplied, o_below_ready, o_sum_ready, o_norm_ready, x_ready = (m.sem(n) for n in ("multiplied", "o_below_ready", "o_sum_ready", "o_norm_ready", "x_ready"))
        waited = m.sem("waited")
        pool_groups = (0, 3)
        turned_tiles = ((0, 8, P), (8, 12, P), (12, 13, JR[-1]))

        def steps(eng, batch):
            batch(0, 0, False)
            batch(0, 1, False)
            with eng.Fori(1, NT - 1) as t:
                batch(t, 0, False)
                batch(t, 1, False)
            batch(NT - 1, 0, True)
            batch(NT - 1, 1, True)

        def load_T(sp, b, t, s):
            for c in range(4):
                cols = slice(CH0[c], CH0[c] + CHW[c])
                sp.dma_start(raw_T[:, s, :, cols], ctxT[b, :, :, cols]).then_inc(T_loaded[s][c], 16)

        def load_N(sp, b, wait):
            for g, (j0, j1) in enumerate(JG):
                if wait:
                    sp.wait_ge(N_split[g], b)
                if g < 3:
                    rows = ctxN[b, j0 * P:j1 * P, :].rearrange("(j p) d -> p j d", p=P)
                    sp.dma_start(raw_N[:, j0:j1, :], rows).then_inc(N_loaded[g], 16)
                else:
                    sp.dma_start(raw_N[0:JR[-1], j0, :], ctxN[b, j0 * P:S2, :]).then_inc(N_loaded[g], 16)

        def prefetch(sp):
            load_T(sp, 0, 0, 0)
            load_N(sp, 0, False)
            load_T(sp, 1, 0, 1)

        norm(prefetch)
        ps_s = m.pb("ps_s", [P, 4, 512])
        ps_t = m.pb("ps_t", [P, 16, S])
        ps_o = m.pb("ps_o", [P, D])
        block = ctx.enter_context(nc.Block())

        @block.sync
        def _(sp):
            with sp.Fori(0, NT - 1) as t:
                for s in range(2):
                    sp.wait_ge(scores_done, 4 * (2 * t + s + 1))
                    load_T(sp, 2 * t + s + 2, t + 1, s)
                    load_N(sp, 2 * t + s + 1, True)
            load_N(sp, B - 1, True)

        @block.scalar
        def _(act):
            def split_N(b):
                for g, (j0, j1) in enumerate(JG):
                    r = JR[j0]
                    act.wait_ge(N_loaded[g], 16 * (b + 1))
                    act.wait_ge(multiplied, b)
                    act.activation(N_hi[0:r, j0:j1, :], raw_N[0:r, j0:j1, :], ACT.Copy).then_inc(N_hi_ready[g], 1)

            def exps(b):
                act.wait_ge(turned, b)
                act.wait_ge(nmax_ready, b + 1)
                for c in range(4):
                    act.activation(sc[:, CH0[c]:CH0[c] + CHV[c]], ps_s[0:S, c, 0:CHV[c]], ACT.Exp, bias=nmax[:, :],
                                   accum_out=csum[:, c:c + 1]).then_inc(exp_ready, 1)

            def turned_high(b):
                act.wait_ge(turned, b + 1)
                act.wait_ge(multiplied, b)
                for j0, j1, r in turned_tiles:
                    act.activation(pT[0:r, j0:j1, 0:S], ps_t[0:r, j0:j1, :], ACT.Copy).then_inc(pT_hi_ready, 1)

            def out_below(b):
                act.wait_ge(multiplied, b + 1)
                act.activation(o_below[:, :], ps_o[S:2 * S, :], ACT.Copy).then_inc(o_below_ready, 1)

            def batch(t, s, last):
                b = 2 * t + s
                split_N(b)
                if not (last and s == 1):
                    exps(b + 1)
                out_below(b)
                if not (last and s == 1):
                    turned_high(b + 1)

            exps(0)
            turned_high(0)
            steps(act, batch)

        @block.gpsimd
        def _(pool):
            with pool.Fori(0, B) as b:
                for g in pool_groups:
                    (j0, j1), r = JG[g], JR[JG[g][0]]
                    pool.wait_ge(N_hi_ready[g], b + 1)
                    pool.tensor_tensor(N_lo[0:r, j0:j1, :], raw_N[0:r, j0:j1, :], as_f32(N_hi[0:r, j0:j1, :]),
                                       ALU.subtract).then_inc(N_split[g], 1)

        @block.vector
        def _(dve):
            def stage_x(b, s):
                dve.tensor_copy(xs[:, s, :, :], xT[:, :, bass.ts(b, S)]).then_inc(xs_ready, 1)

            def split_N(b):
                for g, (j0, j1) in enumerate(JG):
                    if g not in pool_groups:
                        dve.wait_ge(N_hi_ready[g], b + 1)
                        dve.tensor_tensor(N_lo[:, j0:j1, :], raw_N[:, j0:j1, :], as_f32(N_hi[:, j0:j1, :]),
                                          ALU.subtract).then_inc(N_split[g], 1)

            def maxima(b):
                for c in range(4):
                    dve.wait_ge(scores_done, 4 * b + c + 1)
                    dve.tensor_reduce(cmax[:, c:c + 1], ps_s[0:S, c, 0:CHV[c]], AX_X, ALU.max).then_inc(cmax_ready, 1)
                dve.wait_ge(cmax_ready, 4 * b + 4)
                dve.tensor_reduce(rmax[:, :], cmax[:, :], AX_X, ALU.max).then_inc(rmax_ready, 1)
                dve.wait_ge(rmax_ready, b + 1)
                dve.tensor_scalar(nmax[:, :], rmax[:, :], -1.0, None, ALU.mult).then_inc(nmax_ready, 1)

            def turned_low(b):
                for i, (j0, j1, r) in enumerate(turned_tiles):
                    dve.wait_ge(pT_hi_ready, 3 * b + (1 if i == 0 else 3))
                    dve.tensor_tensor(pT[0:r, j0:j1, S:2 * S], ps_t[0:r, j0:j1, :], as_f32(pT[0:r, j0:j1, 0:S]),
                                      ALU.subtract).then_inc(pT_ready, 1)

            def sums(b):
                dve.wait_ge(exp_ready, 4 * (b + 1))
                dve.tensor_reduce(rsum[:, :], csum[:, :], AX_X, ALU.add).then_inc(rsum_ready, 1)
                dve.wait_ge(rsum_ready, b + 1)
                dve.reciprocal(rinv[:, :], rsum[:, :]).then_inc(rinv_ready, 1)

            def add_out(b, t, s):
                q = slice(S * s, S * s + S)
                dve.wait_ge(o_below_ready, b + 1)
                dve.tensor_tensor(o_sum[:, :], ps_o[0:S, :], o_below[:, :], ALU.add).then_inc(o_sum_ready, 1)
                dve.wait_ge(rinv_ready, b + 1)
                dve.wait_ge(o_sum_ready, b + 1)
                dve.tensor_scalar(o_norm[q, :], o_sum[:, :], rinv[:, 0:1], None, ALU.mult).then_inc(o_norm_ready, 1)
                dve.wait_ge(o_norm_ready, b + 1)
                dve.tensor_tensor(x[q, t, :], x[q, t, :], o_norm[q, :], ALU.add).then_inc(x_ready, 1)

            def batch(t, s, last):
                b = 2 * t + s
                split_N(b)
                if not (last and s == 1):
                    maxima(b + 1)
                if not last:
                    stage_x(b + 2, s)
                add_out(b, t, s)
                if not (last and s == 1):
                    sums(b + 1)
                    turned_low(b + 1)

            stage_x(0, 0)
            stage_x(1, 1)
            maxima(0)
            sums(0)
            turned_low(0)
            steps(dve, batch)

        @block.tensor
        def _(pe):
            def scores(b, t, s):
                pe.wait_ge(xs_ready, b + 1)
                for c in range(4):
                    pe.wait_ge(T_loaded[s][c], 16 * (t + 1))
                    for k in range(KT):
                        mm = pe.matmul(ps_s[0:S, c, 0:CHW[c]], xs[:, s, k, :], raw_T[:, s, k, CH0[c]:CH0[c] + CHW[c]],
                                       start=(k == 0), stop=(k == KT - 1))
                    mm.then_inc(scores_done, 1)

            def turn(b):
                pe.wait_ge(pT_ready, 3 * b)
                pe.wait_ge(exp_ready, 4 * (b + 1))
                pe.sem_inc(waited, 1)
                for j in range(NJ):
                    last = pe.transpose(ps_t[0:JR[j], j, :], sc[:, j * P:j * P + JR[j]], ident[0:S, 0:S])
                last.then_inc(turned, 1)

            def values(b):
                pe.wait_ge(pT_ready, 3 * b + 3)
                pe.wait_ge(o_sum_ready, b)
                for g, (j0, j1) in enumerate(JG):
                    pe.wait_ge(N_split[g], b + 1)
                    for j in range(j0, j1):
                        r = JR[j]
                        pairs = [(2 * S, N_hi), (S, N_lo)] if j < NJ - 1 else [(S, N_lo), (2 * S, N_hi)]
                        for n, (rows, half) in enumerate(pairs):
                            mm = pe.matmul(ps_o[0:rows, :], pT[0:r, j, 0:rows], half[0:r, j, :],
                                           start=(j == 0 and n == 0), stop=(j == NJ - 1 and n == 1))
                mm.then_inc(multiplied, 1)

            def batch(t, s, last):
                b = 2 * t + s
                if not (last and s == 1):
                    scores(b + 1, t + s, 1 - s)
                values(b)
                if not (last and s == 1):
                    turn(b + 1)

            scores(0, 0, 0)
            turn(0)
            steps(pe, batch)


def head_attention(nc, stage, norm, x, xn, xT_hi, xT_lo, ident, wqk, wv, wo, bqk, bv, bo, dv, rectified):
    parts = max(1, HG * dv // 512)
    vc = HG * dv // parts
    hp = HG // parts
    ko = vc // P
    kc = max(1, dv // P)
    scale = 1.0 / sqrt(DH)
    with ExitStack() as ctx:
        m = Memory(nc, ctx, stage)
        raw_qk = m.sb("raw_qk", [P, KT, 2 * P])
        raw_v = m.sb("raw_v", [P, KT, vc])
        raw_o = m.sb("raw_o", [P, ko, D])
        qk_hi, qk_lo = m.sb("qk_hi", [P, KT, 2 * P], F32R), m.sb("qk_lo", [P, KT, 2 * P], F32R)
        wv_hi, wv_lo = m.sb("wv_hi", [P, KT, vc], F32R), m.sb("wv_lo", [P, KT, vc], F32R)
        wo_hi, wo_lo = m.sb("wo_hi", [P, ko, D], F32R), m.sb("wo_lo", [P, ko, D], F32R)
        bqk_sb = m.sb("bqk_sb", [P, NG, 2])
        bv_sb = m.sb("bv_sb", [P, parts, vc])
        qk = m.sb("qk", [P, 2, TOK])
        v_sum = m.sb("v_sum", [P, 2, vc])
        v_hi, v_lo = m.sb("v_hi", [P, NT, vc], F32R), m.sb("v_lo", [P, NT, vc], F32R)
        smax, rsum, rinv = m.sb("smax", [P, HG, NT]), m.sb("rsum", [P, HG, NT]), m.sb("rinv", [P, HG, NT])
        sc = m.sb("sc", [P, HG, NT, S])
        probs = m.sb("probs", [P, HG, NT, P])
        pT_hi, pT_lo = m.sb("pT_hi", [P, 2, TOK], F32R), m.sb("pT_lo", [P, 2, TOK], F32R)
        o_hi, o_lo = m.sb("o_hi", [P, ko, TOK], F32R), m.sb("o_lo", [P, ko, TOK], F32R)
        y = m.sb("y", [P, NT, D])

        start_loaded, y_loaded, qk_loaded, v_loaded, o_loaded, bv_loaded = (m.sem(n) for n in ("start_loaded", "y_loaded", "qk_loaded", "v_loaded", "o_loaded", "bv_loaded"))
        wqk_hi_ready, wqk_ready, wv_hi_ready, wv_ready, wo_hi_ready, wo_ready = (m.sem(n) for n in (
            "wqk_hi_ready", "wqk_ready", "wv_hi_ready", "wv_ready", "wo_hi_ready", "wo_ready"))
        qk_done, v_done, y_done = m.sem("qk_done"), m.sem("v_done"), m.sem("y_done")
        qk_added, v_added, y_added = m.sem("qk_added"), m.sem("v_added"), m.sem("y_added")
        qk_sum_ready, qk_ready, scores_done, smax_ready, sub_ready = (m.sem(n) for n in ("qk_sum_ready", "qk_ready", "scores_done", "smax_ready", "sub_ready"))
        exp_ready, rsum_ready, rinv_ready, zero_ready, probs_ready = (m.sem(n) for n in ("exp_ready", "rsum_ready", "rinv_ready", "zero_ready", "probs_ready"))
        turned, pT_hi_ready, pT_ready = (m.sem(n) for n in ("turned", "pT_hi_ready", "pT_ready"))
        v_sum_ready, v_hi_ready, v_ready = (m.sem(n) for n in ("v_sum_ready", "v_hi_ready", "v_ready"))
        o_done, o_hi_ready, o_ready, x_ready = (m.sem(n) for n in ("o_done", "o_hi_ready", "o_ready", "x_ready"))

        n_o = ko if dv >= P else HG

        def uses(g, part, t=0):
            return (g * parts + part) * NT + t

        v_sum_stands = v_sum_ready if rectified else v_added

        def outputs_of(g, h):
            return g * parts * n_o + h * kc

        def load_qk(sp, g, first=False):
            if not first:
                sp.wait_ge(wqk_ready, g)
            sp.dma_start(raw_qk[:, :, :], wqk[g]).then_inc(qk_loaded, 16)

        def load_v(sp, g, part, first=False):
            if not first:
                sp.wait_ge(wv_ready, g * parts + part)
            sp.dma_start(raw_v[:, :, :], wv[g, part]).then_inc(v_loaded, 16)

        def load_o(sp, g, part, first=False):
            if not first:
                sp.wait_ge(wo_ready, g * parts + part)
            sp.dma_start(raw_o[:, :, :], wo[g, part]).then_inc(o_loaded, 16)

        def load_bv(sp, g, first=False):
            if not first:
                sp.wait_ge(v_ready, uses(g, 0))
            sp.dma_start(bv_sb[:, :, :].rearrange("p a c -> p (a c)"),
                         bv[g].to_broadcast([P, HG * dv])).then_inc(bv_loaded, 16)

        def prefetch(sp):
            load_qk(sp, 0, True)
            sp.dma_start(bqk_sb[:, :, :], bqk).then_inc(start_loaded, 16)
            load_v(sp, 0, 0, True)
            load_bv(sp, 0, True)
            load_o(sp, 0, 0, True)
            for t in range(NT):
                sp.dma_start(y[:, t, :], bo.to_broadcast([P, D])).then_inc(y_loaded, 16)

        def split_qk(act, g, first=False):
            act.wait_ge(qk_loaded, 16 * (g + 1))
            if not first:
                act.wait_ge(qk_done, 2 * g)
            act.activation(qk_hi[:, :, :], raw_qk[:, :, :], ACT.Copy).then_inc(wqk_hi_ready, 1)

        def qk_low(pool, g):
            pool.wait_ge(wqk_hi_ready, g + 1)
            pool.tensor_tensor(qk_lo[:, :, :], raw_qk[:, :, :], as_f32(qk_hi[:, :, :]), ALU.subtract).then_inc(wqk_ready, 1)

        def early_pool(pool):
            pool.memset(probs[:, :, :, :], 0.0).then_inc(zero_ready, 1)
            qk_low(pool, 0)

        norm(prefetch, lambda act: split_qk(act, 0, True), early_pool)
        ps_p = m.pb("ps_p", [P, 2, 512])
        ps_s = m.pb("ps_s", [P, HG, 512])
        ps_o = m.pb("ps_o", [P, 2, 512])
        block = ctx.enter_context(nc.Block())

        @block.sync
        def _(sp):
            if parts == 2:
                load_v(sp, 0, 1)
            with sp.Fori(0, NG - 1) as g:
                load_qk(sp, g + 1)
                load_v(sp, g + 1, 0)
                if parts == 2:
                    load_o(sp, g, 1)
                load_bv(sp, g + 1)
                if parts == 2:
                    load_v(sp, g + 1, 1)
                load_o(sp, g + 1, 0)
            if parts == 2:
                load_o(sp, NG - 1, 1)

        @block.scalar
        def _(act):
            def split_v(g, part):
                act.wait_ge(v_loaded, 16 * (g * parts + part + 1))
                act.wait_ge(v_done, uses(g, part))
                act.activation(wv_hi[:, :, :], raw_v[:, :, :], ACT.Copy).then_inc(wv_hi_ready, 1)

            def split_o(g, part):
                act.wait_ge(o_loaded, 16 * (g * parts + part + 1))
                act.wait_ge(y_done, uses(g, part))
                act.activation(wo_hi[:, :, :], raw_o[:, :, :], ACT.Copy).then_inc(wo_hi_ready, 1)

            def exps(g):
                act.wait_ge(sub_ready, HG * (g + 1))
                act.activation(sc[:, :, :, :], sc[:, :, :, :], ACT.Exp, scale=scale).then_inc(exp_ready, 1)

            def values_high(g, part):
                act.wait_ge(o_done, outputs_of(g, part * hp))
                for t in range(NT):
                    act.wait_ge(v_sum_stands, uses(g, part, t + 1))
                    act.activation(v_hi[:, t, :], v_sum[:, t % 2, :], ACT.Copy).then_inc(v_hi_ready, 1)

            def turned_high(g, h):
                act.wait_ge(turned, g * HG + h + 1)
                act.wait_ge(o_done, outputs_of(g, max(0, h - 1)))
                act.activation(pT_hi[:, h % 2, :], ps_s[:, h, :], ACT.Copy).then_inc(pT_hi_ready, 1)

            def output_high(g, n):
                act.wait_ge(y_done, uses(g, n // n_o))
                act.wait_ge(o_done, g * parts * n_o + n + 1)
                k, rows = (n % n_o, slice(0, P)) if dv >= P else (0, slice(dv * n, dv * n + dv))
                act.activation(o_hi[rows, k, :], ps_o[rows, n % 2, :], ACT.Copy).then_inc(o_hi_ready, 1)

            def group(g, last):
                if parts == 1:
                    if not last:
                        split_qk(act, g + 1)
                    output_high(g, 0)
                    turned_high(g, 2)
                    output_high(g, 1)
                    turned_high(g, 3)
                    split_o(g, 0)
                    output_high(g, 2)
                    output_high(g, 3)
                    if not last:
                        split_v(g + 1, 0)
                        exps(g + 1)
                        values_high(g + 1, 0)
                else:
                    for n in range(n_o):
                        output_high(g, n)
                    split_o(g, 0)
                    if not last:
                        split_qk(act, g + 1)
                    values_high(g, 1)
                    turned_high(g, 2)
                    turned_high(g, 3)
                    if last:
                        split_o(g, 1)
                    else:
                        split_v(g + 1, 0)
                    for n in range(n_o, 2 * n_o):
                        output_high(g, n)
                    if not last:
                        split_o(g, 1)
                        exps(g + 1)
                        values_high(g + 1, 0)
                if not last:
                    turned_high(g + 1, 0)
                    turned_high(g + 1, 1)
                    if parts == 2:
                        split_v(g + 1, 1)

            split_v(0, 0)
            exps(0)
            values_high(0, 0)
            turned_high(0, 0)
            turned_high(0, 1)
            if parts == 2:
                split_v(0, 1)
            group(0, False)
            with act.Fori(1, NG - 1) as g:
                group(g, False)
            group(NG - 1, True)

        @block.gpsimd
        def _(pool):
            def wv_low(g, part):
                pool.wait_ge(wv_hi_ready, g * parts + part + 1)
                pool.tensor_tensor(wv_lo[:, :, :], raw_v[:, :, :], as_f32(wv_hi[:, :, :]), ALU.subtract).then_inc(wv_ready, 1)

            def wo_low(g, part):
                pool.wait_ge(wo_hi_ready, g * parts + part + 1)
                pool.tensor_tensor(wo_lo[:, :, :], raw_o[:, :, :], as_f32(wo_hi[:, :, :]), ALU.subtract).then_inc(wo_ready, 1)

            def values_low(g, part):
                for t in range(NT):
                    pool.wait_ge(v_hi_ready, uses(g, part, t + 1))
                    pool.tensor_tensor(v_lo[:, t, :], v_sum[:, t % 2, :], as_f32(v_hi[:, t, :]), ALU.subtract).then_inc(v_ready, 1)

            def group(g, last):
                if parts == 1:
                    if not last:
                        qk_low(pool, g + 1)
                    wo_low(g, 0)
                    if not last:
                        wv_low(g + 1, 0)
                        values_low(g + 1, 0)
                else:
                    wo_low(g, 0)
                    if not last:
                        qk_low(pool, g + 1)
                    values_low(g, 1)
                    if last:
                        wo_low(g, 1)
                    else:
                        wv_low(g + 1, 0)
                        wo_low(g, 1)
                        values_low(g + 1, 0)
                        wv_low(g + 1, 1)

            wv_low(0, 0)
            values_low(0, 0)
            if parts == 2:
                wv_low(0, 1)
            with pool.Fori(0, NG - 1) as g:
                group(g, False)
            group(NG - 1, True)

        @block.vector
        def _(dve):
            def query_key(g, i):
                dve.wait_ge(scores_done, g)
                dve.wait_ge(qk_done, 2 * g + i + 1)
                dve.tensor_scalar(qk[:, i, :], ps_p[:, i, :], bqk_sb[:, g, i:i + 1], None, ALU.add).then_inc(qk_added, 1)
                if rectified:
                    dve.wait_ge(qk_added, 2 * g + i + 1)
                    dve.scalar_tensor_tensor(out=qk[:, i, :], in0=qk[:, i, :], scalar=0.01, in1=qk[:, i, :],
                                             op0=ALU.mult, op1=ALU.max).then_inc(qk_ready, 1)

            def values(g, part, t):
                dve.wait_ge(v_done, uses(g, part, t + 1))
                dve.wait_ge(v_ready, uses(g, part, max(0, t - 1)))
                dve.tensor_tensor(v_sum[:, t % 2, :], ps_p[:, t % 2, 0:vc], bv_sb[:, part, :], ALU.add).then_inc(v_added, 1)
                if rectified:
                    dve.wait_ge(v_added, uses(g, part, t + 1))
                    dve.scalar_tensor_tensor(out=v_sum[:, t % 2, :], in0=v_sum[:, t % 2, :], scalar=0.01,
                                             in1=v_sum[:, t % 2, :], op0=ALU.mult, op1=ALU.max).then_inc(v_sum_ready, 1)

            def softmax_and_values(g):
                dve.wait_ge(scores_done, g + 1)
                for_scores = ps_s[:, :, 0:NT * S].rearrange("p h (t k) -> p h t k", k=S)
                dve.tensor_reduce(smax[:, :, :], for_scores, AX_X, ALU.max).then_inc(smax_ready, 1)
                dve.wait_ge(smax_ready, g + 1)
                for h in range(HG):
                    dve.tensor_tensor(sc[:, h, :, :], for_scores[:, h, :, :],
                                      smax[:, h, :].unsqueeze(2).to_broadcast([P, NT, S]), ALU.subtract).then_inc(sub_ready, 1)
                dve.wait_ge(bv_loaded, 16 * (g + 1))
                values(g, 0, 0)
                dve.wait_ge(exp_ready, g + 1)
                dve.tensor_reduce(rsum[:, :, :], sc[:, :, :, :], AX_X, ALU.add).then_inc(rsum_ready, 1)
                dve.wait_ge(rsum_ready, g + 1)
                dve.reciprocal(rinv[:, :, :], rsum[:, :, :]).then_inc(rinv_ready, 1)
                dve.wait_ge(rinv_ready, g + 1)
                dve.wait_ge(turned, g * HG)
                for half in range(2):
                    q = slice(S * half, S * half + S)
                    own = probs[q, :, :, S * half:S * half + S].rearrange("p h t k -> p (h t) k")
                    dve.tensor_tensor(own, sc[q, :, :, :].rearrange("p h t k -> p (h t) k"),
                                      rinv[q, :, :].rearrange("p h t -> p (h t)").unsqueeze(2).to_broadcast([S, HG * NT, S]),
                                      ALU.mult).then_inc(probs_ready, 1)
                for t in range(1, NT):
                    values(g, 0, t)

            def turned_low(g, h):
                dve.wait_ge(pT_hi_ready, g * HG + h + 1)
                dve.tensor_tensor(pT_lo[:, h % 2, :], ps_s[:, h, :], as_f32(pT_hi[:, h % 2, :]),
                                  ALU.subtract).then_inc(pT_ready, 1)

            def output_low(g, n):
                dve.wait_ge(o_hi_ready, g * parts * n_o + n + 1)
                k, rows = (n % n_o, slice(0, P)) if dv >= P else (0, slice(dv * n, dv * n + dv))
                dve.tensor_tensor(o_lo[rows, k, :], ps_o[rows, n % 2, :], as_f32(o_hi[rows, k, :]),
                                  ALU.subtract).then_inc(o_ready, 1)

            def add_y(g, part, t):
                dve.wait_ge(y_done, uses(g, part, t + 1))
                dve.wait_ge(y_added, uses(g, part))
                dve.tensor_tensor(y[:, t, :], y[:, t, :], ps_p[:, t % 2, :], ALU.add).then_inc(y_added, 1)

            def add_x(t):
                dve.wait_ge(y_added, uses(NG, 0, t + 1 - NT))
                if rectified:
                    dve.scalar_tensor_tensor(out=y[:, t, :], in0=y[:, t, :], scalar=0.01, in1=y[:, t, :],
                                             op0=ALU.mult, op1=ALU.max).then_inc(x_ready, 1)
                    dve.wait_ge(x_ready, NT + 2 * t + 1)
                dve.tensor_tensor(x[:, t, :], x[:, t, :], y[:, t, :], ALU.add).then_inc(x_ready, 1)

            def group(g, last):
                if parts == 1:
                    output_low(g, 0)
                    turned_low(g, 2)
                    output_low(g, 1)
                    turned_low(g, 3)
                    if not last:
                        query_key(g + 1, 0)
                        query_key(g + 1, 1)
                    output_low(g, 2)
                    output_low(g, 3)
                else:
                    for n in range(n_o):
                        output_low(g, n)
                    for t in range(NT):
                        values(g, 1, t)
                    for t in range(NT):
                        add_y(g, 0, t)
                    turned_low(g, 2)
                    turned_low(g, 3)
                    if not last:
                        query_key(g + 1, 0)
                        query_key(g + 1, 1)
                    for n in range(n_o, 2 * n_o):
                        output_low(g, n)
                if not last:
                    softmax_and_values(g + 1)
                elif rectified:
                    for t in range(NT):
                        dve.tensor_tensor(x[:, t, :], x[:, t, :], xn[:, t, :], ALU.add).then_inc(x_ready, 1)
                for t in range(NT):
                    if t == 2 and not last:
                        turned_low(g + 1, 0)
                        turned_low(g + 1, 1)
                    add_y(g, parts - 1, t)
                    if last:
                        add_x(t)

            dve.wait_ge(start_loaded, 16)
            dve.wait_ge(zero_ready, 1)
            query_key(0, 0)
            query_key(0, 1)
            softmax_and_values(0)
            turned_low(0, 0)
            turned_low(0, 1)
            dve.wait_ge(y_loaded, 16 * NT)
            group(0, False)
            with dve.Fori(1, NG - 1) as g:
                group(g, False)
            group(NG - 1, True)

        @block.tensor
        def _(pe):

            def query_key(g, first):
                pe.wait_ge(wqk_ready, g + 1)
                for i in range(2):
                    if not first:
                        if parts == 2:
                            pe.wait_ge(y_added, uses(g - 1, 0, i + 3))
                        else:
                            pe.wait_ge(y_added, uses(g - 1, 0))
                            pe.wait_ge(v_added, uses(g, 0))
                    for k in range(KT):
                        cols = slice(P * i, P * i + P)
                        for n, (w, a) in enumerate(three(qk_hi[:, k, cols], qk_lo[:, k, cols], xT_hi[:, k, :], xT_lo[:, k, :])):
                            mm = pe.matmul(ps_p[:, i, :], w, a, start=(k == 0 and n == 0), stop=(k == KT - 1 and n == 2))
                    mm.then_inc(qk_done, 1)

            def scores(g):
                pe.wait_ge(qk_ready if rectified else qk_added, 2 * g + 2)
                pe.wait_ge(pT_ready, g * HG)
                for t in range(NT):
                    for half in range(2):
                        for h in range(HG):
                            r = slice(DH * h, DH * h + DH)
                            tok = slice(t * P + half * S, t * P + half * S + S)
                            mm = pe.matmul(ps_s[half * S:half * S + S, h, t * S:t * S + S], qk[r, 0, tok], qk[r, 1, tok],
                                           start=True, stop=True)
                mm.then_inc(scores_done, 1)

            def values(g, part):
                pe.wait_ge(wv_ready, g * parts + part + 1)
                for t in range(NT):
                    if t >= 2:
                        pe.wait_ge(v_added, uses(g, part, t - 1))
                    elif part:
                        pe.wait_ge(y_added, uses(g, 0))
                        pe.wait_ge(v_added, uses(g, 1))
                    for k in range(KT):
                        tok = slice(t * P, t * P + P)
                        for n, (a, w) in enumerate(three(xT_hi[:, k, tok], xT_lo[:, k, tok], wv_hi[:, k, :], wv_lo[:, k, :])):
                            mm = pe.matmul(ps_p[:, t % 2, 0:vc], a, w, start=(k == 0 and n == 0), stop=(k == KT - 1 and n == 2))
                    mm.then_inc(v_done, 1)

            def turn(g, h):
                if h % hp == 0:
                    pe.wait_ge(probs_ready, 2 * (g + 1))
                for t in range(NT):
                    mm = pe.transpose(ps_s[:, h, t * P:(t + 1) * P], probs[:, h, t, :], ident[:, :])
                mm.then_inc(turned, 1)

            def outputs(g, h):
                part = h // hp
                pe.wait_ge(pT_ready, g * HG + h + 1)
                for c in range(kc):
                    n = h * kc + c
                    pe.wait_ge(o_ready, g * parts * n_o + max(0, n - 1))
                    v0 = (h - part * hp) * dv + c * P if dv >= P else 0
                    for t in range(NT):
                        if h % hp == 0 and c == 0:
                            pe.wait_ge(v_ready, uses(g, part, t + 1))
                        tok = slice(t * P, t * P + P)
                        for i, (v, p) in enumerate(three(v_hi[:, t, v0:v0 + P], v_lo[:, t, v0:v0 + P],
                                                         pT_hi[:, h % 2, tok], pT_lo[:, h % 2, tok])):
                            mm = pe.matmul(ps_o[:, n % 2, tok], v, p, start=(i == 0), stop=(i == 2))
                    mm.then_inc(o_done, 1)

            def project(g, part, t, last):
                if t == 0:
                    pe.wait_ge(wo_ready, g * parts + part + 1)
                    pe.wait_ge(o_ready, (g * parts + part + 1) * n_o)
                if t >= 2:
                    pe.wait_ge(y_added, uses(g, part, t - 1))
                elif part < parts - 1:
                    pe.wait_ge(v_added, uses(g, part + 1, t + 3))
                elif last:
                    pe.wait_ge(y_added, uses(g, part))
                else:
                    pe.wait_ge(v_added, uses(g + 1, 0, t + 3))
                for k in range(ko):
                    tok = slice(t * P, t * P + P)
                    for n, (o, w) in enumerate(three(o_hi[:, k, tok], o_lo[:, k, tok], wo_hi[:, k, :], wo_lo[:, k, :])):
                        mm = pe.matmul(ps_p[:, t % 2, :], o, w, start=(k == 0 and n == 0), stop=(k == ko - 1 and n == 2))
                mm.then_inc(y_done, 1)

            def group(g, last):
                if parts == 1:
                    outputs(g, 0)
                    turn(g, 2)
                    outputs(g, 1)
                    turn(g, 3)
                else:
                    outputs(g, 0)
                    outputs(g, 1)
                    values(g, 1)
                    for t in range(NT):
                        project(g, 0, t, last)
                    turn(g, 2)
                    turn(g, 3)
                if not last:
                    query_key(g + 1, False)
                outputs(g, 2)
                outputs(g, 3)
                if not last:
                    scores(g + 1)
                    values(g + 1, 0)
                for t in range(NT):
                    if t == 2 and not last:
                        turn(g + 1, 0)
                        turn(g + 1, 1)
                    project(g, parts - 1, t, last)

            query_key(0, True)
            scores(0)
            values(0, 0)
            turn(0, 0)
            turn(0, 1)
            group(0, False)
            with pe.Fori(1, NG - 1) as g:
                group(g, False)
            group(NG - 1, True)


def experts(nc, stage, norm, x, xT_hi, xT_lo, ident, before, gate, w1, w3, w2, b1, b3, b2):
    NR = NE - 1
    with ExitStack() as ctx:
        m = Memory(nc, ctx, stage)
        raw = [m.sb(f"raw{i}", [P, KT, D]) for i in range(3)]
        w_hi = [m.sb(f"w_hi{i}", [P, KT, D], F32R) for i in range(3)]
        w_lo = [m.sb(f"w_lo{i}", [P, KT, D], F32R) for i in range(3)]
        b1_sb, b3_sb, b2_sb = m.sb("b1", [P, NE, KT]), m.sb("b3", [P, NE, KT]), m.sb("b2", [NE, D])
        gate_sb = m.sb("gate", [P, KT, NR])
        gate_hi, gate_lo = m.sb("gate_hi", [P, KT, NR], F32R), m.sb("gate_lo", [P, KT, NR], F32R)
        before_sb = m.sb("before", [P, NR, NR])
        lg, pr = m.sb("lg", [P, NT, NR]), m.sb("pr", [P, NT, NR])
        rmax, rsum, rinv = m.sb("rmax", [P, NT]), m.sb("rsum", [P, NT]), m.sb("rinv", [P, NT])
        beats, ties = m.sb("beats", [P, NT, NR, NR]), m.sb("ties", [P, NT, NR, NR])
        rank, chosen = m.sb("rank", [P, NT, NR]), m.sb("chosen", [P, NT, NR])
        weight = m.sb("weight", [P, NE, NT])
        weightT = m.sb("weightT", [NE, TOK])
        logitsT = m.sb("logitsT", [NR, TOK])
        gated = m.sb("gated", [P, 2, TOK])
        h32 = m.sb("h32", [P, KT, TOK])
        h_hi, h_lo = m.sb("h_hi", [P, KT, TOK], F32R), m.sb("h_lo", [P, KT, TOK], F32R)

        small_loaded, gate_hi_ready, gate_ready, logits_done, router, weight_ready = (m.sem(n) for n in (
            "small_loaded", "gate_hi_ready", "gate_ready", "logits_done", "router", "weight_ready"))
        router_exp, weight_turned, weightT_ready, bias_done = (m.sem(n) for n in ("router_exp", "weight_turned", "weightT_ready", "bias_done"))
        loaded, hi_ready, lo_ready = m.sems("loaded", 3), m.sems("hi_ready", 3), m.sems("lo_ready", 3)
        up_done, down_done = m.sem("up_done"), m.sem("down_done")
        gated_ready, h_ready, h_hi_ready, h_lo_ready = (m.sem(n) for n in ("gated_ready", "h_ready", "h_hi_ready", "h_lo_ready"))
        bias_added, x_ready = m.sem("bias_added"), m.sem("x_ready")
        logitsT_ready, logits_turned = m.sem("logitsT_ready"), m.sem("logits_turned")
        weights = (w1, w3, w2)

        def load(sp, e, i):
            sp.dma_start(raw[i][:, :, :], weights[i][e]).then_inc(loaded[i], 16)

        def prefetch(sp):
            load(sp, 0, 0)
            for to, of in ((gate_sb[:, :, :], gate), (before_sb[:, :, :], before.to_broadcast([P, NR * NR]).rearrange("p (a b) -> p a b", b=NR)),
                           (b1_sb[:, :, :], b1), (b3_sb[:, :, :], b3), (b2_sb[:, :], b2)):
                sp.dma_start(to, of).then_inc(small_loaded, 16)
            load(sp, 0, 1)
            load(sp, 0, 2)

        def split(act, e, i, first=False):
            act.wait_ge(loaded[i], 16 * (e + 1))
            if not first and i < 2:
                act.wait_ge(up_done, KT * e)
            elif not first:
                act.wait_ge(down_done, NT * e)
            act.activation(w_hi[i][:, :, :], raw[i][:, :, :], ACT.Copy).then_inc(hi_ready[i], 1)

        def low(eng, e, i):
            eng.wait_ge(hi_ready[i], e + 1)
            eng.tensor_tensor(w_lo[i][:, :, :], raw[i][:, :, :], as_f32(w_hi[i][:, :, :]),
                              ALU.subtract).then_inc(lo_ready[i], 1)

        norm(prefetch)
        ps_1, ps_3, ps_y = m.pb("ps_1", [P, 2, TOK]), m.pb("ps_3", [P, 2, TOK]), m.pb("ps_y", [P, 2, D])
        ps_g = m.pb("ps_g", [P, NT, NR])
        ps_w = m.pb("ps_w", [NE, TOK])
        block = ctx.enter_context(nc.Block())

        @block.sync
        def _(sp):
            with sp.Fori(0, NE - 1) as e:
                for i in range(3):
                    sp.wait_ge(lo_ready[i], e + 1)
                    load(sp, e + 1, i)

        @block.scalar
        def _(act):
            act.wait_ge(small_loaded, 16 * 5)
            act.activation(gate_hi[:, :, :], gate_sb[:, :, :], ACT.Copy).then_inc(gate_hi_ready, 1)

            def gate_slice(e, k):
                act.wait_ge(up_done, KT * e + k + 1)
                act.wait_ge(h_ready, KT * e + max(0, k - 1))
                act.activation(gated[:, k % 2, :], ps_1[:, k % 2, :], ACT.Silu,
                               bias=b1_sb[:, e, k:k + 1]).then_inc(gated_ready, 1)

            def high_slice(e, k):
                act.wait_ge(h_ready, KT * e + k + 1)
                act.wait_ge(down_done, NT * e)
                act.activation(h_hi[:, k, :], h32[:, k, :], ACT.Copy).then_inc(h_hi_ready, 1)

            def expert(e, last):
                for k in range(KT):
                    gate_slice(e, k)
                    high_slice(e, k)
                if not last:
                    for i in range(3):
                        split(act, e + 1, i)

            split(act, 0, 0, True)
            split(act, 0, 1, True)
            act.wait_ge(router, 2)
            act.activation(pr[:, :, :], lg[:, :, :], ACT.Exp).then_inc(router_exp, 1)
            split(act, 0, 2, True)
            expert(0, False)
            with act.Fori(1, NE - 1) as e:
                expert(e, False)
            expert(NE - 1, True)

        @block.gpsimd
        def _(pool):
            low(pool, 0, 1)
            with pool.Fori(0, NE - 1) as e:
                low(pool, e, 2)
                low(pool, e + 1, 0)
            low(pool, NE - 1, 2)

        @block.vector
        def _(dve):
            steps = [0]

            def step(ins):
                ins.then_inc(router, 1)
                steps[0] += 1
                dve.wait_ge(router, steps[0])

            def each(ap):
                return ap.unsqueeze(2).to_broadcast([P, NT, NR])

            def hidden(e):
                for k in range(KT):
                    dve.wait_ge(gated_ready, KT * e + k + 1)
                    dve.wait_ge(h_lo_ready, KT * e)
                    dve.scalar_tensor_tensor(out=h32[:, k, :], in0=ps_3[:, k % 2, :], scalar=b3_sb[:, e, k:k + 1],
                                             in1=gated[:, k % 2, :], op0=ALU.add, op1=ALU.mult).then_inc(h_ready, 1)
                    dve.wait_ge(h_hi_ready, KT * e + k + 1)
                    dve.tensor_tensor(h_lo[:, k, :], h32[:, k, :], as_f32(h_hi[:, k, :]), ALU.subtract).then_inc(h_lo_ready, 1)

            dve.wait_ge(gate_hi_ready, 1)
            dve.tensor_tensor(gate_lo[:, :, :], gate_sb[:, :, :], as_f32(gate_hi[:, :, :]), ALU.subtract).then_inc(gate_ready, 1)
            low(dve, 0, 0)
            dve.wait_ge(small_loaded, 16 * 5)
            dve.wait_ge(logits_done, 1)
            dve.tensor_copy(logitsT[:, :], ps_w[0:NR, :]).then_inc(logitsT_ready, 1)
            dve.wait_ge(logits_turned, 1)
            step(dve.tensor_reduce(rmax[:, :], ps_g[:, :, :], AX_X, ALU.max))
            step(dve.tensor_tensor(lg[:, :, :], ps_g[:, :, :], each(rmax[:, :]), ALU.subtract))
            dve.wait_ge(router_exp, 1)
            step(dve.tensor_reduce(rsum[:, :], pr[:, :, :], AX_X, ALU.add))
            step(dve.reciprocal(rinv[:, :], rsum[:, :]))
            step(dve.tensor_tensor(pr[:, :, :], pr[:, :, :], each(rinv[:, :]), ALU.mult))
            for t in range(NT):
                other = pr[:, t, :].unsqueeze(1).to_broadcast([P, NR, NR])
                own = pr[:, t, :].unsqueeze(2).to_broadcast([P, NR, NR])
                step(dve.tensor_tensor(beats[:, t, :, :], other, own, ALU.is_gt))
                step(dve.tensor_tensor(ties[:, t, :, :], other, own, ALU.is_equal))
                step(dve.tensor_tensor(ties[:, t, :, :], ties[:, t, :, :], before_sb[:, :, :], ALU.mult))
            step(dve.tensor_tensor(beats[:, :, :, :], beats[:, :, :, :], ties[:, :, :, :], ALU.add))
            step(dve.tensor_reduce(rank[:, :, :], beats[:, :, :, :], AX_X, ALU.add))
            step(dve.tensor_scalar(chosen[:, :, :], rank[:, :, :], 2.0, None, ALU.is_lt))
            step(dve.memset(weight[:, NR, :], 1.0))
            dve.tensor_tensor(weight[:, 0:NR, :].rearrange("p e t -> p t e"), pr[:, :, :], chosen[:, :, :],
                              ALU.mult).then_inc(weight_ready, 1)
            hidden(0)
            dve.wait_ge(weight_turned, 1)
            dve.tensor_copy(weightT[:, :], ps_w[:, :]).then_inc(weightT_ready, 1)

            def add(e, last):
                for t in range(NT):
                    if t == 2 and not last:
                        low(dve, e + 1, 1)
                    dve.wait_ge(down_done, NT * e + t + 1)
                    dve.wait_ge(x_ready, NT * e)
                    dve.scalar_tensor_tensor(out=x[:, t, :], in0=ps_y[:, t % 2, :], scalar=weight[:, e, t:t + 1],
                                             in1=x[:, t, :], op0=ALU.mult, op1=ALU.add).then_inc(x_ready, 1)

            add(0, False)
            hidden(1)
            with dve.Fori(1, NE - 2) as e:
                add(e, False)
                hidden(e + 1)
            add(NE - 2, False)
            dve.wait_ge(x_ready, NT * (NE - 1))
            for t in range(NT):
                dve.wait_ge(bias_done, t + 1)
                dve.tensor_tensor(x[:, t, :], x[:, t, :], ps_y[:, t % 2, :], ALU.add).then_inc(bias_added, 1)
            hidden(NE - 1)
            dve.wait_ge(bias_added, NT)
            add(NE - 1, True)

        @block.tensor
        def _(pe):
            pe.wait_ge(gate_ready, 1)
            for k in range(KT):
                for n, (w, a) in enumerate(three(gate_hi[:, k, :], gate_lo[:, k, :], xT_hi[:, k, :], xT_lo[:, k, :])):
                    mm = pe.matmul(ps_w[0:NR, :], w, a, start=(k == 0 and n == 0), stop=(k == KT - 1 and n == 2))
            mm.then_inc(logits_done, 1)
            pe.wait_ge(logitsT_ready, 1)
            for t in range(NT):
                mm = pe.transpose(ps_g[:, t, :], logitsT[:, t * P:(t + 1) * P], ident[0:NR, 0:NR])
            mm.then_inc(logits_turned, 1)

            def up(e):
                for k in range(KT):
                    pe.wait_ge(h_ready, KT * e + max(0, k - 1))
                    cols = slice(P * k, P * k + P)
                    for i, ps in ((0, ps_1), (1, ps_3)):
                        if k == 0:
                            pe.wait_ge(lo_ready[i], e + 1)
                        for j in range(KT):
                            for n, (w, a) in enumerate(three(w_hi[i][:, j, cols], w_lo[i][:, j, cols], xT_hi[:, j, :], xT_lo[:, j, :])):
                                mm = pe.matmul(ps[:, k % 2, :], w, a, start=(j == 0 and n == 0), stop=(j == KT - 1 and n == 2))
                    mm.then_inc(up_done, 1)

            def down(e):
                pe.wait_ge(lo_ready[2], e + 1)
                for t0 in (0, 2):
                    for t, js in ((t0, range(KT - 1)), (t0 + 1, range(KT - 1)), (t0, (KT - 1,)), (t0 + 1, (KT - 1,))):
                        if js[0] == 0:
                            pe.wait_ge(x_ready, NT * e + max(0, t - 1))
                        tok = slice(t * P, t * P + P)
                        for j in js:
                            if t == 0:
                                pe.wait_ge(h_lo_ready, KT * e + j + 1)
                            for n, (a, w) in enumerate(three(h_hi[:, j, tok], h_lo[:, j, tok], w_hi[2][:, j, :], w_lo[2][:, j, :])):
                                mm = pe.matmul(ps_y[:, t % 2, :], a, w, start=(j == 0 and n == 0), stop=(j == KT - 1 and n == 2))
                        if js[-1] == KT - 1:
                            mm.then_inc(down_done, 1)

            up(0)
            pe.wait_ge(weight_ready, 1)
            for t in range(NT):
                mm = pe.transpose(ps_w[:, t * P:(t + 1) * P], weight[:, :, t], ident[:, :])
            mm.then_inc(weight_turned, 1)
            down(0)
            up(1)
            with pe.Fori(1, NE - 2) as e:
                down(e)
                up(e + 1)
            down(NE - 2)
            pe.wait_ge(small_loaded, 16 * 5)
            pe.wait_ge(weightT_ready, 1)
            for t in range(NT):
                if t < 2:
                    pe.wait_ge(x_ready, NT * (NE - 1) - 1 + t)
                else:
                    pe.wait_ge(bias_added, t - 1)
                pe.matmul(ps_y[:, t % 2, :], weightT[:, t * P:(t + 1) * P], b2_sb[:, :], start=True, stop=True).then_inc(bias_done, 1)
            up(NE - 1)
            pe.wait_ge(bias_added, NT)
            down(NE - 1)


def project_queries(nc, stage, norm, q, xT_hi, xT_lo, weights, sources, wq_hi, wq_lo, biases, loads_ahead):
    with ExitStack() as ctx:
        m = Memory(nc, ctx, stage)
        halves = [(wq_hi, wq_lo), *weights]
        raw = [m.sb(f"raw{i}", [P, KT, D]) for i in range(3)]
        loaded, hi_ready, lo_ready = m.sems("loaded", 3), m.sems("hi_ready", 3), m.sems("lo_ready", 3)
        bias_loaded, done, q_ready = m.sem("bias_loaded"), m.sem("done"), m.sem("q_ready")

        def prefetch(sp):
            for i in range(3):
                sp.dma_start(raw[i][:, :, :], sources[i]).then_inc(loaded[i], 16)
            for to, of in biases:
                sp.dma_start(to, of).then_inc(bias_loaded, 16)
            loads_ahead(sp)

        def split(act, i):
            hi = halves[i][0]
            act.wait_ge(loaded[i], 16)
            act.activation(hi[:, :, :], raw[i][:, :, :], ACT.Copy).then_inc(hi_ready[i], 1)

        def low(pool, i):
            hi, lo = halves[i]
            pool.wait_ge(hi_ready[i], 1)
            pool.tensor_tensor(lo[:, :, :], raw[i][:, :, :], as_f32(hi[:, :, :]), ALU.subtract).then_inc(lo_ready[i], 1)

        norm(prefetch, lambda act: split(act, 0), lambda pool: low(pool, 0))
        ps = m.pb("ps", [P, NG, TOK])
        block = ctx.enter_context(nc.Block())

        @block.scalar
        def _(act):
            split(act, 1)
            split(act, 2)

        @block.gpsimd
        def _(pool):
            low(pool, 2)

        @block.tensor
        def _(pe):
            pe.wait_ge(lo_ready[0], 1)
            for g in range(NG):
                for k in range(KT):
                    cols = slice(P * g, P * g + P)
                    for n, (w, a) in enumerate(three(wq_hi[:, k, cols], wq_lo[:, k, cols], xT_hi[:, k, :], xT_lo[:, k, :])):
                        mm = pe.matmul(ps[:, g, :], w, a, start=(k == 0 and n == 0), stop=(k == KT - 1 and n == 2))
                mm.then_inc(done, 1)

        @block.vector
        def _(dve):
            low(dve, 1)
            dve.wait_ge(bias_loaded, 16 * len(biases))
            for g in range(NG):
                dve.wait_ge(done, g + 1)
                dve.tensor_scalar(q[:, g, :], ps[:, g, :], biases[0][0][:, g:g + 1], 1.0 / sqrt(DH), ALU.add, ALU.mult).then_inc(q_ready, 1)


def load_chunk(sp, b, c, raw_T, ctxT, T_loaded):
    cols = slice(CH0[c], CH0[c] + CHW[c])
    sp.dma_start(raw_T[:, c % 2, :, 0:CHW[c]], ctxT[b, :, :, cols]).then_inc(T_loaded[c % 2], 16)


def masked_context_attention(nc, stage, q, ident, wk, wv, bk, bv, raw_T, T_loaded, ctxT, mask, gain, load_after):
    with ExitStack() as ctx:
        m = Memory(nc, ctx, stage)
        (wk_hi, wk_lo), (wv_hi, wv_lo) = wk, wv
        HV = 2
        VC = D // HV
        VSLOTS = 3
        RING = 4
        T_hi, T_lo = m.sb("T_hi", [P, KT, S2P], F32R), m.sb("T_lo", [P, KT, S2P], F32R)
        k_hi, k_lo = m.sb("k_hi", [P, S2P], F32R), m.sb("k_lo", [P, S2P], F32R)
        v_sum = m.sb("v_sum", [P, VSLOTS, VC])
        v_pair = m.sb("v_pair", [P, NJ, 4, P], F32R)
        qb_hi, qb_lo = m.sb("qb_hi", [P, NG, P], F32R), m.sb("qb_lo", [P, NG, P], F32R)
        pr = m.sb("pr", [P, 2, S2])
        mask_sb = m.sb("mask", [P, S2], I32)
        neg = m.sb("neg", [P, S2])
        gn = m.sb("gn", [P, S2])
        cmax = m.sb("cmax", [P, 2, 4])
        rmax, nmax, rsum, rinv = m.sb("rmax", [P, 2]), m.sb("nmax", [P, 2]), m.sb("rsum", [P, 2]), m.sb("rinv", [P, 2])
        pT = m.sb("pT", [P, RING, 4, 2 * P], F32R)
        o_high = m.sb("o_high", [S, 2, 2, S])
        o_low = m.sb("o_low", [S, 2, S])
        ps_p = m.pb("ps_p", [P, 3, 512])
        ps_r = m.pb("ps_r", [P, RING, 512])
        ps_o = m.pb("ps_o", [P, 2, 2 * P])

        n_p = NG * 4 + HV * NJ
        assert n_p % 3 == 0
        T_hi_ready, T_split = m.sem("T_hi_ready"), m.sems("T_split", 4)
        mask_loaded, gain_loaded, neg_ready = m.sem("mask_loaded"), m.sem("gain_loaded"), m.sem("neg_ready")
        zero_ready, qb_hi_ready, qb_ready = m.sem("zero_ready"), m.sem("qb_hi_ready"), m.sem("qb_ready")
        proj_done, proj_free, k_hi_ready = m.sem("proj_done"), m.sems("proj_free", 3), m.sem("k_hi_ready")
        v_hi_ready, v_ready = m.sem("v_hi_ready"), m.sem("v_ready")
        scores_done, masked, rmax_ready, nmax_ready, exp_ready, rinv_ready, share_ready = (
            m.sems(n, 2) for n in ("scores_done", "masked", "rmax_ready", "nmax_ready", "exp_ready", "rinv_ready", "share_ready"))
        turned, pT_hi_ready, pT_ready, pT_used = m.sem("turned"), m.sem("pT_hi_ready"), m.sem("pT_ready"), m.sem("pT_used")
        o_ready, o_part_ready, att_ready = (m.sem(n) for n in ("o_ready", "o_part_ready", "att_ready"))
        waited = m.sems("waited", 3)
        block = ctx.enter_context(nc.Block())

        order = [("k", 0, c) for c in range(4)] + [("v", 0, j) for j in range(NJ)]
        order += [("k", g, c) for g in range(1, NG) for c in range(4)] + [("v", 1, j) for j in range(NJ)]
        use_of = {what: n for n, what in enumerate(order)}
        last_of = [(CH0[c] + CHV[c] - 1) // P for c in range(4)]

        def freed(b, u):
            return b * (n_p // 3) + u // 3 + 1

        def tiles(n):
            j0, j1 = JG[n % 4]
            return j0, j1, JR[j0]

        def chunk(c):
            return slice(CH0[c], CH0[c] + CHW[c])

        @block.sync
        def _(sp):
            def load_T(b, c):
                load_chunk(sp, b, c, raw_T, ctxT, T_loaded)

            def load_mask(b):
                sp.dma_start(mask_sb[0:S, :], mask[b]).then_inc(mask_loaded, 16)
                sp.dma_start(mask_sb[S:P, :], mask[b]).then_inc(mask_loaded, 16)

            def load_gain(b):
                sp.dma_start(gn[0:S, :], gain[b]).then_inc(gain_loaded, 16)
                sp.dma_start(gn[S:P, :], gain[b]).then_inc(gain_loaded, 16)

            load_mask(0)
            for c in (2, 3):
                sp.wait_ge(T_split[c - 2], 1)
                load_T(0, c)
            load_gain(0)
            with sp.Fori(0, B - 1) as b:
                for c in range(4):
                    if c == 2:
                        sp.wait_ge(neg_ready, b + 1)
                        load_mask(b + 1)
                    sp.wait_ge(T_split[(c + 2) % 4], b + 1 + c // 2)
                    load_T(b + 1, c)
                for i in range(2):
                    sp.wait_ge(share_ready[i], NG * (b + 1))
                load_gain(b + 1)
            for c in (2, 3):
                sp.wait_ge(T_split[c], B)
            load_after(sp)

        @block.scalar
        def _(act):
            def split_T(b, c):
                act.wait_ge(T_loaded[c % 2], 16 * (2 * b + c // 2 + 1))
                act.activation(T_hi[:, :, chunk(c)], raw_T[:, c % 2, :, 0:CHW[c]], ACT.Copy).then_inc(T_hi_ready, 1)

            def queries_high(b):
                for i in range(2):
                    act.wait_ge(scores_done[i], 4 * NG * b)
                for h in range(HG):
                    rows, cols = slice(DH * h, DH * h + DH), slice(S * (h % 2), S * (h % 2) + S)
                    if h == 0:
                        act.sem_inc(waited[0], 1)
                    act.activation(qb_hi[rows, :, cols], q[rows, :, bass.ts(b, S)], ACT.Copy).then_inc(qb_hi_ready, 1)

            def keys_high(b, g, c):
                u = use_of["k", g, c]
                for i in range(2):
                    act.wait_ge(scores_done[i], 4 * (NG * b + g))
                act.wait_ge(proj_done, n_p * b + u + 1)
                act.activation(k_hi[:, chunk(c)], ps_p[:, u % 3, 0:CHW[c]], ACT.Identity,
                               bias=bk[:, g:g + 1]).then_inc(k_hi_ready, 1)

            def values_high(b, half, j):
                u, r = use_of["v", half, j], JR[j]
                if j == 0:
                    act.wait_ge(pT_used, 32 * b + 16 * half)
                act.wait_ge(proj_free[u % 3], freed(b, u))
                act.activation(v_pair[0:r, j, :, 0:S], v_sum[0:r, j % VSLOTS, :].rearrange("p (a c) -> p a c", c=S),
                               ACT.Copy).then_inc(v_hi_ready, 1)

            def exps(b, g):
                for i in range(2):
                    act.wait_ge(nmax_ready[i], NG * b + g + 1)
                    act.activation(pr[:, i, :], pr[:, i, :], ACT.Exp, bias=nmax[:, i:i + 1],
                                   accum_out=rsum[:, i:i + 1]).then_inc(exp_ready[i], 1)

            def turned_high(b, g, first, end):
                for n in range(first, end):
                    j0, j1, r = tiles(n)
                    act.wait_ge(turned, 32 * b + 8 * g + n + 1)
                    act.wait_ge(pT_used, 32 * b + 8 * g + max(0, n - RING + 1))
                    act.activation(pT[0:r, n % RING, 0:j1 - j0, 0:P],
                                   ps_r[0:r, n % RING, 0:(j1 - j0) * P].rearrange("p (j c) -> p j c", c=P),
                                   ACT.Copy).then_inc(pT_hi_ready, 1)

            def outputs(b, g):
                act.wait_ge(pT_used, 32 * b + 8 * (g + 1))
                act.wait_ge(att_ready, HG * (NG * b + g))
                for h in range(2):
                    rows = slice(DH * h, DH * h + DH)
                    own = ps_o[rows, :, :].rearrange("p i (a c) -> p i a c", c=P)[:, :, :, S * h:S * h + S]
                    act.activation(o_high[rows, :, :, :], own, ACT.Copy).then_inc(o_ready, 1)
                    act.activation(o_low[rows, :, :], ps_o[S + DH * h:S + DH * h + DH, :, S * h:S * h + S],
                                   ACT.Copy).then_inc(o_ready, 1)

            def keys_and_turned(key_b, key_g, b, g):
                for c in range(3):
                    keys_high(key_b, key_g, c)
                    if key_g == 0 and c == 1:
                        queries_high(key_b)
                turned_high(b, g, 0, 2)
                keys_high(key_b, key_g, 3)
                turned_high(b, g, 2, 8)

            def batch(b, last):
                exps(b, 0)
                for j in range(NJ):
                    values_high(b, 0, j)
                keys_and_turned(b, 1, b, 0)
                outputs(b, 0)
                for g in (1, 2):
                    exps(b, g)
                    if g == 1:
                        keys_and_turned(b, 2, b, 1)
                    else:
                        for c in range(4):
                            keys_high(b, 3, c)
                        for j in range(NJ):
                            if j == NJ - 1:
                                turned_high(b, 2, 0, 2)
                            values_high(b, 1, j)
                            if j in last_of[:3] and not last:
                                act.wait_ge(proj_done, n_p * b + use_of["v", 1, j] + 1)
                                split_T(b + 1, last_of.index(j))
                        turned_high(b, 2, 2, 8)
                    outputs(b, g)
                if not last:
                    act.wait_ge(proj_done, n_p * (b + 1))
                    split_T(b + 1, 3)
                exps(b, 3)
                if last:
                    turned_high(b, 3, 0, 8)
                else:
                    keys_and_turned(b + 1, 0, b, 3)
                outputs(b, 3)

            act.wait_ge(zero_ready, 2)
            for c in range(4):
                split_T(0, c)
            queries_high(0)
            for c in range(4):
                keys_high(0, 0, c)
            batch(0, False)
            with act.Fori(1, B - 1) as b:
                batch(b, False)
            batch(B - 1, True)

        @block.gpsimd
        def _(pool):
            def added_mask(b):
                for i in range(2):
                    pool.wait_ge(masked[i], 4 * NG * b)
                pool.wait_ge(mask_loaded, 32 * (b + 1))
                pool.wait_ge(v_ready, 2 * NJ * b)
                pool.sem_inc(waited[1], 1)
                pool.tensor_scalar(neg[:, :], mask_sb[:, :], -1.0, 1.0e9, ALU.add, ALU.mult).then_inc(neg_ready, 1)

            def queries_low(b):
                pool.wait_ge(qb_hi_ready, HG * (b + 1))
                pool.wait_ge(neg_ready, b + 1)
                for h in range(HG):
                    rows, cols = slice(DH * h, DH * h + DH), slice(S * (h % 2), S * (h % 2) + S)
                    if h:
                        pool.wait_ge(qb_ready, HG * b + h)
                    pool.sem_inc(waited[1], 1)
                    pool.tensor_tensor(qb_lo[rows, :, cols], q[rows, :, bass.ts(b, S)], as_f32(qb_hi[rows, :, cols]),
                                       ALU.subtract).then_inc(qb_ready, 1)
                pool.wait_ge(qb_ready, HG * (b + 1))

            def values_low(b, half):
                for j in range(NJ):
                    r = JR[j]
                    pool.wait_ge(v_hi_ready, 2 * NJ * b + NJ * half + j + 1)
                    pool.tensor_tensor(v_pair[0:r, j, :, S:P], v_sum[0:r, j % VSLOTS, :].rearrange("p (a c) -> p a c", c=S),
                                       as_f32(v_pair[0:r, j, :, 0:S]), ALU.subtract).then_inc(v_ready, 1)

            def split_T(b, c):
                pool.wait_ge(T_hi_ready, 4 * b + c + 1)
                pool.tensor_tensor(T_lo[:, :, chunk(c)], raw_T[:, c % 2, :, 0:CHW[c]], as_f32(T_hi[:, :, chunk(c)]),
                                   ALU.subtract).then_inc(T_split[c], 1)

            def outputs(b, g):
                n = NG * b + g
                pool.wait_ge(o_ready, 4 * n + 4)
                for h in range(2):
                    rows = slice(DH * h, DH * h + DH)
                    if h:
                        pool.wait_ge(o_part_ready, 2 * n + 1)
                    pool.tensor_tensor(o_low[rows, :, :], o_high[rows, :, 0, :], o_low[rows, :, :], ALU.add).then_inc(o_part_ready, 1)
                pool.wait_ge(o_part_ready, 2 * n + 2)
                for i in range(2):
                    for h in range(2):
                        rows = slice(DH * h, DH * h + DH)
                        to = slice(S * i + DH * h, S * i + DH * h + DH)
                        if i or h:
                            pool.wait_ge(att_ready, 4 * n + 2 * i + h)
                        pool.sem_inc(waited[1], 1)
                        pool.tensor_tensor(q[to, g, bass.ts(b, S)], o_high[rows, i, 1, :],
                                           o_low[rows, i, :], ALU.add).then_inc(att_ready, 1)
                pool.wait_ge(att_ready, 4 * n + 4)

            def batch(b, last):
                values_low(b, 0)
                outputs(b, 0)
                outputs(b, 1)
                values_low(b, 1)
                pool.wait_ge(v_ready, 2 * NJ * (b + 1))
                if not last:
                    split_T(b + 1, 2)
                    pool.wait_ge(T_split[2], b + 2)
                outputs(b, 2)
                if not last:
                    split_T(b + 1, 3)
                    added_mask(b + 1)
                    queries_low(b + 1)
                outputs(b, 3)

            pool.memset(as_f32(qb_hi[:, :, :]), 0.0).then_inc(zero_ready, 1)
            pool.memset(as_f32(qb_lo[:, :, :]), 0.0).then_inc(zero_ready, 1)
            pool.wait_ge(zero_ready, 2)
            split_T(0, 2)
            split_T(0, 3)
            added_mask(0)
            queries_low(0)
            batch(0, False)
            with pool.Fori(1, B - 1) as b:
                batch(b, False)
            batch(B - 1, True)

        @block.vector
        def _(dve):
            def split_T(b, c):
                dve.wait_ge(T_hi_ready, 4 * b + c + 1)
                dve.tensor_tensor(T_lo[:, :, chunk(c)], raw_T[:, c % 2, :, 0:CHW[c]], as_f32(T_hi[:, :, chunk(c)]),
                                  ALU.subtract).then_inc(T_split[c], 1)

            def keys_low(b, g, c):
                u = use_of["k", g, c]
                dve.wait_ge(k_hi_ready, 4 * (NG * b + g) + c + 1)
                dve.scalar_tensor_tensor(out=k_lo[:, chunk(c)], in0=ps_p[:, u % 3, 0:CHW[c]], scalar=bk[:, g:g + 1],
                                         in1=as_f32(k_hi[:, chunk(c)]), op0=ALU.add, op1=ALU.subtract).then_inc(proj_free[u % 3], 1)

            def values(b, half, j):
                u, r = use_of["v", half, j], JR[j]
                dve.wait_ge(proj_done, n_p * b + u + 1)
                dve.wait_ge(v_ready, 2 * NJ * b + NJ * half + max(0, j - VSLOTS + 1))
                dve.tensor_tensor(v_sum[0:r, j % VSLOTS, :], ps_p[0:r, u % 3, 0:VC], bv[0:r, VC * half:VC * half + VC],
                                  ALU.add).then_inc(proj_free[u % 3], 1)

            def mask_scores(b, g):
                dve.wait_ge(neg_ready, b + 1)
                dve.wait_ge(turned, 32 * b + 8 * g)
                for i in range(2):
                    for c in range(4):
                        cols = slice(CH0[c], CH0[c] + CHV[c])
                        dve.wait_ge(scores_done[i], 4 * (NG * b + g) + c + 1)
                        dve.sem_inc(waited[2], 1)
                        dve.tensor_tensor_reduce(pr[:, i, cols], ps_r[:, c, 0:CHV[c]], neg[:, cols],
                                                 1.0, LOW, ALU.add, ALU.max, cmax[:, i, c:c + 1]).then_inc(masked[i], 1)
                    dve.wait_ge(masked[i], 4 * (NG * b + g + 1))
                    dve.tensor_reduce(rmax[:, i:i + 1], cmax[:, i, :], AX_X, ALU.max).then_inc(rmax_ready[i], 1)
                    dve.wait_ge(rmax_ready[i], NG * b + g + 1)
                    dve.tensor_scalar(nmax[:, i:i + 1], rmax[:, i:i + 1], -1.0, None, ALU.mult).then_inc(nmax_ready[i], 1)

            def shares(b, g, i):
                dve.wait_ge(exp_ready[i], NG * b + g + 1)
                dve.reciprocal(rinv[:, i:i + 1], rsum[:, i:i + 1]).then_inc(rinv_ready[i], 1)
                dve.wait_ge(gain_loaded, 32 * (b + 1))
                dve.wait_ge(rinv_ready[i], NG * b + g + 1)
                dve.scalar_tensor_tensor(out=pr[:, i, :], in0=pr[:, i, :], scalar=rinv[:, i:i + 1],
                                         in1=gn[:, :], op0=ALU.mult, op1=ALU.mult).then_inc(share_ready[i], 1)

            def turned_low(b, g, first, end):
                for n in range(first, end):
                    j0, j1, r = tiles(n)
                    dve.wait_ge(pT_hi_ready, 32 * b + 8 * g + n + 1)
                    dve.tensor_tensor(pT[0:r, n % RING, 0:j1 - j0, P:2 * P],
                                      ps_r[0:r, n % RING, 0:(j1 - j0) * P].rearrange("p (j c) -> p j c", c=P),
                                      as_f32(pT[0:r, n % RING, 0:j1 - j0, 0:P]), ALU.subtract).then_inc(pT_ready, 1)

            def shares_and_keys(b, g, next_b, next_g):
                shares(b, g, 0)
                keys_low(next_b, next_g, 0)
                shares(b, g, 1)
                keys_low(next_b, next_g, 1)
                keys_low(next_b, next_g, 2)
                if g != 2:
                    keys_and_turned(next_b, next_g, b, g)
                else:
                    keys_low(next_b, next_g, 3)

            def keys_and_turned(key_b, key_g, b, g):
                turned_low(b, g, 0, 2)
                keys_low(key_b, key_g, 3)
                turned_low(b, g, 2, 8)

            def batch(b, last):
                values(b, 0, 0)
                values(b, 0, 1)
                shares(b, 0, 0)
                values(b, 0, 2)
                shares(b, 0, 1)
                for j in range(3, NJ):
                    values(b, 0, j)
                for c in range(3):
                    keys_low(b, 1, c)
                keys_and_turned(b, 1, b, 0)
                mask_scores(b, 1)
                for g in (1, 2):
                    shares_and_keys(b, g, b, g + 1)
                    if g == 2:
                        for j in range(NJ):
                            if j == NJ - 1:
                                turned_low(b, 2, 0, 2)
                            values(b, 1, j)
                            if j - 2 in last_of[:2] and not last:
                                split_T(b + 1, last_of.index(j - 2))
                        turned_low(b, 2, 2, 8)
                    mask_scores(b, g + 1)
                if last:
                    shares(b, 3, 0)
                    shares(b, 3, 1)
                    turned_low(b, 3, 0, 8)
                else:
                    shares_and_keys(b, 3, b + 1, 0)
                    mask_scores(b + 1, 0)

            for c in range(2):
                split_T(0, c)
            for c in range(4):
                keys_low(0, 0, c)
            mask_scores(0, 0)
            batch(0, False)
            with dve.Fori(1, B - 1) as b:
                batch(b, False)
            batch(B - 1, True)

        @block.tensor
        def _(pe):
            def bank(b, u):
                pe.wait_ge(proj_free[u % 3], b * (n_p // 3) + u // 3)
                return ps_p[:, u % 3, :]

            def keys(b, g, turn_for=None):
                for c in range(4):
                    if c == 3 and turn_for:
                        first_turns(*turn_for)
                    full = bank(b, use_of["k", g, c])
                    if g == 0:
                        pe.wait_ge(T_split[c], b + 1)
                    for k in range(KT):
                        cols = slice(P * g, P * g + P)
                        for n, (a, t) in enumerate(three(wk_hi[:, k, cols], wk_lo[:, k, cols], T_hi[:, k, chunk(c)], T_lo[:, k, chunk(c)])):
                            mm = pe.matmul(full[:, 0:CHW[c]], a, t, start=(k == 0 and n == 0), stop=(k == KT - 1 and n == 2))
                    mm.then_inc(proj_done, 1)

            def values(b, half, turn_for=None):
                for j in range(NJ):
                    if j == NJ - 1 and turn_for:
                        first_turns(*turn_for)
                    full = bank(b, use_of["v", half, j])
                    r = JR[j]
                    for k in range(KT):
                        rows, cols = slice(P * j, P * j + r), slice(VC * half, VC * half + VC)
                        for n, (t, w) in enumerate(three(T_hi[:, k, rows], T_lo[:, k, rows], wv_hi[:, k, cols], wv_lo[:, k, cols])):
                            mm = pe.matmul(full[0:r, 0:VC], t, w, start=(k == 0 and n == 0), stop=(k == KT - 1 and n == 2))
                    mm.then_inc(proj_done, 1)

            def scores(b, g, i, c):
                if i == 0:
                    if g == 0 and c == 0:
                        pe.wait_ge(qb_ready, HG * (b + 1))
                    u = use_of["k", g, c]
                    pe.wait_ge(proj_free[u % 3], freed(b, u))
                else:
                    pe.wait_ge(masked[0], 4 * (NG * b + g) + c + 1)
                r = slice(S * i, S * i + S)
                for n, (a, t) in enumerate(three(qb_hi[r, g, :], qb_lo[r, g, :], k_hi[r, chunk(c)], k_lo[r, chunk(c)])):
                    mm = pe.matmul(ps_r[:, c, 0:CHW[c]], a, t, start=(n == 0), stop=(n == 2))
                mm.then_inc(scores_done[i], 1)

            def first_turns(b, g):
                turn(b, g, 0)
                turn(b, g, 1)

            def turn(b, g, n):
                j0, j1, r = tiles(n)
                if n % 4 == 0:
                    pe.wait_ge(share_ready[n // 4], NG * b + g + 1)
                if n >= RING:
                    pe.wait_ge(pT_ready, 32 * b + 8 * g + n - RING + 1)
                for j in range(j0, j1):
                    mm = pe.transpose(ps_r[0:r, n % RING, (j - j0) * P:(j - j0 + 1) * P], pr[:, n // 4, j * P:j * P + r], ident[:, :])
                mm.then_inc(turned, 1)

            def multiply(b, g, n):
                j0, j1, r = tiles(n)
                pe.wait_ge(pT_ready, 32 * b + 8 * g + n + 1)
                if n < 4:
                    pe.wait_ge(v_ready, 2 * NJ * b + NJ * (g // 2) + j1)
                for j in range(j0, j1):
                    mm = pe.matmul(ps_o[:, n // 4, :], v_pair[0:r, j, 2 * (g % 2) + n // 4, :], pT[0:r, n % RING, j - j0, :],
                                   start=(j == 0), stop=(j == NJ - 1))
                mm.then_inc(pT_used, 1)

            def outputs_and_scores(b, g, after, turned_ahead=2):
                pe.wait_ge(o_ready, 4 * (NG * b + g))
                for n in range(turned_ahead, 8):
                    if n >= RING:
                        multiply(b, g, n - RING)
                    turn(b, g, n)
                multiply(b, g, 4)
                multiply(b, g, 5)
                if after:
                    scores(*after, 0, 0)
                    scores(*after, 0, 1)
                multiply(b, g, 6)
                multiply(b, g, 7)
                if after:
                    for i, c in ((0, 2), (0, 3), (1, 0), (1, 1), (1, 2), (1, 3)):
                        scores(*after, i, c)

            keys(0, 0)
            for i in range(2):
                for c in range(4):
                    scores(0, 0, i, c)

            def batch(b, last):
                values(b, 0)
                keys(b, 1, (b, 0))
                outputs_and_scores(b, 0, (b, 1))
                keys(b, 2, (b, 1))
                outputs_and_scores(b, 1, (b, 2))
                keys(b, 3)
                values(b, 1, (b, 2))
                outputs_and_scores(b, 2, (b, 3))
                if last:
                    outputs_and_scores(b, 3, None, 0)
                else:
                    keys(b + 1, 0, (b, 3))
                    outputs_and_scores(b, 3, (b + 1, 0))

            batch(0, False)
            with pe.Fori(1, B - 1) as b:
                batch(b, False)
            batch(B - 1, True)


def project_attended(nc, stage, x, att, raw, loaded, bias):
    with ExitStack() as ctx:
        m = Memory(nc, ctx, stage)
        a_hi, a_lo = m.sb("a_hi", [P, KT, TOK], F32R), m.sb("a_lo", [P, KT, TOK], F32R)
        w_hi, w_lo = m.sb("w_hi", [P, KT, D], F32R), m.sb("w_lo", [P, KT, D], F32R)
        bo = m.sb("bo", [P, D])
        ps = m.pb("ps", [P, NT, D])
        bo_loaded, a_hi_ready, a_lo_ready, w_hi_ready, w_lo_ready = (m.sem(n) for n in (
            "bo_loaded", "a_hi_ready", "a_lo_ready", "w_hi_ready", "w_lo_ready"))
        done, bias_added, x_ready = m.sem("done"), m.sem("bias_added"), m.sem("x_ready")
        block = ctx.enter_context(nc.Block())

        @block.sync
        def _(sp):
            sp.dma_start(bo[:, :], bias.to_broadcast([P, D])).then_inc(bo_loaded, 16)

        @block.scalar
        def _(act):
            act.wait_ge(loaded, 16)
            for k in range(KT):
                act.activation(a_hi[:, k, :], att[:, k, :], ACT.Copy).then_inc(a_hi_ready, 1)
                act.activation(w_hi[:, k, :], raw[:, k, :], ACT.Copy).then_inc(w_hi_ready, 1)

        @block.vector
        def _(dve):
            for k in range(KT):
                dve.wait_ge(a_hi_ready, k + 1)
                dve.tensor_tensor(a_lo[:, k, :], att[:, k, :], as_f32(a_hi[:, k, :]), ALU.subtract).then_inc(a_lo_ready, 1)
                dve.wait_ge(w_hi_ready, k + 1)
                dve.tensor_tensor(w_lo[:, k, :], raw[:, k, :], as_f32(w_hi[:, k, :]), ALU.subtract).then_inc(w_lo_ready, 1)
            dve.wait_ge(bo_loaded, 16)
            for t in range(NT):
                dve.tensor_tensor(x[:, t, :], x[:, t, :], bo[:, :], ALU.add).then_inc(bias_added, 1)
            for t in range(NT):
                dve.wait_ge(done, t + 1)
                dve.wait_ge(bias_added, t + 1)
                dve.tensor_tensor(x[:, t, :], x[:, t, :], ps[:, t, :], ALU.add).then_inc(x_ready, 1)

        @block.tensor
        def _(pe):
            for t in range(NT):
                tok = slice(t * P, t * P + P)
                for k in range(KT):
                    if t == 0:
                        pe.wait_ge(a_lo_ready, k + 1)
                        pe.wait_ge(w_lo_ready, k + 1)
                    for n, (a, w) in enumerate(three(a_hi[:, k, tok], a_lo[:, k, tok], w_hi[:, k, :], w_lo[:, k, :])):
                        mm = pe.matmul(ps[:, t, :], a, w, start=(k == 0 and n == 0), stop=(k == KT - 1 and n == 2))
                mm.then_inc(done, 1)


def quantized_blocks(nc, stage, norm, x, h, hT_hi, hT_lo, ident, codes, scales, la, lb, bias, gamma, beta, store):
    RANK = 32
    NBK = 3
    GROUP = 16
    GP = P // GROUP
    with ExitStack() as ctx:
        m = Memory(nc, ctx, stage)
        code = m.sb("code", [P, 2, KT, D], I32)
        scale = m.sb("scale", [P, 2, KT, D])
        la_sb, lb_sb = m.sb("la", [RANK, 2, D]), m.sb("lb", [RANK, 2, D])
        w = m.sb("w", [P, 2, KT, D])
        w_hi, w_lo = m.sb("w_hi", [P, 2, KT, D], F32R), m.sb("w_lo", [P, 2, KT, D], F32R)
        bias_sb = m.sb("bias", [P, 2 * NBK, D])
        gamma_sb, beta_sb = m.sb("gamma", [P, NBK, KT]), m.sb("beta", [P, NBK, KT])
        z = m.sb("z", [P, NT, D])
        zT = m.sb("zT", [P, KT, TOK])
        zT_hi, zT_lo = m.sb("zT_hi", [P, KT, TOK], F32R), m.sb("zT_lo", [P, KT, TOK], F32R)
        stats, mv = m.sb("stats", [P, NT, 6]), m.sb("mv", [P, NT, 2])
        var, std, rstd = m.sb("var", [P, NT]), m.sb("std", [P, NT]), m.sb("rstd", [P, NT])
        scratch = m.sb("scratch", [P, 1])

        loaded, rank_loaded, small_loaded = m.sems("loaded", 2), m.sems("rank_loaded", 2), m.sem("small_loaded")
        w_coded, w_scaled, rank_done, w_summed, w_hi_ready, w_ready = (m.sems(n, 2) for n in (
            "w_coded", "w_scaled", "rank_done", "w_summed", "w_hi_ready", "w_ready"))
        y_done, y_read = m.sems("y_done", 2), m.sems("y_read", 2)
        stats_ready, mv_ready, var_ready, std_ready, rstd_ready = (m.sem(n) for n in ("stats_ready", "mv_ready", "var_ready", "std_ready", "rstd_ready"))
        scratch_ready = m.sem("scratch_ready")
        z_ready, gelu_ready, h_biased, x_ready = (m.sem(n) for n in ("z_ready", "gelu_ready", "h_biased", "x_ready"))
        turned, hi_ready, lo_ready = m.sems("turned", 2), m.sems("hi_ready", 2), m.sems("lo_ready", 2)
        waited = m.sems("waited", 2)

        def load(sp, b, s, first=False):
            if not first:
                sp.wait_ge(w_scaled[s], KT * b)
            sp.dma_start(code[:, s, :, :], codes[2 * b + s]).then_inc(loaded[s], 16)
            for k in range(KT):
                rows = scales[2 * b + s, GP * k:GP * k + GP, :].unsqueeze(1).to_broadcast([GP, GROUP, D])
                sp.dma_start(scale[:, s, k, :], rows).then_inc(loaded[s], 16)
            if not first:
                sp.wait_ge(rank_done[s], KT * b)
            sp.dma_start(la_sb[:, s, :], la[2 * b + s]).then_inc(rank_loaded[s], 16)
            sp.dma_start(lb_sb[:, s, :], lb[2 * b + s]).then_inc(rank_loaded[s], 16)

        def prefetch(sp):
            load(sp, 0, 0, True)
            load(sp, 0, 1, True)
            sp.dma_start(gamma_sb[:, :, :], gamma).then_inc(small_loaded, 16)
            sp.dma_start(beta_sb[:, :, :], beta).then_inc(small_loaded, 16)
            for i in range(2 * NBK):
                sp.dma_start(bias_sb[:, i, :], bias[i].to_broadcast([P, D])).then_inc(small_loaded, 16)

        def from_codes(pool, b, s, first=False):
            pool.wait_ge(loaded[s], 16 * (KT + 1) * (b + 1))
            if not first:
                pool.wait_ge(w_ready[s], KT * b)
                pool.sem_inc(waited[0], 1)
            pool.tensor_scalar(w[:, s, :, :], code[:, s, :, :], 1.0 / 7.5, -1.0, ALU.mult, ALU.add).then_inc(w_coded[s], 1)
            pool.wait_ge(w_coded[s], b + 1)
            for k in range(KT):
                pool.tensor_tensor(w[:, s, k, :], w[:, s, k, :], scale[:, s, k, :], ALU.mult).then_inc(w_scaled[s], 1)

        norm(prefetch, None, lambda pool: from_codes(pool, 0, 0, True))
        ps_l, ps_y, ps_t = m.pb("ps_l", [P, 2, D]), m.pb("ps_y", [P, 2, D]), m.pb("ps_t", [P, KT, TOK])
        block = ctx.enter_context(nc.Block())

        @block.sync
        def _(sp):
            with sp.Fori(0, NBK - 1) as b:
                load(sp, b + 1, 0)
                load(sp, b + 1, 1)
            for t in range(NT):
                sp.wait_ge(x_ready, NT + t + 1)
                store(sp, t)

        @block.gpsimd
        def _(pool):
            def low(b, s):
                for k in range(KT):
                    pool.wait_ge(w_hi_ready[s], KT * b + k + 1)
                    pool.tensor_tensor(w_lo[:, s, k, :], w[:, s, k, :], as_f32(w_hi[:, s, k, :]), ALU.subtract).then_inc(w_ready[s], 1)

            def blk(b, last):
                if not last:
                    from_codes(pool, b + 1, 0)
                low(b, 1)
                if not last:
                    from_codes(pool, b + 1, 1)
                    low(b + 1, 0)

            low(0, 0)
            from_codes(pool, 0, 1, True)
            with pool.Fori(0, NBK - 1) as b:
                blk(b, False)
            blk(NBK - 1, True)

        @block.scalar
        def _(act):
            def high(b, s):
                act.wait_ge(y_done[s], NT * b)
                for k in range(KT):
                    act.wait_ge(w_summed[s], KT * b + k + 1)
                    act.activation(w_hi[:, s, k, :], w[:, s, k, :], ACT.Copy).then_inc(w_hi_ready[s], 1)

            def gelu(b):
                for k in range(KT):
                    act.wait_ge(turned[0], KT * b + k + 1)
                    act.sem_inc(waited[1], 1)
                    act.activation(zT[:, k, :], ps_t[:, k, :], ACT.Gelu, bias=beta_sb[:, b, k:k + 1],
                                   scale=gamma_sb[:, b, k:k + 1]).then_inc(gelu_ready, 1)
                    act.wait_ge(gelu_ready, KT * b + k + 1)
                    act.activation(zT_hi[:, k, :], zT[:, k, :], ACT.Copy).then_inc(hi_ready[0], 1)

            def turned_high(b):
                for k in range(KT):
                    act.wait_ge(turned[1], KT * b + k + 1)
                    act.activation(hT_hi[:, k, :], ps_t[:, k, :], ACT.Copy).then_inc(hi_ready[1], 1)

            def blk(b, last):
                high(b, 1)
                act.wait_ge(var_ready, b + 1)
                act.activation(std[:, :], var[:, :], ACT.Sqrt).then_inc(std_ready, 1)
                act.activation(scratch[:, :], var[:, 0:1], ACT.Gelu).then_inc(scratch_ready, 1)
                gelu(b)
                if not last:
                    high(b + 1, 0)
                    turned_high(b)

            high(0, 0)
            act.wait_ge(small_loaded, 16 * (2 * NBK + 2))
            blk(0, False)
            with act.Fori(1, NBK - 1) as b:
                blk(b, False)
            blk(NBK - 1, True)

        @block.vector
        def _(dve):
            def add_rank(b, s, ks):
                for k in ks:
                    dve.wait_ge(w_scaled[s], KT * b + k + 1)
                    dve.wait_ge(rank_done[s], KT * b + k + 1)
                    dve.tensor_tensor(w[:, s, k, :], w[:, s, k, :], ps_l[:, k % 2, :], ALU.add).then_inc(w_summed[s], 1)

            def read_A(b, t):
                dve.wait_ge(y_done[0], NT * b + t + 1)
                dve.wait_ge(turned[0], KT * b)
                dve.tensor_tensor(z[:, t, :], ps_y[:, t % 2, :], bias_sb[:, 2 * b, :], ALU.add).then_inc(y_read[0], 1)
                dve.wait_ge(y_read[0], NT * b + t + 1)
                dve.bn_stats(stats[:, t, :], z[:, t, :]).then_inc(stats_ready, 1)

            def read_B(b, t):
                dve.wait_ge(y_done[1], NT * b + t + 1)
                dve.wait_ge(h_biased, NT * b + t + 1)
                dve.tensor_tensor(h[:, t, :], h[:, t, :], ps_y[:, t % 2, :], ALU.add).then_inc(y_read[1], 1)

            def blk(b, last):
                for t in range(NT):
                    if t == 2:
                        add_rank(b, 1, (2, 3))
                    read_A(b, t)
                    if t < NT - 1:
                        dve.tensor_tensor(h[:, t, :], h[:, t, :], bias_sb[:, 2 * b + 1, :], ALU.add).then_inc(h_biased, 1)
                dve.wait_ge(stats_ready, NT * (b + 1))
                dve.tensor_tensor(h[:, NT - 1, :], h[:, NT - 1, :], bias_sb[:, 2 * b + 1, :], ALU.add).then_inc(h_biased, 1)
                for t in range(NT):
                    dve.bn_aggr(mv[:, t, :], stats[:, t, :]).then_inc(mv_ready, 1)
                dve.wait_ge(mv_ready, NT * (b + 1))
                dve.tensor_scalar(var[:, :], mv[:, :, 1], EPS, None, ALU.add).then_inc(var_ready, 1)
                dve.wait_ge(std_ready, b + 1)
                dve.reciprocal(rstd[:, :], std[:, :]).then_inc(rstd_ready, 1)
                dve.wait_ge(rstd_ready, b + 1)
                for t in range(NT):
                    dve.tensor_scalar(z[:, t, :], z[:, t, :], mv[:, t, 0:1], rstd[:, t:t + 1],
                                      ALU.subtract, ALU.mult).then_inc(z_ready, 1)
                for k in range(KT):
                    dve.wait_ge(hi_ready[0], KT * b + k + 1)
                    dve.tensor_tensor(zT_lo[:, k, :], zT[:, k, :], as_f32(zT_hi[:, k, :]), ALU.subtract).then_inc(lo_ready[0], 1)
                if last:
                    dve.wait_ge(h_biased, NT * NBK)
                    for t in range(NT):
                        dve.tensor_tensor(x[:, t, :], x[:, t, :], h[:, t, :], ALU.add).then_inc(x_ready, 1)
                    for t in range(NT):
                        dve.wait_ge(y_done[1], NT * b + t + 1)
                        dve.wait_ge(x_ready, t + 1)
                        dve.tensor_tensor(x[:, t, :], x[:, t, :], ps_y[:, t % 2, :], ALU.add).then_inc(x_ready, 1)
                else:
                    add_rank(b + 1, 0, (0, 1))
                    for t in range(NT):
                        if t == 2:
                            add_rank(b + 1, 0, (2, 3))
                        read_B(b, t)
                    for k in range(KT):
                        dve.wait_ge(hi_ready[1], KT * b + k + 1)
                        dve.tensor_tensor(hT_lo[:, k, :], ps_t[:, k, :], as_f32(hT_hi[:, k, :]), ALU.subtract).then_inc(lo_ready[1], 1)
                    add_rank(b + 1, 1, (0, 1))

            add_rank(0, 0, range(KT))
            add_rank(0, 1, (0, 1))
            dve.wait_ge(small_loaded, 16 * (2 * NBK + 2))
            blk(0, False)
            with dve.Fori(1, NBK - 1) as b:
                blk(b, False)
            blk(NBK - 1, True)

        @block.tensor
        def _(pe):
            def rank_product(b, s, ks):
                for k in ks:
                    if k == 0:
                        pe.wait_ge(rank_loaded[s], 32 * (b + 1))
                    if k >= 2:
                        pe.wait_ge(w_summed[s], KT * b + k - 1)
                    elif s:
                        pe.wait_ge(w_summed[0], KT * (b + 1))
                    else:
                        pe.wait_ge(w_summed[1], KT * b)
                    pe.matmul(ps_l[:, k % 2, :], la_sb[:, s, P * k:P * k + P], lb_sb[:, s, :],
                              start=True, stop=True).then_inc(rank_done[s], 1)

            def linear(b, s, hi, lo, t, last=False):
                if t >= 2 and last and s:
                    pe.wait_ge(x_ready, NT + t - 1)
                elif t >= 2:
                    pe.wait_ge(y_read[s], NT * b + t - 1)
                elif s:
                    pe.wait_ge(y_read[0], NT * (b + 1))
                else:
                    pe.wait_ge(y_read[1], NT * b)
                tok = slice(t * P, t * P + P)
                for k in range(KT):
                    if t == 0:
                        pe.wait_ge(w_ready[s], KT * b + k + 1)
                        pe.wait_ge(lo_ready[0] if s else lo_ready[1], KT * b + (k + 1 if s else 0))
                    for n, (a, v) in enumerate(three(hi[:, k, tok], lo[:, k, tok], w_hi[:, s, k, :], w_lo[:, s, k, :])):
                        mm = pe.matmul(ps_y[:, t % 2, :], a, v, start=(k == 0 and n == 0), stop=(k == KT - 1 and n == 2))
                mm.then_inc(y_done[s], 1)

            def turn(b, s, of):
                for t in range(NT):
                    if s == 0:
                        pe.wait_ge(z_ready, NT * b + t + 1)
                    else:
                        pe.wait_ge(y_read[1], NT * b + t + 1)
                    for k in range(KT):
                        mm = pe.transpose(ps_t[:, k, t * P:(t + 1) * P], of[:, t, P * k:P * k + P], ident[:, :])
                        if t == NT - 1:
                            mm.then_inc(turned[s], 1)

            def blk(b, last):
                for t in range(NT):
                    if t == 2:
                        rank_product(b, 1, (2, 3))
                    linear(b, 0, hT_hi, hT_lo, t)
                if not last:
                    rank_product(b + 1, 0, (0, 1))
                turn(b, 0, z)
                for t in range(NT):
                    if t == 2 and not last:
                        rank_product(b + 1, 0, (2, 3))
                    linear(b, 1, zT_hi, zT_lo, t, last)
                if not last:
                    rank_product(b + 1, 1, (0, 1))
                    turn(b, 1, h)

            rank_product(0, 0, range(KT))
            rank_product(0, 1, (0, 1))
            blk(0, False)
            with pe.Fori(1, NBK - 1) as b:
                blk(b, False)
            blk(NBK - 1, True)


def perceiver(nc, a, out):
    with ExitStack() as ctx:
        m = Memory(nc, ctx, "all")
        x, ident = m.sb("x", [P, NT, D]), m.sb("ident", [P, P])
        x_loaded, stored = m.sems("x_loaded", NT + 1), m.sem("stored")

        with ExitStack() as first:
            m = Memory(nc, first, "first")
            xT = m.sb("xT", [P, KT, TOK])

            def norm(prefetch):
                def loads(sp):
                    for t in range(NT):
                        sp.dma_start(x[:, t, :], a["x"][t * P:(t + 1) * P, :]).then_inc(x_loaded[t], 16)
                    sp.dma_start(ident[:, :], a["ident"]).then_inc(x_loaded[NT], 16)
                    prefetch(sp)

                with ExitStack() as stage:
                    xn = Memory(nc, stage, "n0").sb("xn", [P, NT, D])
                    layernorm(nc, "ln0", x, xn, xT, None, ident, loads, x_loaded=x_loaded)
            context_attention(nc, "ctx", norm, x, xT, ident, a["ctxT"], a["ctxN"])

        with ExitStack() as second:
            m = Memory(nc, second, "second")
            xT_hi, xT_lo = m.sb("xT_hi", [P, KT, TOK], F32R), m.sb("xT_lo", [P, KT, TOK], F32R)
            xn = m.sb("xn", [P, NT, D])
            head_attention(nc, "att0", lambda *beside: layernorm(nc, "ln1", x, xn, xT_hi, xT_lo, ident, *beside),
                           x, xn, xT_hi, xT_lo, ident, a["a0_wqk"], a["a0_wv"], a["a0_wo"], a["a0_bqk"],
                           a["a0_bv"], a["a0_bo"], DH, False)
            experts(nc, "moe", lambda *beside: layernorm(nc, "ln2", x, xn, xT_hi, xT_lo, ident, *beside),
                    x, xT_hi, xT_lo, ident, a["before"], a["gate"], a["w1"], a["w3"], a["w2"], a["b1"], a["b3"], a["b2"])

        with ExitStack() as cross:
            m = Memory(nc, cross, "cross")
            bq, bk, bv = m.sb("bq", [P, NG]), m.sb("bk", [P, NG]), m.sb("bv", [P, D])
            q = m.sb("q", [P, NG, TOK])
            with ExitStack() as kv:
                m = Memory(nc, kv, "kv")
                wk = m.sb("wk_hi", [P, KT, D], F32R), m.sb("wk_lo", [P, KT, D], F32R)
                wv = m.sb("wv_hi", [P, KT, D], F32R), m.sb("wv_lo", [P, KT, D], F32R)
                raw_T = m.sb("raw_T", [P, 2, KT, CHW[0]])
                wo_raw = raw_T[:, :, :, :].rearrange("p s k c -> p (s k c)")[:, 0:KT * D].rearrange("p (k d) -> p k d", d=D)
                T_loaded, wo_loaded = m.sems("T_loaded", 2), m.sem("wo_loaded")

                def loads_ahead(sp):
                    for c in range(2):
                        load_chunk(sp, 0, c, raw_T, a["ctxT"], T_loaded)

                with ExitStack() as stage:
                    m = Memory(nc, stage, "query")
                    xn = m.sb("xn", [P, NT, D])
                    xT_hi, xT_lo = m.sb("xT_hi", [P, KT, TOK], F32R), m.sb("xT_lo", [P, KT, TOK], F32R)
                    wq_hi, wq_lo = m.sb("wq_hi", [P, KT, D], F32R), m.sb("wq_lo", [P, KT, D], F32R)
                    project_queries(nc, "pq", lambda *beside: layernorm(nc, "ln3", x, xn, xT_hi, xT_lo, ident, *beside),
                                    q, xT_hi, xT_lo, (wk, wv), (a["wq"], a["wk"], a["wv"]), wq_hi, wq_lo,
                                    ((bq[:, :], a["bq"]), (bk[:, :], a["bk"]), (bv[:, :], a["bv"].to_broadcast([P, D]))),
                                    loads_ahead)
                masked_context_attention(nc, "cross", q, ident, wk, wv, bk, bv, raw_T, T_loaded, a["ctxT"], a["mask"], a["gain"],
                                         lambda sp: sp.dma_start(wo_raw, a["wo"]).then_inc(wo_loaded, 16))
                project_attended(nc, "po", x, q, wo_raw, wo_loaded, a["bo"])

        def store(sp, t):
            sp.dma_start(out[t * P:(t + 1) * P, :], x[:, t, :]).then_inc(stored, 16)
            if t == NT - 1:
                sp.wait_ge(stored, 16 * NT)

        with ExitStack() as last:
            m = Memory(nc, last, "last")
            xn = m.sb("xn", [P, NT, D])
            xT_hi, xT_lo = m.sb("xT_hi", [P, KT, TOK], F32R), m.sb("xT_lo", [P, KT, TOK], F32R)
            head_attention(nc, "att1", lambda *beside: layernorm(nc, "ln4", x, xn, xT_hi, xT_lo, ident, *beside),
                           x, xn, xT_hi, xT_lo, ident, a["a1_wqk"], a["a1_wv"], a["a1_wo"], a["a1_bqk"],
                           a["a1_bv"], a["a1_bo"], D // 2, True)
            quantized_blocks(nc, "quant", lambda *beside: layernorm(nc, "ln5", x, xn, xT_hi, xT_lo, ident, *beside),
                             x, xn, xT_hi, xT_lo, ident, a["codes"], a["scales"], a["la"], a["lb"],
                             a["bias"], a["gamma"], a["beta"], store)




def _slices(w):
    return w.reshape(w.shape[0] // P, P, -1).transpose(1, 0, 2)


def _head_groups(np, wq, wk, wv, wo, bq, bk, bv, bo, dv):
    parts = max(1, HG * dv // 512)
    vc = HG * dv // parts
    both = [np.concatenate([wq[:, g * P:g * P + P], wk[:, g * P:g * P + P]], 1) for g in range(NG)]
    return {
        "wqk": np.stack([_slices(w) for w in both]),
        "wv": np.stack([_slices(wv[:, i * vc:i * vc + vc]) for i in range(NG * parts)]).reshape(NG, parts, P, KT, vc),
        "wo": np.stack([_slices(wo[i * vc:i * vc + vc]) for i in range(NG * parts)]).reshape(NG, parts, P, vc // P, D),
        "bqk": np.stack([bq.reshape(NG, P), bk.reshape(NG, P)], -1).transpose(1, 0, 2),
        "bv": bv.reshape(NG, 1, HG * dv),
        "bo": bo.reshape(1, D),
    }


def kernel(**inputs):
    import numpy as np
    import concourse.bacc as bacc
    from concourse.bass_utils import run_bass_kernel_spmd

    i = {name: np.asarray(v) for name, v in inputs.items()}
    ctx = i["ctx_1024"]
    padded = np.concatenate([ctx.transpose(0, 2, 1), np.zeros((B, D, S2P - S2), ctx.dtype)], 2)
    a = {
        "x": i["x"].reshape(TOK, D),
        "ident": np.eye(P, dtype=np.float32),
        "before": np.tril(np.ones((NE - 1, NE - 1), np.float32), -1).reshape(1, -1),
        "ctxN": ctx,
        "ctxT": padded.reshape(B, KT, P, S2P).transpose(0, 2, 1, 3),
        "mask": i["mask_BxSxS2_ik1"],
        "gain": i["fside_BxSxS2_0"],
    }
    w, b = i["L0_attn_Wqkv"], i["L0_attn_bqkv"]
    layer = _head_groups(np, w[:, 0:D], w[:, D:2 * D], w[:, 2 * D:], i["L0_attn_Wo"], b[0:D], b[D:2 * D], b[2 * D:],
                         i["L0_attn_bo"], DH)
    a.update({f"a0_{n}": v for n, v in layer.items()})
    w, b = i["L1_attn_Wc"].T, i["L1_attn_bc"]
    layer = _head_groups(np, w[:, 0:D], w[:, D:2 * D], w[:, 2 * D:], i["L1_attn_Wo"].T, b[0:D], b[D:2 * D], b[2 * D:],
                         i["L1_attn_bo"], D // 2)
    a.update({f"a1_{n}": v for n, v in layer.items()})
    a["gate"] = _slices(i["L0_ffn_gate_w"].T)
    for n in "132":
        a[f"w{n}"] = np.stack([_slices(v) for v in [*i[f"L0_ffn_w{n}"], i[f"L0_ffn_sw{n}"]]])
        bias = np.concatenate([i[f"L0_ffn_b{n}"], i[f"L0_ffn_sb{n}"][None]])
        a[f"b{n}"] = bias if n == "2" else bias.reshape(NE, KT, P).transpose(2, 0, 1)
    for n in "qkvo":
        a[f"w{n}"] = _slices(i[f"L1_xattn_w{n}_k"])
        bias = i[f"L1_xattn_w{n}_b"]
        a[f"b{n}"] = bias.reshape(NG, P).T if n in "qk" else bias.reshape(1, D)
    a["codes"] = np.stack([_slices(c.T) for c in i["L1_ffn_qweights"]])
    a["scales"] = i["L1_ffn_scales"].transpose(0, 2, 1)
    a["la"] = i["L1_ffn_lora_a"]
    a["lb"] = i["L1_ffn_lora_b"].transpose(0, 2, 1)
    a["bias"] = i["L1_ffn_biases"].reshape(-1, 1, D)
    a["gamma"] = i["L1_ffn_ln_gamma"].reshape(-1, KT, P).transpose(2, 0, 1)
    a["beta"] = i["L1_ffn_ln_beta"].reshape(-1, KT, P).transpose(2, 0, 1)

    nc = bacc.Bacc("TRN2", target_bir_lowering=False, num_devices=1)
    arrays = {f"in_{n}": np.ascontiguousarray(v) for n, v in a.items()}
    aps = {n: nc.dram_tensor(f"in_{n}", arrays[f"in_{n}"].shape, mybir.dt.from_np(arrays[f"in_{n}"].dtype),
                             kind="ExternalInput").ap() for n in a}
    out = nc.dram_tensor("out", (TOK, D), F32, kind="ExternalOutput").ap()
    perceiver(nc, aps, out)
    r = run_bass_kernel_spmd(nc, [arrays], core_ids=[0])
    return r.results[0]["out"].reshape(B, S, D)
```
